# Optimizing a Trainium2 kernel written in Bass

```python
import numpy as np
import jax
import jax.numpy as jnp

def _softmax(x, axis=-1):
    return jax.nn.softmax(x, axis=axis)

def _gelu(x):
    return jax.nn.gelu(x, approximate=True)

def _silu(x):
    return jax.nn.silu(x)

def _sigmoid(x):
    return jax.nn.sigmoid(x)

def _layernorm(x, axis=-1, eps=1e-05):
    m = jnp.mean(x, axis=axis, keepdims=True)
    v = jnp.var(x, axis=axis, keepdims=True)
    return (x - m) / jnp.sqrt(v + eps)

def _scatter_add(tgt, idx, src, axis=0):
    return tgt.at[idx].add(src)

def _segment_sum(src, seg, n):
    return jax.ops.segment_sum(src, seg, n)
kernel_name = 'mk_xattn_ffn_d2_seqx_r2_f8144e'

def setup_inputs(seed: int=0):
    np.random.seed(seed)
    _w = jnp.asarray

    def _rec_inputs():
        import jax
        import jax.numpy as jnp
        _rk = jax.random.key(seed)
        x = -0.0002928 + 1 * jax.random.normal(jax.random.fold_in(_rk, 1), (2, 2048, 512), jnp.float32)
        _lenS = 2048 - jax.random.randint(jax.random.fold_in(_rk, 7), (2,), 0, max(1, 2048 // 4) + 1, jnp.int32)
        _lenS2 = 154 - jax.random.randint(jax.random.fold_in(_rk, 8), (2,), 0, max(1, 154 // 4) + 1, jnp.int32)
        _ctx_512P = jax.random.normal(jax.random.fold_in(_rk, 11), (2, 16, 256), jnp.float32)
        _ctx_512c = jax.random.dirichlet(jax.random.fold_in(_rk, 511), 0.3 * jnp.ones((16,), jnp.float32), (2, 154))
        _ctx_512t = jnp.einsum('bsk,bkd->bsd', _ctx_512c, _ctx_512P)
        _ctx_512t = _ctx_512t * jax.lax.rsqrt(jnp.mean(jnp.square(_ctx_512t)) + 1e-12) * 0.953939
        ctx_512 = -0.000514642 + 1.00011 * (_ctx_512t + 0.3 * jax.random.normal(jax.random.fold_in(_rk, 611), (2, 154, 256), jnp.float32))
        return (x, ctx_512)
    x, ctx_512 = _rec_inputs()

    def _L0_xattn_setup():
        import jax, jax.numpy as jnp
        import numpy as np
        DIM = 512
        LATENT_DIM = 256
        NUM_HEADS = 16
        HEAD_DIM = DIM // NUM_HEADS
        SCALE = HEAD_DIM ** (-0.5)
        key = jax.random.key(seed)
        k1, k2, k3, k4, k5 = jax.random.split(key, 5)
        B, xN, zN = (2, 1024, 1024)
        x = jax.random.normal(k1, (B, xN, DIM), dtype=jnp.float32)
        z = jax.random.normal(k2, (B, zN, LATENT_DIM), dtype=jnp.float32)
        Wq = jax.random.normal(k3, (DIM, DIM), dtype=jnp.float32) * DIM ** (-0.5)
        Wkv = jax.random.normal(k4, (2 * DIM, LATENT_DIM), dtype=jnp.float32) * LATENT_DIM ** (-0.5)
        Wo = jax.random.normal(k5, (DIM, DIM), dtype=jnp.float32) * DIM ** (-0.5)
        return {'x': x, 'z': z, 'Wq': Wq, 'Wkv': Wkv, 'Wo': Wo}
    _L0_xattn_all = _L0_xattn_setup()
    _L0_xattn_in = {k: v for k, v in _L0_xattn_all.items() if k in ('Wq', 'Wkv', 'Wo')}
    del _L0_xattn_all

    def _L0_ffn_setup():
        import jax, jax.numpy as jnp
        import numpy as np
        import math
        BETA = 0.9
        THRESHOLD = 1.0
        NUM_STEPS = 5
        ALPHA = 2.0

        @jax.custom_vjp
        def spike_fn(u):
            return (u > 0).astype(u.dtype)

        def _spike_fwd(u):
            return (spike_fn(u), u)

        def _spike_bwd(u, g):
            s = jnp.pi / 2.0 * ALPHA * u
            return (g * (ALPHA / 2.0) / (1.0 + s * s),)
        spike_fn.defvjp(_spike_fwd, _spike_bwd)
        key = jax.random.key(seed)
        k1, k2, k3 = jax.random.split(key, 3)
        n_embd = 512
        x = jax.random.normal(k1, (4, 1024, n_embd), dtype=jnp.float32)
        W_fc = jax.random.normal(k2, (4 * n_embd, n_embd), dtype=jnp.float32) / math.sqrt(n_embd)
        W_proj = jax.random.normal(k3, (n_embd, 4 * n_embd), dtype=jnp.float32) / math.sqrt(4 * n_embd)
        return {'x': x, 'W_fc': W_fc, 'W_proj': W_proj}
    _L0_ffn_all = _L0_ffn_setup()
    _L0_ffn_in = {k: v for k, v in _L0_ffn_all.items() if k in ('W_fc', 'W_proj')}
    del _L0_ffn_all

    def _L1_xattn_setup():
        import jax, jax.numpy as jnp
        import numpy as np
        B, LQ, LK = (8, 1024, 1024)
        QD, KD, VD = (512, 256, 256)
        key = jax.random.key(seed)
        ks = jax.random.split(key, 9)
        s = 0.02
        return {'query': jax.random.normal(ks[0], (B, LQ, QD), jnp.float32), 'key': jax.random.normal(ks[1], (B, LK, KD), jnp.float32), 'value': jax.random.normal(ks[2], (B, LK, VD), jnp.float32), 'Wq': jax.random.normal(ks[3], (QD, QD), jnp.float32) * s, 'bq': jnp.zeros((QD,), jnp.float32), 'Wk': jax.random.normal(ks[4], (KD, QD), jnp.float32) * s, 'bk': jnp.zeros((QD,), jnp.float32), 'Wv': jax.random.normal(ks[5], (VD, QD), jnp.float32) * s, 'bv': jnp.zeros((QD,), jnp.float32)}
    _L1_xattn_all = _L1_xattn_setup()
    _L1_xattn_in = {k: v for k, v in _L1_xattn_all.items() if k in ('Wq', 'bq', 'Wk', 'bk', 'Wv', 'bv')}
    del _L1_xattn_all

    def _L1_ffn_setup():
        import jax, jax.numpy as jnp
        import numpy as np
        B, S, K, N = (8, 4096, 512, 512)
        key = jax.random.key(seed)
        k1, k2, k3, k4 = jax.random.split(key, 4)
        x = jax.random.normal(k1, (B, S, K), dtype=jnp.float32)
        CB = jnp.clip(jnp.round(jax.random.normal(k2, (N, K), dtype=jnp.float32) * 42.0), -127.0, 127.0)
        SCB = jax.random.uniform(k3, (N,), dtype=jnp.float32, minval=0.5, maxval=2.0)
        bias = jax.random.normal(k4, (N,), dtype=jnp.float32) * 0.02
        return {'x': x, 'CB': CB, 'SCB': SCB, 'bias': bias}
    _L1_ffn_all = _L1_ffn_setup()
    _L1_ffn_in = {k: v for k, v in _L1_ffn_all.items() if k in ('CB', 'SCB', 'bias')}
    del _L1_ffn_all
    return {'x': x, 'ctx_512': ctx_512, 'L0_xattn_Wq': _L0_xattn_in['Wq'], 'L0_xattn_Wkv': _L0_xattn_in['Wkv'], 'L0_xattn_Wo': _L0_xattn_in['Wo'], 'L0_ffn_W_fc': _L0_ffn_in['W_fc'], 'L0_ffn_W_proj': _L0_ffn_in['W_proj'], 'L1_xattn_Wq': _L1_xattn_in['Wq'], 'L1_xattn_bq': _L1_xattn_in['bq'], 'L1_xattn_Wk': _L1_xattn_in['Wk'], 'L1_xattn_bk': _L1_xattn_in['bk'], 'L1_xattn_Wv': _L1_xattn_in['Wv'], 'L1_xattn_bv': _L1_xattn_in['bv'], 'L1_ffn_CB': _L1_ffn_in['CB'], 'L1_ffn_SCB': _L1_ffn_in['SCB'], 'L1_ffn_bias': _L1_ffn_in['bias']}

def reference(x, ctx_512, L0_xattn_Wq, L0_xattn_Wkv, L0_xattn_Wo, L0_ffn_W_fc, L0_ffn_W_proj, L1_xattn_Wq, L1_xattn_bq, L1_xattn_Wk, L1_xattn_bk, L1_xattn_Wv, L1_xattn_bv, L1_ffn_CB, L1_ffn_SCB, L1_ffn_bias):
    import jax
    import jax.numpy as jnp

    def _L0_xattn_ref(x, z, Wq, Wkv, Wo):
        import jax, jax.numpy as jnp
        import numpy as np
        DIM = 512
        LATENT_DIM = 256
        NUM_HEADS = 16
        HEAD_DIM = DIM // NUM_HEADS
        SCALE = HEAD_DIM ** (-0.5)
        B, xN, _ = x.shape
        _, zN, _ = z.shape
        Q = (x @ Wq.T).reshape(B, xN, NUM_HEADS, HEAD_DIM)
        KV = (z @ Wkv.T).reshape(B, zN, 2, NUM_HEADS, HEAD_DIM)
        K = KV[:, :, 0]
        V = KV[:, :, 1]
        attn = jnp.einsum('bqhd,bkhd->bhqk', Q, K) * SCALE
        attn = jax.nn.softmax(attn, axis=-1)
        O = jnp.einsum('bhqk,bkhd->bqhd', attn, V).reshape(B, xN, DIM)
        return O @ Wo.T

    def _L0_ffn_ref(x, W_fc, W_proj):
        import jax, jax.numpy as jnp
        import numpy as np
        import math
        BETA = 0.9
        THRESHOLD = 1.0
        NUM_STEPS = 5
        ALPHA = 2.0

        @jax.custom_vjp
        def spike_fn(u):
            return (u > 0).astype(u.dtype)

        def _spike_fwd(u):
            return (spike_fn(u), u)

        def _spike_bwd(u, g):
            s = jnp.pi / 2.0 * ALPHA * u
            return (g * (ALPHA / 2.0) / (1.0 + s * s),)
        spike_fn.defvjp(_spike_fwd, _spike_bwd)
        h = jnp.square(jax.nn.relu(jnp.einsum('bsd,fd->bsf', x, W_fc)))
        y = jnp.einsum('bsf,df->bsd', h, W_proj)

        def step(mem, _):
            reset = jax.lax.stop_gradient(spike_fn(mem - THRESHOLD))
            mem_new = BETA * mem + y - reset * THRESHOLD
            spk = spike_fn(mem_new - THRESHOLD)
            return (mem_new, spk)
        mem0 = jnp.zeros_like(y)
        _, spks = jax.lax.scan(step, mem0, None, length=NUM_STEPS)
        return jnp.sum(spks, axis=0) / NUM_STEPS

    def _L1_xattn_ref(query, key, value, Wq, bq, Wk, bk, Wv, bv):
        import jax, jax.numpy as jnp
        import numpy as np
        B, LQ, LK = (8, 1024, 1024)
        QD, KD, VD = (512, 256, 256)
        q = jnp.einsum('bld,de->ble', query, Wq) + bq
        k = jnp.einsum('bld,de->ble', key, Wk) + bk
        v = jnp.einsum('bld,de->ble', value, Wv) + bv
        scores = jnp.einsum('bqe,bke->bqk', q, k)
        attn = jax.nn.softmax(scores, axis=-1)
        out = jnp.einsum('bqk,bke->bqe', attn, v)
        return out

    def _L1_ffn_ref(x, CB, SCB, bias):
        import jax, jax.numpy as jnp
        import numpy as np
        B, S, K, N = (8, 4096, 512, 512)
        out = jnp.einsum('bsk,nk->bsn', x, CB)
        out = out * (SCB * (1.0 / 127.0)) + bias
        return out
    x = x + _L0_xattn_ref(_layernorm(x, axis=-1), ctx_512, L0_xattn_Wq, L0_xattn_Wkv, L0_xattn_Wo)
    x = x + _L0_ffn_ref(_layernorm(x, axis=-1), L0_ffn_W_fc, L0_ffn_W_proj)
    x = x + _L1_xattn_ref(_layernorm(x, axis=-1), ctx_512, ctx_512, L1_xattn_Wq, L1_xattn_bq, L1_xattn_Wk, L1_xattn_bk, L1_xattn_Wv, L1_xattn_bv)
    x = x + _L1_ffn_ref(_layernorm(x, axis=-1), L1_ffn_CB, L1_ffn_SCB, L1_ffn_bias)
    return x

_drawn_inputs = setup_inputs


def setup_inputs(seed=0):
    import zlib

    import numpy as np

    out = dict(_drawn_inputs(seed))
    spreads = {'L1_xattn_bq': (0.0, 0.1), 'L1_xattn_bk': (0.0, 2.0), 'L1_xattn_bv': (0.0, 0.1)}
    factors = {'L1_ffn_bias': 31.239}
    for name, (base, spread) in spreads.items():
        noise = np.random.default_rng([zlib.crc32(name.encode()), seed]).standard_normal(out[name].shape)
        drawn = base * np.exp(spread * noise) if base else spread * noise
        out[name] = jnp.asarray(drawn.astype(out[name].dtype))
    for name, factor in factors.items():
        out[name] = (out[name] * factor).astype(out[name].dtype)
    return out
```

```python
from contextlib import ExitStack

import concourse.bass as bass
import numpy as np
from concourse import mybir
from concourse.alu_op_type import AluOpType as ALU

ACT = mybir.ActivationFunctionType
AX_X = mybir.AxisListType.X
F32 = mybir.dt.float32
F32R = mybir.dt.float32r

P = 128
D = 512
BATCH, SEQ = 2, 2048
ROWS = BATCH * SEQ
CTX, CTXD = 154, 256
HEADS, HD = 16, 32
FF = 2048
KT = D // P
T = 4
CH = T * P
NCH = ROWS // CH
NF = FF // P
EPS = 1e-5
LIF_BETA, LIF_THRESHOLD, LIF_STEPS = 0.9, 1.0, 5


def split_matmul(nc, out, stat, mov, start, stop):
    nc.tensor.matmul(out, stat[0], mov[0], start=start, stop=False)
    nc.tensor.matmul(out, stat[0], mov[1], start=False, stop=False)
    return nc.tensor.matmul(out, stat[1], mov[0], start=False, stop=stop)


def spike_thresholds():
    one, beta = np.float32(LIF_THRESHOLD), np.float32(LIF_BETA)

    def count(y):
        mem, n = np.float32(0), 0
        for _ in range(LIF_STEPS):
            reset = one if mem > one else np.float32(0)
            mem = np.float32(np.float32(beta * mem + y) - reset)
            n += bool(mem > one)
        return n

    found = []
    for n in range(LIF_STEPS):
        low, high = np.float32(0), np.float32(2)
        while np.nextafter(low, high) < high:
            mid = np.float32((np.float64(low) + np.float64(high)) / 2)
            if mid in (low, high):
                break
            low, high = (low, mid) if count(mid) > n else (mid, high)
        found.append(float(low))
    return found


def wait_apart(engine, sem, value, spare):
    engine.wait_ge(sem, value)
    engine.sem_inc(spare, 1)



def multi_head_attention(nc, x_in, x_out, ctx_t, wq_t, wk_t, wv_t, wo_t):
    KC = CTXD // P
    NG = HEADS * HD // P
    GH = P // HD
    GC = GH * CTX
    NB = -(-GC // P)
    size = [min(P, GC - b * P) for b in range(NB)]
    SCALE = HD ** -0.5
    with ExitStack() as ctx:
        def sb(name, shape, dt=F32):
            return ctx.enter_context(nc.sbuf_tensor(name, shape, dt))

        def bank(name, shape):
            return ctx.enter_context(nc.psum_tensor(name, shape, F32))

        def sem(name):
            return ctx.enter_context(nc.semaphore("a_" + name))

        wq_hi, wq_lo = sb("wq_hi", [P, KT, D], F32R), sb("wq_lo", [P, KT, D], F32R)
        wo_hi, wo_lo = sb("wo_hi", [P, NG, D], F32R), sb("wo_lo", [P, NG, D], F32R)
        k_hi, k_lo = sb("k_hi", [P, BATCH, NG, GC], F32R), sb("k_lo", [P, BATCH, NG, GC], F32R)
        v_hi, v_lo = sb("va_hi", [P, BATCH, NG, NB, P], F32R), sb("va_lo", [P, BATCH, NG, NB, P], F32R)
        x_ln = sb("x_ln", [P, T, D])
        x_res = sb("x_res", [P, 2, D])
        xt_hi, xt_lo = sb("xta_hi", [P, KT, CH], F32R), sb("xta_lo", [P, KT, CH], F32R)
        q_hi, q_lo = sb("q_hi", [P, 2, CH], F32R), sb("q_lo", [P, 2, CH], F32R)
        probs = sb("probs_a", [P, 2, T, GC])
        pt_hi, pt_lo = sb("pta_hi", [P, NB, CH], F32R), sb("pta_lo", [P, NB, CH], F32R)
        o_hi, o_lo = sb("o_hi", [P, NG, CH], F32R), sb("o_lo", [P, NG, CH], F32R)
        ctx_sb = sb("ctx_a", [P, KC, BATCH * CTX])
        mask = sb("mask", [P, NB, GH, HD])
        ident = sb("ident_a", [P, P])
        minus_half = sb("minus_half_a", [P, 1])
        stats, mean_var = sb("stats_a", [P, T, 6]), sb("mean_var_a", [P, T, 2])
        var_eps, rstd = sb("var_eps_a", [P, T]), sb("rstd_a", [P, T])
        minus_max, bias_max = sb("minus_max_a", [P, T, GH]), sb("bias_max_a", [P, T, GH])
        weight_sum, inv_sum = sb("weight_sum_a", [P, T, GH]), sb("inv_sum_a", [P, T, GH])
        flat = probs[:].rearrange("p a t c -> p (a t c)")
        ctx_rep = flat[:, 0:BATCH * KC * GC].rearrange("p (b k c) -> p b k c", b=BATCH, k=KC)
        wk_sb = flat[:, 4 * GC:4 * GC + KC * D].rearrange("p (k n) -> p k n", k=KC)
        wv_sb = flat[:, 6 * GC:6 * GC + KC * D].rearrange("p (k n) -> p k n", k=KC)

        psum_s = bank("psum_s_a", [P, 2, 2, 512])
        psum_tr = bank("psum_tr", [P, 2, 512])
        psum_q, psum_o = bank("psum_q", [P, CH]), bank("psum_o_a", [P, CH])

        ctx_loaded, rep_loaded = sem("ctx_loaded"), sem("rep_loaded")
        raw_loaded = [sem("raw_loaded0"), sem("raw_loaded1")]
        consts_set, blocks_zeroed = sem("consts_set"), sem("blocks_zeroed")
        k_filled, k_hi_done, k_lo_done = sem("k_filled"), sem("k_hi_done"), sem("k_lo_done")
        v_filled, v_hi_done, v_diff, v_lo_done = sem("v_filled"), sem("v_hi_done"), sem("v_diff"), sem("v_lo_done")
        w_hi_done, w_lo_done = sem("w_hi_done"), sem("w_lo_done")
        ln_loaded = [sem("ln_loaded0"), sem("ln_loaded1")]
        stats_done, mean_var_done, var_eps_done = sem("stats_done"), sem("mean_var_done"), sem("var_eps_done")
        rstd_done, xn_ready, xt_hi_done = sem("rstd_done"), sem("xn_ready"), sem("xt_hi_done")
        tr_filled, tr_free = sem("tr_filled"), sem("tr_free")
        q_filled, q_hi_done, q_lo_done = sem("q_filled"), sem("q_hi_done"), sem("q_lo_done")
        o_hi_done, o_lo_done = sem("o_hi_done"), sem("o_lo_done")
        pt_hi_done, pv_done = sem("pt_hi_done"), sem("pv_done")
        s_filled, max_done, bias_done = sem("s_filled"), sem("max_done"), sem("bias_done")
        exp_done, inv_done, probs_ready = sem("exp_done"), sem("inv_done"), sem("probs_ready")
        res_loaded, x_stored = [sem("res_loaded0"), sem("res_loaded1")], [sem("x_stored0"), sem("x_stored1")]
        spare = sem("spare")

        x_view = x_in.rearrange("(b m t p) d -> b m t p d", b=BATCH, t=T, p=P)
        o_view = x_out.rearrange("(b m t p) d -> b m t p d", b=BATCH, t=T, p=P)

        def after(n, m, par):
            return (n + 1, m + par, 1 - par)

        def before(n, m, par):
            return (n - 1, m - 1 + par, 1 - par)

        def chunks(engine, body):
            body((0, 0, 0), True, False)
            with engine.Fori(1, NCH // 2) as i:
                body((i * 2 - 1, i - 1, 1), False, False)
                body((i * 2, i, 0), False, False)
            body((NCH - 1, NCH // 2 - 1, 1), False, True)

        TR_USES = NG * NB + 2 * T
        step_start = [0, NB, 2 * NB + T, 3 * NB + T]

        def is_chunk(n, number):
            return isinstance(n, int) and n == number

        def use_pt(n, g, b):
            if is_chunk(n, 0) and g == 1:
                return T + b
            alone = g in (0, 2) or (g == NG - 1 and is_chunk(n, NCH - 1))
            place = b if alone else min(2 * b, NB + T - 1)
            return n * TR_USES + (step_start[g] + place - NB - (T if is_chunk(n, NCH) else 0))

        def use_wo(n, t):
            if is_chunk(n, NCH - 1):
                return NCH * TR_USES - T + t
            return (n + 1) * TR_USES + (2 * t + 1)

        def use_xt(n, t):
            if is_chunk(n, 0):
                return t
            return (n - 1) * TR_USES + (step_start[NG - 1] + 2 * t + 1 - NB)

        def tr_bank(use, n, *place):
            return use(n if isinstance(n, int) else 2, *place) % 2

        assert TR_USES % 2 == 0

        def has_before(c, g):
            return not (isinstance(c[0], int) and c[0] == 0 and g == 0)

        block = ctx.enter_context(nc.Block())

        @block.sync
        def _(sp):
            def load_ln(c, t):
                n, m, par = c
                sp.dma_start(x_ln[:, t], x_view[par, m, t]).then_inc(ln_loaded[t % 2], 16)

            def load_res(c, t):
                n, m, par = c
                if not (isinstance(n, int) and 2 * n + t // 2 == 0):
                    sp.wait_ge(x_stored[t % 2], (n * 2 + t // 2) * 16)
                sp.dma_start(x_res[:, t % 2], x_view[par, m, t]).then_inc(res_loaded[t % 2], 16)

            for t in range(2):
                load_ln((0, 0, 0), t)
            sp.dma_start(ctx_sb[:], ctx_t).then_inc(ctx_loaded, 16)
            sp.dma_start(wk_sb, wk_t).then_inc(ctx_loaded, 16)
            for j in range(2 * KT):
                if j >= 2:
                    sp.wait_ge(w_lo_done, j - 1)
                src = wq_t[:, j] if j < KT else wo_t[:, j - KT]
                sp.dma_start(x_res[:, j % 2], src).then_inc(raw_loaded[j % 2], 16)
                if j == 1:
                    for t in range(2, T):
                        sp.wait_ge(ln_loaded[t % 2], 16)
                        load_ln((0, 0, 0), t)
                    sp.dma_start(wv_sb, wv_t).then_inc(rep_loaded, 16)
                    for b in range(BATCH):
                        for h in range(GH):
                            sp.dma_start(ctx_rep[:, b, :, h * CTX:(h + 1) * CTX],
                                         ctx_t[:, :, b * CTX:(b + 1) * CTX]).then_inc(rep_loaded, 16)
            sp.wait_ge(w_lo_done, 2 * KT)

            def residual(c):
                n, m, par = c
                load_res(c, 0)
                load_res(c, 1)
                for t in range(T):
                    sp.wait_ge(tr_free, use_wo(n, t) + 1)
                    sp.dma_start(o_view[par, m, t], x_res[:, t % 2]).then_inc(x_stored[t % 2], 16)
                    if t + 2 < T:
                        load_res(c, t + 2)

            def body(c, first, last):
                if not last:
                    for t in range(T):
                        sp.wait_ge(tr_filled, use_xt(c[0], t) + 1)
                        if t >= 2:
                            sp.wait_ge(ln_loaded[t % 2], (after(*c)[0] * 2 + 1) * 16)
                        load_ln(after(*c), t)
                if not first:
                    residual(before(*c))

            chunks(sp, body)
            residual((NCH - 1, NCH // 2 - 1, 1))
            for parity in range(2):
                sp.wait_ge(x_stored[parity], 16 * NCH * T // 2)

        @block.gpsimd
        def _(pool):
            nc.gpsimd.memset(ident[:], 0.0).then_inc(consts_set, 1)
            pool.wait_ge(consts_set, 1)
            nc.gpsimd.affine_select(out=ident[:], in_=ident[:], compare_op=ALU.not_equal, fill=1.0,
                                    base=0, pattern=[[-1, P]], channel_multiplier=1).then_inc(consts_set, 1)
            nc.gpsimd.memset(minus_half[:], -0.5).then_inc(consts_set, 1)
            nc.gpsimd.memset(mask[:], 1.0).then_inc(consts_set, 1)
            pool.wait_ge(consts_set, 4)

            def inverse_std(n, t):
                q = n * T + t
                wait_apart(pool, mean_var_done, q + 1, spare)
                nc.gpsimd.tensor_scalar(var_eps[:, t:t + 1], mean_var[:, t, 1:2], EPS, None,
                                        ALU.add).then_inc(var_eps_done, 1)
                pool.wait_ge(var_eps_done, q + 1)
                nc.gpsimd.tensor_tensor(rstd[:, t:t + 1], var_eps[:, t:t + 1], minus_half[:],
                                        ALU.pow).then_inc(rstd_done, 1)

            for t in range(T):
                inverse_std(0, t)
            for blk in (k_hi, k_lo):
                nc.gpsimd.memset(blk[:].bitcast(F32), 0.0).then_inc(blocks_zeroed, 1)
            nc.gpsimd.affine_select(out=mask[:], in_=mask[:], compare_op=ALU.is_ge, fill=0.0, base=0,
                                    pattern=[[P, NB], [-CTX, GH], [0, HD]], channel_multiplier=1).then_inc(consts_set, 1)
            pool.wait_ge(consts_set, 5)
            nc.gpsimd.affine_select(out=mask[:], in_=mask[:], compare_op=ALU.is_ge, fill=0.0, base=CTX - 1,
                                    pattern=[[-P, NB], [CTX, GH], [0, HD]], channel_multiplier=-1).then_inc(consts_set, 1)

            def body(c, first, last):
                for g in range(NG):
                    for t in range(T):
                        s = c[0] * (NG * T) + (g * T + t)
                        tile = probs[:, g % 2, t].rearrange("p (h c) -> p h c", h=GH)
                        pool.wait_ge(inv_done, s + 1)
                        nc.gpsimd.tensor_tensor(tile, tile, inv_sum[:, t].unsqueeze(2).to_broadcast([P, GH, CTX]),
                                                ALU.mult).then_inc(probs_ready, 1)
                        if not last and g in (1, 2) and t < 2:
                            inverse_std(after(*c)[0], 2 * (g - 1) + t)

            chunks(pool, body)

        @block.scalar
        def _(act):
            def x_hi(n, t):
                act.wait_ge(tr_filled, use_xt(n, t) + 1)
                nc.scalar.copy(xt_hi[:, :, t * P:(t + 1) * P],
                               psum_tr[:, tr_bank(use_xt, n, t)].rearrange(
                                   "p (k c) -> p k c", k=KT)).then_inc(xt_hi_done, 1)

            def group_hi(filled, count, out, in_, done):
                act.wait_ge(filled, count)
                nc.scalar.copy(out, in_).then_inc(done, 1)

            for j in range(KT):
                act.wait_ge(raw_loaded[j % 2], 16 * (j // 2 + 1))
                nc.scalar.copy(wq_hi[:, j], x_res[:, j % 2]).then_inc(w_hi_done, 1)
            for t in range(T):
                x_hi(0, t)
            act.wait_ge(k_filled, NG)
            act.wait_ge(blocks_zeroed, 2)
            for b in range(BATCH):
                for h in range(GH):
                    rows = slice(h * HD, (h + 1) * HD)
                    nc.scalar.copy(k_hi[rows, b, :, h * CTX:(h + 1) * CTX],
                                   psum_s[rows, :, :, b * CTX:(b + 1) * CTX].rearrange("p a c n -> p (a c) n")
                                   ).then_inc(k_hi_done, 1)
            group_hi(q_filled, 1, q_hi[:, 0], psum_q[:], q_hi_done)
            for j in range(KT, 2 * KT):
                act.wait_ge(raw_loaded[j % 2], 16 * (j // 2 + 1))
                nc.scalar.copy(wo_hi[:, j - KT], x_res[:, j % 2]).then_inc(w_hi_done, 1)

            def p_hi(c, g, b):
                G = c[0] * NG + (g - 1)
                if not (isinstance(G, int) and G == 0):
                    act.wait_ge(pv_done, G * NB + (b + 1 - NB))
                act.wait_ge(tr_filled, use_pt(c[0], g, b) + 1)
                nc.scalar.copy(pt_hi[0:size[b], b], psum_tr[0:size[b], tr_bank(use_pt, c[0], g, b)]).then_inc(pt_hi_done, 1)

            def exps(c, g, t):
                s = c[0] * (NG * T) + (g * T + t)
                act.wait_ge(bias_done, s + 1)
                for h in range(GH):
                    ins = nc.scalar.activation(probs[:, g % 2, t, h * CTX:(h + 1) * CTX],
                                               psum_s[:, t % 2, h // 2, (h % 2) * CTX:(h % 2 + 1) * CTX], ACT.Exp,
                                               bias=bias_max[:, t, h:h + 1], scale=SCALE,
                                               accum_out=weight_sum[:, t, h:h + 1])
                ins.then_inc(exp_done, 1)

            def finish(c, g, before_there, after_there):
                G = c[0] * NG + g
                if before_there:
                    p_hi(c, g, NB - 1)
                if after_there:
                    group_hi(q_filled, G + 2, q_hi[:, (g + 1) % 2], psum_q[:], q_hi_done)
                if before_there:
                    group_hi(pv_done, G * NB, o_hi[:, (g - 1) % NG], psum_o[:], o_hi_done)

            def body(c, first, last):
                for g in range(NG):
                    there = has_before(c, g)
                    for t in range(T):
                        if there:
                            p_hi(c, g, t)
                        exps(c, g, t)
                        if g == NG - 1 and not last:
                            x_hi(after(*c)[0], t)
                    finish(c, g, there, not (last and g == NG - 1))

            chunks(act, body)
            end = (NCH, 0, 0)
            for b in range(NB - 1):
                p_hi(end, 0, b)
            finish(end, 0, True, False)

        @block.vector
        def _(dve):
            def ln_stats(n, t):
                q = n * T + t
                if not (isinstance(n, int) and n == 0):
                    wait_apart(dve, rstd_done, n * T, spare)
                wait_apart(dve, ln_loaded[t % 2], (n * 2 + (t // 2 + 1)) * 16, spare)
                nc.vector.bn_stats(stats[:, t], x_ln[:, t]).then_inc(stats_done, 1)
                wait_apart(dve, stats_done, q + 1, spare)
                nc.vector.bn_aggr(mean_var[:, t], stats[:, t]).then_inc(mean_var_done, 1)

            def ln_apply(n, t):
                dve.wait_ge(rstd_done, n * T + (t + 1))
                nc.vector.tensor_scalar(x_ln[:, t], x_ln[:, t], mean_var[:, t, 0:1], rstd[:, t:t + 1],
                                        ALU.subtract, ALU.mult).then_inc(xn_ready, 1)

            def x_lo(n, t):
                cols = slice(t * P, (t + 1) * P)
                bank = tr_bank(use_xt, n, t)
                dve.wait_ge(xt_hi_done, n * T + (t + 1))
                nc.vector.tensor_tensor(xt_lo[:, :, cols], psum_tr[:, bank].rearrange("p (k c) -> p k c", k=KT),
                                        xt_hi[:, :, cols].bitcast(F32), ALU.subtract).then_inc(tr_free, 1)

            def group_lo(hi_done, G, out, in_, hi, done):
                dve.wait_ge(hi_done, G + 1)
                nc.vector.tensor_tensor(out, in_, hi.bitcast(F32), ALU.subtract).then_inc(done, 1)

            dve.wait_ge(consts_set, 4)
            for t in range(T):
                ln_stats(0, t)
            for t in range(T):
                ln_apply(0, t)
            for j in range(KT):
                dve.wait_ge(w_hi_done, j + 1)
                nc.vector.tensor_tensor(wq_lo[:, j], x_res[:, j % 2], wq_hi[:, j].bitcast(F32),
                                        ALU.subtract).then_inc(w_lo_done, 1)
            for t in range(T):
                x_lo(0, t)
            dve.wait_ge(k_hi_done, BATCH * GH)
            for b in range(BATCH):
                for h in range(GH):
                    rows = slice(h * HD, (h + 1) * HD)
                    nc.vector.tensor_tensor(k_lo[rows, b, :, h * CTX:(h + 1) * CTX],
                                            psum_s[rows, :, :, b * CTX:(b + 1) * CTX].rearrange("p a c n -> p (a c) n"),
                                            k_hi[rows, b, :, h * CTX:(h + 1) * CTX].bitcast(F32),
                                            ALU.subtract).then_inc(k_lo_done, 1)
            dve.wait_ge(consts_set, 6)
            for j in range(BATCH * NB):
                b, blk = j // NB, j % NB
                rows = slice(0, size[blk])
                src = (psum_q, psum_o)[j % 2][rows].rearrange("p (g c) -> p g c", g=NG)
                keep = mask[rows, blk].rearrange("p h c -> p (h c)").unsqueeze(1).to_broadcast([size[blk], NG, P])
                hi, lo = v_hi[rows, b, :, blk], v_lo[rows, b, :, blk]
                dve.wait_ge(v_filled, j + 1)
                nc.vector.tensor_tensor(hi, src, keep, ALU.mult).then_inc(v_hi_done, 1)
                dve.wait_ge(v_hi_done, j + 1)
                nc.vector.tensor_tensor(lo, src, hi.bitcast(F32), ALU.subtract).then_inc(v_diff, 1)
                dve.wait_ge(v_diff, j + 1)
                nc.vector.tensor_tensor(lo, lo.bitcast(F32), keep, ALU.mult).then_inc(v_lo_done, 1)
            group_lo(q_hi_done, 0, q_lo[:, 0], psum_q[:], q_hi[:, 0], q_lo_done)
            for j in range(KT, 2 * KT):
                dve.wait_ge(w_hi_done, j + 1)
                nc.vector.tensor_tensor(wo_lo[:, j - KT], x_res[:, j % 2], wo_hi[:, j - KT].bitcast(F32),
                                        ALU.subtract).then_inc(w_lo_done, 1)

            def p_lo(c, g, b):
                G = c[0] * NG + (g - 1)
                dve.wait_ge(pt_hi_done, G * NB + (b + 1))
                nc.vector.tensor_tensor(pt_lo[0:size[b], b], psum_tr[0:size[b], tr_bank(use_pt, c[0], g, b)],
                                        pt_hi[0:size[b], b].bitcast(F32), ALU.subtract).then_inc(tr_free, 1)

            def maxima(c, g, t):
                s = c[0] * (NG * T) + (g * T + t)
                dve.wait_ge(s_filled, s + 1)
                nc.vector.tensor_reduce(minus_max[:, t],
                                        psum_s[:, t % 2, :, 0:2 * CTX].rearrange("p a (h c) -> p a h c", h=2),
                                        AX_X, ALU.max, negate=True).then_inc(max_done, 1)
                dve.wait_ge(max_done, s + 1)
                nc.vector.tensor_scalar(bias_max[:, t], minus_max[:, t], SCALE, None, ALU.mult).then_inc(bias_done, 1)

            def inverse(c, g, t):
                s = c[0] * (NG * T) + (g * T + t)
                if not (isinstance(s, int) and s < T):
                    dve.wait_ge(probs_ready, s + (1 - T))
                dve.wait_ge(exp_done, s + 1)
                nc.vector.reciprocal(inv_sum[:, t], weight_sum[:, t]).then_inc(inv_done, 1)

            def wo_rows(c, t):
                n = c[0]
                dve.wait_ge(res_loaded[t % 2], (n * 2 + (t // 2 + 1)) * 16)
                dve.wait_ge(tr_filled, use_wo(n, t) + 1)
                nc.vector.tensor_tensor(x_res[:, t % 2], psum_tr[:, tr_bank(use_wo, c[0], t)], x_res[:, t % 2],
                                        ALU.add).then_inc(tr_free, 1)

            def finish(c, g, before_there, after_there):
                G = c[0] * NG + g
                if before_there:
                    p_lo(c, g, NB - 1)
                if after_there:
                    inverse(c, g, T - 1)
                    group_lo(q_hi_done, G + 1, q_lo[:, (g + 1) % 2], psum_q[:], q_hi[:, (g + 1) % 2], q_lo_done)
                elif g:
                    inverse(c, g, T - 1)
                if before_there:
                    group_lo(o_hi_done, G - 1, o_lo[:, (g - 1) % NG], psum_o[:], o_hi[:, (g - 1) % NG], o_lo_done)

            def body(c, first, last):
                for g in range(NG):
                    there = has_before(c, g)
                    for t in range(T):
                        maxima(c, g, t)
                        if there:
                            p_lo(c, g, t)
                        if g == 1 and not first:
                            wo_rows(before(*c), t)
                        if t:
                            inverse(c, g, t - 1)
                        if not last:
                            if g in (1, 2):
                                tile = 2 * (g - 1) + t % 2
                                (ln_stats if t < 2 else ln_apply)(after(*c)[0], tile)
                            if g == NG - 1:
                                x_lo(after(*c)[0], t)
                    finish(c, g, there, not (last and g == NG - 1))

            chunks(dve, body)
            end = (NCH, NCH // 2, 0)
            for b in range(NB - 1):
                p_lo(end, 0, b)
            finish(end, 0, True, False)
            for t in range(T):
                wo_rows(before(*end), t)

        @block.tensor
        def _(pe):
            def claim_tr(use):
                if not (isinstance(use, int) and use < 2):
                    pe.wait_ge(tr_free, use - 1)

            def x_transposes(n, t):
                bank = tr_bank(use_xt, n, t)
                pe.wait_ge(xn_ready, n * T + (t + 1))
                claim_tr(use_xt(n, t))
                for k in range(KT):
                    mm = nc.tensor.transpose(psum_tr[:, bank, k * P:(k + 1) * P], x_ln[:, t, k * P:(k + 1) * P], ident[:])
                mm.then_inc(tr_filled, 1)

            def q_part(G, g, k):
                mm = split_matmul(nc, psum_q[:], (wq_hi[:, k, g * P:(g + 1) * P], wq_lo[:, k, g * P:(g + 1) * P]),
                                  (xt_hi[:, k], xt_lo[:, k]), k == 0, k == KT - 1)
                if k == KT - 1:
                    mm.then_inc(q_filled, 1)

            pe.wait_ge(consts_set, 4)
            for t in range(T):
                x_transposes(0, t)
            pe.wait_ge(ctx_loaded, 32)
            for g in range(NG):
                for k in range(KC):
                    mm = nc.tensor.matmul(psum_s[:, g // 2, g % 2, 0:BATCH * CTX], wk_sb[:, k, g * P:(g + 1) * P],
                                          ctx_sb[:, k], start=(k == 0), stop=(k == KC - 1))
                mm.then_inc(k_filled, 1)
            pe.wait_ge(rep_loaded, 16 * (1 + BATCH * GH))
            for j in range(BATCH * NB):
                b, blk = j // NB, j % NB
                if j >= 2:
                    pe.wait_ge(v_diff, j - 1)
                for k in range(KC):
                    mm = nc.tensor.matmul((psum_q, psum_o)[j % 2][0:size[blk]],
                                          ctx_rep[:, b, k, blk * P:blk * P + size[blk]], wv_sb[:, k],
                                          start=(k == 0), stop=(k == KC - 1))
                mm.then_inc(v_filled, 1)
            pe.wait_ge(tr_free, T)
            pe.wait_ge(w_lo_done, KT)
            pe.wait_ge(v_diff, BATCH * NB - 1)
            for k in range(KT):
                q_part(0, 0, k)
            pe.wait_ge(v_lo_done, BATCH * NB)
            pe.wait_ge(k_lo_done, BATCH * GH)

            def scores(c, g, t):
                n, m, par = c
                s = n * (NG * T) + (g * T + t)
                if t == 0:
                    pe.wait_ge(q_lo_done, n * NG + (g + 1))
                if not (isinstance(s, int) and s < 2):
                    pe.wait_ge(exp_done, s - 1)
                rows = slice(t * P, (t + 1) * P)
                for pair in range(2):
                    keys = slice(pair * 2 * CTX, (pair + 1) * 2 * CTX)
                    mm = split_matmul(nc, psum_s[:, t % 2, pair, 0:2 * CTX],
                                      (q_hi[:, g % 2, rows], q_lo[:, g % 2, rows]),
                                      (k_hi[:, par, g, keys], k_lo[:, par, g, keys]), True, True)
                mm.then_inc(s_filled, 1)

            def p_transposes(c, g, b):
                if b == 0:
                    pe.wait_ge(probs_ready, c[0] * (NG * T) + g * T)
                claim_tr(use_pt(c[0], g, b))
                cols = slice(b * P, b * P + size[b])
                for t in range(T):
                    mm = nc.tensor.transpose(psum_tr[0:size[b], tr_bank(use_pt, c[0], g, b), t * P:(t + 1) * P],
                                             probs[:, (g - 1) % 2, t, cols], ident[:])
                mm.then_inc(tr_filled, 1)

            def values(c, g, b):
                G = c[0] * NG + (g - 1)
                gb = (g - 1) % NG
                par = c[2] if g else 1 - c[2]
                if b == 0 and not (isinstance(G, int) and G == 0):
                    pe.wait_ge(o_lo_done, G)
                pe.wait_ge(tr_free, use_pt(c[0], g, b) + 1)
                rows = slice(0, size[b])
                mm = split_matmul(nc, psum_o[:], (v_hi[rows, par, gb, b], v_lo[rows, par, gb, b]),
                                  (pt_hi[rows, b], pt_lo[rows, b]), b == 0, b == NB - 1)
                mm.then_inc(pv_done, 1)

            def wo_product(c, t):
                if t == 0:
                    pe.wait_ge(w_lo_done, 2 * KT)
                    pe.wait_ge(o_lo_done, c[0] * NG + NG)
                claim_tr(use_wo(c[0], t))
                rows = slice(t * P, (t + 1) * P)
                for g in range(NG):
                    mm = split_matmul(nc, psum_tr[:, tr_bank(use_wo, c[0], t)], (o_hi[:, g, rows], o_lo[:, g, rows]),
                                      (wo_hi[:, g], wo_lo[:, g]), g == 0, g == NG - 1)
                mm.then_inc(tr_filled, 1)

            def body(c, first, last):
                n = c[0]
                for g in range(NG):
                    there = has_before(c, g)
                    for t in range(T):
                        if there:
                            p_transposes(c, g, t)
                        if g == 1 and not first:
                            wo_product(before(*c), t)
                        if g == NG - 1 and not last:
                            x_transposes(after(*c)[0], t)
                        scores(c, g, t)
                        if there and t:
                            values(c, g, t - 1)
                        if t == T - 1 and there:
                            p_transposes(c, g, NB - 1)
                        if g < NG - 1:
                            q_part(n * NG + (g + 1), g + 1, t)
                    if there:
                        values(c, g, NB - 2)
                    if g == NG - 1 and not last:
                        pe.wait_ge(tr_free, use_xt(after(*c)[0], T - 1) + 1)
                        for k in range(KT):
                            q_part(n * NG + NG, 0, k)
                    if there:
                        values(c, g, NB - 1)

            chunks(pe, body)
            end = (NCH, NCH // 2, 0)
            for b in range(NB - 1):
                p_transposes(end, 0, b)
                if b:
                    values(end, 0, b - 1)
            p_transposes(end, 0, NB - 1)
            values(end, 0, NB - 2)
            values(end, 0, NB - 1)
            for t in range(T):
                wo_product(before(*end), t)


def spiking_ffn(nc, x_in, x_out, w_fc, w_proj):
    XT_STEP = 11
    thresholds = spike_thresholds()
    with ExitStack() as ctx:
        def sb(name, shape, dt=F32):
            return ctx.enter_context(nc.sbuf_tensor(name, shape, dt))

        def sem(name):
            return ctx.enter_context(nc.semaphore("b_" + name))

        wfc_hi = sb("wfc_hi", [P, NF, KT, P], F32R)
        wfc_lo = sb("wfc_lo", [P, NF, KT, P], F32R)
        wpr_hi = sb("wpr_hi", [P, NF, D], F32R)
        wpr_lo = sb("wpr_lo", [P, NF, D], F32R)
        xt_hi = sb("xt_hi", [P, 2, KT, CH], F32R)
        xt_lo = sb("xt_lo", [P, 2, KT, CH], F32R)
        x_rows = sb("x_rows", [P, 2, T, D])
        xn = sb("xn", [P, 2, D])
        relu = sb("relu", [P, 2, CH])
        h_hi = sb("h_hi", [P, 2, CH], F32R)
        h_lo = sb("h_lo", [P, 2, CH], F32R)
        y = sb("y", [P, T, D])
        count = sb("count", [P, 2, D])
        stats = sb("stats", [P, T, 6])
        moments = sb("moments", [P, 5, T])
        mean = sb("mean", [P, T])
        var_eps = sb("var_eps", [P, T])
        rstd = sb("rstd", [P, T])
        minus_half = sb("minus_half", [P, T])
        ident = sb("ident_b", [P, P])
        raw = y

        psum_fc = ctx.enter_context(nc.psum_tensor("psum_fc", [P, 2, CH], F32))
        psum_y = ctx.enter_context(nc.psum_tensor("psum_y", [P, T, D], F32))
        psum_xt = ctx.enter_context(nc.psum_tensor("psum_xt", [P, 2, KT * P], F32))

        ident_ready = sem("ident_ready")
        raw_loaded = [sem(f"raw_loaded{i}") for i in range(4)]
        w_hi_done, w_lo_done = sem("w_hi_done"), sem("w_lo_done")
        x_loaded, x_stored = sem("x_loaded"), sem("x_stored")
        stat_step = sem("stat_step")
        rstd_done = sem("rstd_done")
        var_ready = sem("var_ready")
        xn_ready = sem("xn_ready")
        xt_filled = sem("xt_filled")
        xt_hi_done, xt_lo_done = sem("xt_hi_done"), sem("xt_lo_done")
        fc_done = sem("fc_done")
        relu_done, sq_done = sem("relu_done"), sem("sq_done")
        h_hi_done, h_lo_done = sem("h_hi_done"), sem("h_lo_done")
        proj_done = sem("proj_done")
        y_copied = sem("y_copied")
        lif_step = sem("lif_step")
        out_ready = sem("out_ready")

        x_view = x_in.rearrange("(n t p) d -> n p t d", p=P, t=T)
        o_view = x_out.rearrange("(n t p) d -> n p t d", p=P, t=T)
        W_TILES = 2 * NF

        def w_tile(j):
            f = j // 2
            if j % 2 == 0:
                flat = lambda w: w[:, f, :, :].rearrange("p k n -> p (k n)")
                return w_fc[:, f, :], flat(wfc_hi), flat(wfc_lo)
            return w_proj[:, f, :], wpr_hi[:, f, :], wpr_lo[:, f, :]

        def chunks(engine, body):
            body(0, 0, True, False)
            with engine.Fori(1, NCH // 2) as i:
                for u in range(2):
                    body(i * 2 + (u - 1), (u + 1) % 2, False, False)
            body(NCH - 1, 1, False, True)

        block = ctx.enter_context(nc.Block())

        @block.sync
        def _(sp):
            sp.dma_start(x_rows[:, 0], x_view[0]).then_inc(x_loaded, 16)
            for j in range(W_TILES):
                if j == T:
                    sp.wait_ge(x_loaded, 16)
                    sp.dma_start(x_rows[:, 1], x_view[1]).then_inc(x_loaded, 16)
                if j >= T:
                    sp.wait_ge(w_lo_done, j - T + 1)
                sp.dma_start(raw[:, j % T, :], w_tile(j)[0]).then_inc(raw_loaded[j % T], 16)

            def body(n, par, first, last):
                if not first and not last:
                    sp.wait_ge(x_stored, 16 * T * n)
                    sp.dma_start(x_rows[:, 1 - par], x_view[n + 1]).then_inc(x_loaded, 16)
                for t in range(T):
                    sp.wait_ge(out_ready, T * n + t + 1)
                    sp.dma_start(o_view[n, :, t], x_rows[:, par, t]).then_inc(x_stored, 16)

            chunks(sp, body)
            sp.wait_ge(x_stored, 16 * T * NCH)

        @block.gpsimd
        def _(pool):
            nc.gpsimd.memset(ident[:], 0.0).then_inc(ident_ready, 1)
            pool.wait_ge(ident_ready, 1)
            nc.gpsimd.affine_select(out=ident[:], in_=ident[:], compare_op=ALU.not_equal, fill=1.0,
                                    base=0, pattern=[[-1, P]], channel_multiplier=1).then_inc(ident_ready, 1)
            nc.gpsimd.memset(minus_half[:], -0.5).then_inc(ident_ready, 1)
            pool.wait_ge(ident_ready, 3)

            def inverse_std(n):
                pool.wait_ge(var_ready, n + 1)
                nc.gpsimd.tensor_tensor(rstd[:], var_eps[:], minus_half[:], ALU.pow).then_inc(rstd_done, 1)

            def weights_lo(f):
                for j in (2 * f, 2 * f + 1):
                    pool.wait_ge(w_hi_done, j + 1)
                    _, hi, lo = w_tile(j)
                    nc.gpsimd.tensor_tensor(lo, raw[:, j % T, :], hi.bitcast(F32), ALU.subtract).then_inc(w_lo_done, 1)

            inverse_std(0)
            for f in range(2):
                weights_lo(f)

            def body(n, par, first, last):
                for f in range(NF):
                    if first and f + 2 < NF:
                        weights_lo(f + 2)
                    if f == 9 and not last:
                        inverse_std(n + 1)
                    pool.wait_ge(h_hi_done, NF * n + f + 1)
                    nc.gpsimd.tensor_tensor(h_lo[:, f % 2], relu[:, f % 2], h_hi[:, f % 2].bitcast(F32),
                                            ALU.subtract).then_inc(h_lo_done, 1)

            chunks(pool, body)

        @block.scalar
        def _(act):
            def x_hi(n, par, t):
                act.wait_ge(xt_filled, T * n + t + 1)
                nc.scalar.copy(xt_hi[:, par, :, t * P:(t + 1) * P],
                               psum_xt[:, t % 2].rearrange("p (k c) -> p k c", k=KT)).then_inc(xt_hi_done, 1)

            def weights_hi(f):
                for j in (2 * f, 2 * f + 1):
                    act.wait_ge(raw_loaded[j % T], 16 * (j // T + 1))
                    nc.scalar.copy(w_tile(j)[1], raw[:, j % T, :]).then_inc(w_hi_done, 1)

            for f in range(2):
                weights_hi(f)
            for t in range(T):
                x_hi(0, 0, t)

            def h_first(n, f):
                act.wait_ge(fc_done, NF * n + f + 1)
                if not (isinstance(n, int) and NF * n + f < 2):
                    act.wait_ge(h_lo_done, NF * n + f - 1)
                nc.scalar.activation(relu[:, f % 2], psum_fc[:, f % 2], ACT.Relu).then_inc(relu_done, 1)

            def h_second(n, f):
                act.wait_ge(sq_done, NF * n + f + 1)
                if not (isinstance(n, int) and NF * n + f < 2):
                    act.wait_ge(proj_done, NF * n + f - 1)
                nc.scalar.copy(h_hi[:, f % 2], relu[:, f % 2]).then_inc(h_hi_done, 1)

            def copy_y(n):
                act.wait_ge(proj_done, NF * (n + 1))
                for t in range(T):
                    nc.scalar.copy(y[:, t], psum_y[:, t]).then_inc(y_copied, 1)

            def body(n, par, first, last):
                for f in range(NF):
                    if first and f + 2 < NF:
                        weights_hi(f + 2)
                    h_first(n, f)
                    h_second(n, f)
                    if not last and XT_STEP <= f < XT_STEP + T:
                        x_hi(n + 1, 1 - par, f - XT_STEP)
                    if f == 0 and not first:
                        copy_y(n - 1)
                if first:
                    act.wait_ge(w_lo_done, W_TILES)
                else:
                    act.wait_ge(out_ready, T * n)
                if last:
                    copy_y(n)

            chunks(act, body)

        @block.vector
        def _(dve):
            def ln_stats(n, par, t):
                if t == 0:
                    dve.wait_ge(x_loaded, 16 * (n + 1))
                nc.vector.bn_stats(stats[:, t], x_rows[:, par, t]).then_inc(stat_step, 1)

            def ln_variance(n):
                mean_e, m2_e, mean_o, m2_o = (stats[:, :, c] for c in (1, 2, 4, 5))
                done = T * n + T + 6 * n
                dve.wait_ge(stat_step, done)
                nc.vector.tensor_tensor(moments[:, 0], mean_e, mean_o, ALU.add).then_inc(stat_step, 1)
                nc.vector.tensor_tensor(moments[:, 1], mean_e, mean_o, ALU.subtract).then_inc(stat_step, 1)
                nc.vector.tensor_tensor(moments[:, 2], m2_e, m2_o, ALU.add).then_inc(stat_step, 1)
                dve.wait_ge(stat_step, done + 2)
                nc.vector.scalar_tensor_tensor(out=moments[:, 3], in0=moments[:, 1], scalar=D / 4.0,
                                               in1=moments[:, 1], op0=ALU.mult, op1=ALU.mult).then_inc(stat_step, 1)
                nc.vector.tensor_scalar(mean[:], moments[:, 0], 0.5, None, ALU.mult).then_inc(stat_step, 1)
                dve.wait_ge(stat_step, done + 4)
                nc.vector.tensor_tensor(moments[:, 4], moments[:, 3], moments[:, 2], ALU.add).then_inc(stat_step, 1)
                dve.wait_ge(stat_step, done + 6)
                nc.vector.tensor_scalar(var_eps[:], moments[:, 4], 1.0 / D, EPS, ALU.mult, ALU.add).then_inc(var_ready, 1)

            def ln_apply(n, par, t):
                if t == 0:
                    dve.wait_ge(rstd_done, n + 1)
                if not (isinstance(n, int) and T * n + t < 2):
                    dve.wait_ge(xt_filled, T * n + t - 1)
                nc.vector.tensor_scalar(xn[:, t % 2], x_rows[:, par, t], mean[:, t:t + 1],
                                        rstd[:, t:t + 1], ALU.subtract, ALU.mult).then_inc(xn_ready, 1)

            def x_lo(n, par, t):
                dve.wait_ge(xt_hi_done, T * n + t + 1)
                cols = slice(t * P, (t + 1) * P)
                nc.vector.tensor_tensor(xt_lo[:, par, :, cols],
                                        psum_xt[:, t % 2].rearrange("p (k c) -> p k c", k=KT),
                                        xt_hi[:, par, :, cols].bitcast(F32), ALU.subtract).then_inc(xt_lo_done, 1)

            def square(n, f):
                dve.wait_ge(relu_done, NF * n + f + 1)
                nc.vector.scalar_tensor_tensor(out=relu[:, f % 2], in0=psum_fc[:, f % 2], scalar=0.0,
                                               in1=relu[:, f % 2], op0=ALU.max, op1=ALU.mult).then_inc(sq_done, 1)

            def neuron(n, par, t, s):
                c = count[:, t % 2]
                pair, j = LIF_STEPS * (T * n + t - t % 2), t % 2
                if s == 0:
                    if t >= 2:
                        dve.wait_ge(out_ready, T * n + t - 1)
                    dve.wait_ge(y_copied, T * n + t + 1)
                    nc.vector.tensor_scalar(c, y[:, t], thresholds[0], None, ALU.is_gt).then_inc(lif_step, 1)
                elif s < LIF_STEPS:
                    dve.wait_ge(lif_step, pair + 2 * s - 1 + j)
                    nc.vector.scalar_tensor_tensor(out=c, in0=y[:, t], scalar=thresholds[s], in1=c,
                                                   op0=ALU.is_gt, op1=ALU.add).then_inc(lif_step, 1)
                else:
                    dve.wait_ge(lif_step, pair + 2 * LIF_STEPS - 1 + j)
                    nc.vector.scalar_tensor_tensor(out=x_rows[:, par, t], in0=c, scalar=1.0 / LIF_STEPS,
                                                   in1=x_rows[:, par, t], op0=ALU.mult, op1=ALU.add).then_inc(out_ready, 1)

            def neurons(n, par, part):
                for s in range(2 * (part % 3), 2 * (part % 3) + 2):
                    for t in (2 * (part // 3), 2 * (part // 3) + 1):
                        neuron(n, par, t, s)

            def whole_ln(n, par):
                for t in range(T):
                    ln_stats(n, par, t)
                ln_variance(n)
                for t in range(T):
                    ln_apply(n, par, t)
                    if t >= 1:
                        x_lo(n, par, t - 1)
                x_lo(n, par, T - 1)

            dve.wait_ge(ident_ready, 3)
            whole_ln(0, 0)

            def body(n, par, first, last):
                for f in range(NF):
                    square(n, f)
                    if not first and 1 <= f <= 6:
                        neurons(n - 1, 1 - par, f - 1)
                    if last:
                        continue
                    if f == 8:
                        for t in range(T):
                            ln_stats(n + 1, 1 - par, t)
                        ln_variance(n + 1)
                    if XT_STEP - 2 <= f < XT_STEP + T - 2:
                        ln_apply(n + 1, 1 - par, f - XT_STEP + 2)
                    if XT_STEP <= f < XT_STEP + T:
                        x_lo(n + 1, 1 - par, f - XT_STEP)
                if last:
                    for part in range(6):
                        neurons(n, par, part)

            chunks(dve, body)

        @block.tensor
        def _(pe):
            def transposes(n, t):
                pe.wait_ge(xn_ready, T * n + t + 1)
                if not (isinstance(n, int) and T * n + t < 2):
                    pe.wait_ge(xt_lo_done, T * n + t - 1)
                for k in range(KT):
                    mm = nc.tensor.transpose(psum_xt[:, t % 2, k * P:(k + 1) * P], xn[:, t % 2, k * P:(k + 1) * P], ident[:])
                mm.then_inc(xt_filled, 1)

            def hidden(n, par, f):
                if not (isinstance(n, int) and NF * n + f < 2):
                    pe.wait_ge(sq_done, NF * n + f - 1)
                for k in range(KT):
                    mm = split_matmul(nc, psum_fc[:, f % 2], (wfc_hi[:, f, k], wfc_lo[:, f, k]),
                                      (xt_hi[:, par, k], xt_lo[:, par, k]), k == 0, k == KT - 1)
                mm.then_inc(fc_done, 1)

            def project(n, f):
                pe.wait_ge(h_lo_done, NF * n + f + 1)
                for t in range(T):
                    cols = slice(t * P, (t + 1) * P)
                    mm = split_matmul(nc, psum_y[:, t], (h_hi[:, f % 2, cols], h_lo[:, f % 2, cols]),
                                      (wpr_hi[:, f], wpr_lo[:, f]), f == 0, f == NF - 1)
                mm.then_inc(proj_done, 1)

            pe.wait_ge(ident_ready, 3)
            for t in range(T):
                transposes(0, t)

            pe.wait_ge(xt_lo_done, T)
            pe.wait_ge(w_lo_done, 2)
            hidden(0, 0, 0)

            def body(n, par, first, last):
                for f in range(NF):
                    if not last and XT_STEP <= f < XT_STEP + T:
                        transposes(n + 1, f - XT_STEP)
                    if f + 1 < NF:
                        if first:
                            pe.wait_ge(w_lo_done, 2 * (f + 2))
                        hidden(n, par, f + 1)
                    elif not last:
                        pe.wait_ge(xt_lo_done, T * (n + 2))
                        hidden(n + 1, 1 - par, 0)
                    if f == 0 and not first:
                        pe.wait_ge(y_copied, T * n)
                    project(n, f)

            chunks(pe, body)



def single_head_attention_and_linear(nc, x_in, x_out, ctx_t, wq_t, bq, wk, bk, wv, bv, cb_t, scb, bias):
    KC = CTXD // P
    HK = CTX // 2
    NT = ROWS // P
    LAST_LAG = 6
    with ExitStack() as ctx:
        def sb(name, shape, dt=F32):
            return ctx.enter_context(nc.sbuf_tensor(name, shape, dt))

        def bank(name, shape):
            return ctx.enter_context(nc.psum_tensor(name, shape, F32))

        def sem(name):
            return ctx.enter_context(nc.semaphore("c_" + name))

        x_all = sb("x_all", [P, NT, D])
        ctx_sb = sb("ctx_sb", [P, KC, BATCH * CTX])
        wk_sb, wv_sb = sb("wk_sb", [P, KC, D]), sb("wv_sb", [P, KC, D])
        wq_sb = sb("wq_sb", [P, KT, D])
        bq_sb, bk_sb = sb("bq_sb", [P, KT]), sb("bk_sb", [P, KT])
        bv_rows, bias_rows, scb_rows = sb("bv_rows", [P, D]), sb("bias_rows", [P, D]), sb("scb_rows", [P, D])
        k_t = sb("k_t", [P, KT, BATCH * CTX])
        m_hi, m_lo = sb("m_hi", [P, KT, BATCH * CTX], F32R), sb("m_lo", [P, KT, BATCH * CTX], F32R)
        bqk = sb("bqk", [P, BATCH * CTX])
        bqk_hi, bqk_lo = sb("bqk_hi", [P, BATCH * CTX], F32R), sb("bqk_lo", [P, BATCH * CTX], F32R)
        v_rows = sb("v_rows", [HK, 2, D])
        v_hi, v_lo = sb("v_hi", [HK, BATCH, 2, D], F32R), sb("v_lo", [HK, BATCH, 2, D], F32R)
        cb_raw = sb("cb_raw", [P, KT, D])
        cb_hi, cb_lo = sb("cb_hi", [P, KT, D], F32R), sb("cb_lo", [P, KT, D], F32R)
        ident, ones, ones_r = sb("ident_c", [P, P]), sb("ones_c", [P, P]), sb("ones_r", [P, P], F32R)
        minus_half = sb("minus_half_c", [P, 1])

        stats = [sb(f"stats{a}", [P, 2, 6]) for a in (1, 2)]
        mean_var = [sb(f"mean_var{a}", [P, 2, 2]) for a in (1, 2)]
        var_eps = [sb(f"var_eps{a}", [P, 2]) for a in (1, 2)]
        rstd = [sb(f"rstd{a}", [P, 2]) for a in (1, 2)]
        xn = [sb(f"xn{a}", [P, 2, D]) for a in (1, 2)]
        xt_hi = [sb(f"xt_hi{a}", [P, 2, KT, P], F32R) for a in (1, 2)]
        xt_lo = [sb(f"xt_lo{a}", [P, 2, KT, P], F32R) for a in (1, 2)]
        minus_max, weight_sum, inv_sum = sb("minus_max", [P, 2]), sb("weight_sum", [P, 2]), sb("inv_sum", [P, 2])
        probs = sb("probs", [P, 2, CTX])
        pt_hi, pt_lo = sb("pt_hi", [HK, 2, 2, P], F32R), sb("pt_lo", [HK, 2, 2, P], F32R)
        scaled = sb("scaled", [P, 2, D])

        psum_xt = [bank(f"psum_xt{a}", [P, KT, P]) for a in (1, 2)]
        psum_s, psum_pt = bank("psum_s", [P, CTX]), bank("psum_pt", [HK, 2, P])
        psum_o, psum_f = bank("psum_o", [P, D]), bank("psum_f", [P, D])
        psum_prep = bank("psum_prep", [P, 2, D])

        consts_loaded = sem("consts_loaded")
        consts_set, ones_ready = sem("consts_set"), sem("ones_ready")
        prep_filled, prep_read = sem("prep_filled"), sem("prep_read")
        prep_step, weights_ready = sem("prep_step"), sem("weights_ready")
        x_loaded, x_stored = sem("x_loaded"), sem("x_stored")
        stats_done = [sem(f"stats_done{a}") for a in (1, 2)]
        mean_var_done = [sem(f"mean_var_done{a}") for a in (1, 2)]
        var_eps_done = [sem(f"var_eps_done{a}") for a in (1, 2)]
        rstd_done = [sem(f"rstd_done{a}") for a in (1, 2)]
        xn_ready = [sem(f"xn_ready{a}") for a in (1, 2)]
        xt_filled = [sem(f"xt_filled{a}") for a in (1, 2)]
        xt_hi_done = [sem(f"xt_hi_done{a}") for a in (1, 2)]
        xt_lo_done = [sem(f"xt_lo_done{a}") for a in (1, 2)]
        s_filled, max_done, exp_done = sem("s_filled"), sem("max_done"), sem("exp_done")
        pt_filled, pt_hi_done, pt_lo_done = sem("pt_filled"), sem("pt_hi_done"), sem("pt_lo_done")
        inv_done, o_filled, x_mid = sem("inv_done"), sem("o_filled"), sem("x_mid")
        f_filled, scaled_done, biased, out_ready = sem("f_filled"), sem("scaled_done"), sem("biased"), sem("out_ready")
        spare = sem("spare")

        x_view = x_in.rearrange("(b i s p) d -> b i p s d", b=BATCH, s=2, p=P)
        o_view = x_out.rearrange("(b i s p) d -> b i p s d", b=BATCH, s=2, p=P)
        slots = x_all[:].rearrange("p (m b) d -> p m b d", b=BATCH)

        def steps(engine, step):
            begin, end = 7, NT - 1
            known = lambda q: isinstance(q, int)
            for g in range(-1, begin):
                step(g, g % 4, lambda q: 0 <= q < NT)
            with engine.Fori(0, (end - begin) // 4) as i:
                for u in range(4):
                    step(i * 4 + (begin + u), (begin + u) % 4, lambda q: True)
            for g in range(end, NT + LAST_LAG):
                step(g, g % 4, lambda q: 0 <= q < NT)

        def free(engine, sem, q, ring):
            if isinstance(q, int):
                if q - ring >= 0:
                    engine.wait_ge(sem, q - ring + 1)
            else:
                engine.wait_ge(sem, q + (1 - ring))

        block = ctx.enter_context(nc.Block())

        @block.sync
        def _(sp):
            def load(m):
                for b in range(BATCH):
                    sp.dma_start(slots[:, 2 * m:2 * m + 2, b], x_view[b, m]).then_inc(x_loaded, 16)

            for dst, src in ((ctx_sb, ctx_t), (wk_sb, wk), (bk_sb, bk), (wq_sb, wq_t), (bq_sb, bq), (wv_sb, wv)):
                sp.dma_start(dst[:], src).then_inc(consts_loaded, 16)
            for dst, src in ((bv_rows, bv), (bias_rows, bias), (scb_rows, scb)):
                sp.dma_start(dst[:], src.broadcast_to([P, D])).then_inc(consts_loaded, 16)
            load(0)
            sp.dma_start(cb_raw[:], cb_t).then_inc(consts_loaded, 16)
            for m in range(1, NT // 4):
                sp.wait_ge(x_loaded, 32 * m)
                load(m)
            with sp.Fori(0, NT // 4) as m:
                sp.wait_ge(out_ready, m * 4 + 4)
                for b in range(BATCH):
                    sp.dma_start(o_view[b, m], slots[:, bass.ds(m * 2, 2), b]).then_inc(x_stored, 16)
            sp.wait_ge(x_stored, 32 * (NT // 4))

        @block.gpsimd
        def _(pool):
            nc.gpsimd.memset(ident[:], 0.0).then_inc(consts_set, 1)
            pool.wait_ge(consts_set, 1)
            nc.gpsimd.affine_select(out=ident[:], in_=ident[:], compare_op=ALU.not_equal, fill=1.0,
                                    base=0, pattern=[[-1, P]], channel_multiplier=1).then_inc(consts_set, 1)
            nc.gpsimd.memset(minus_half[:], -0.5).then_inc(consts_set, 1)
            nc.gpsimd.memset(ones[:], 1.0).then_inc(consts_set, 1)
            pool.wait_ge(consts_set, 4)
            pool.wait_ge(consts_loaded, 16 * 10)

            def inverse_std(a, q, par):
                wait_apart(pool, mean_var_done[a], q + 1, spare)
                nc.gpsimd.tensor_scalar(var_eps[a][:, par:par + 1], mean_var[a][:, par, 1:2], EPS, None,
                                        ALU.add).then_inc(var_eps_done[a], 1)
                pool.wait_ge(var_eps_done[a], q + 1)
                nc.gpsimd.tensor_tensor(rstd[a][:, par:par + 1], var_eps[a][:, par:par + 1], minus_half[:],
                                        ALU.pow).then_inc(rstd_done[a], 1)

            def step(g, r, has):
                if has(g + 1):
                    inverse_std(0, g + 1, (r + 1) % 2)
                if has(g - 5):
                    wait_apart(pool, xn_ready[1], g - 4, spare)
                    nc.gpsimd.tensor_tensor(x_all[:, g - 5], x_all[:, g - 5], bias_rows[:], ALU.add).then_inc(biased, 1)
                if has(g - 3):
                    inverse_std(1, g - 3, (r + 1) % 2)
                if has(g - 6):
                    pool.wait_ge(biased, g - 5)
                    wait_apart(pool, scaled_done, g - 5, spare)
                    nc.gpsimd.tensor_tensor(x_all[:, g - 6], scaled[:, r % 2], x_all[:, g - 6], ALU.add).then_inc(out_ready, 1)

            steps(pool, step)

        @block.scalar
        def _(act):
            act.wait_ge(consts_loaded, 16 * 10)
            for k in range(KT):
                nc.scalar.copy(cb_hi[:, k], cb_raw[:, k]).then_inc(weights_ready, 1)

            def copy_hi(filled, q, out, in_, done):
                act.wait_ge(filled, q + 1)
                nc.scalar.copy(out, in_).then_inc(done, 1)

            def step(g, r, has):
                if has(g):
                    free(act, s_filled, g, 2)
                    copy_hi(xt_filled[0], g, xt_hi[0][:, r % 2], psum_xt[0][:], xt_hi_done[0])
                if has(g - 1):
                    par = (r + 1) % 2
                    free(act, pt_filled, g - 1, 2)
                    free(act, inv_done, g - 1, 2)
                    act.wait_ge(max_done, g)
                    nc.scalar.activation(probs[:, par], psum_s[:], ACT.Exp, bias=minus_max[:, par:par + 1],
                                         accum_out=weight_sum[:, par:par + 1]).then_inc(exp_done, 1)
                if has(g - 2):
                    free(act, o_filled, g - 2, 2)
                    copy_hi(pt_filled, g - 2, pt_hi[:, r % 2], psum_pt[:], pt_hi_done)
                if has(g - 5):
                    free(act, f_filled, g - 5, 2)
                    copy_hi(xt_filled[1], g - 5, xt_hi[1][:, (r + 1) % 2], psum_xt[1][:], xt_hi_done[1])

            steps(act, step)

        @block.vector
        def _(dve):
            dve.wait_ge(consts_set, 4)
            nc.vector.tensor_copy(ones_r[:], ones[:]).then_inc(ones_ready, 1)
            dve.wait_ge(consts_loaded, 16 * 10)
            nc.vector.tensor_scalar(scb_rows[:], scb_rows[:], 1.0 / 127.0, None, ALU.mult).then_inc(prep_step, 1)
            for e in range(KT):
                dve.wait_ge(prep_filled, e + 1)
                nc.vector.tensor_scalar(k_t[:, e], psum_prep[:, e % 2, 0:BATCH * CTX], bk_sb[:, e:e + 1], None,
                                        ALU.add).then_inc(prep_read, 1)
            dve.wait_ge(prep_read, KT)
            nc.vector.tensor_scalar(bqk[:], k_t[:, 0], bq_sb[:, 0:1], None, ALU.mult).then_inc(prep_step, 1)
            for e in range(1, KT):
                dve.wait_ge(prep_step, e + 1)
                nc.vector.scalar_tensor_tensor(out=bqk[:], in0=k_t[:, e], scalar=bq_sb[:, e:e + 1], in1=bqk[:],
                                               op0=ALU.mult, op1=ALU.add).then_inc(prep_step, 1)
            dve.wait_ge(prep_step, KT + 1)
            nc.vector.tensor_copy(bqk_hi[:], bqk[:]).then_inc(prep_step, 1)
            dve.wait_ge(prep_step, KT + 2)
            nc.vector.tensor_tensor(bqk_lo[:], bqk[:], bqk_hi[:].bitcast(F32), ALU.subtract).then_inc(prep_step, 1)
            for k in range(KT):
                src = psum_prep[:, k % 2, 0:BATCH * CTX]
                dve.wait_ge(prep_filled, KT + k + 1)
                nc.vector.tensor_copy(m_hi[:, k], src).then_inc(prep_step, 1)
                dve.wait_ge(prep_step, KT + 4 + k)
                nc.vector.tensor_tensor(m_lo[:, k], src, m_hi[:, k].bitcast(F32), ALU.subtract).then_inc(prep_read, 1)
            for j in range(2 * BATCH):
                b, half = j // 2, j % 2
                base = 2 * KT + 3 + 2 * j
                dve.wait_ge(prep_filled, 2 * KT + j + 1)
                nc.vector.tensor_tensor(v_rows[:, half], psum_prep[0:HK, j % 2], bv_rows[0:HK], ALU.add).then_inc(prep_read, 1)
                dve.wait_ge(prep_read, 2 * KT + j + 1)
                nc.vector.tensor_copy(v_hi[:, b, half], v_rows[:, half]).then_inc(prep_step, 1)
                dve.wait_ge(prep_step, base + 1)
                nc.vector.tensor_tensor(v_lo[:, b, half], v_rows[:, half], v_hi[:, b, half].bitcast(F32),
                                        ALU.subtract).then_inc(prep_step, 1)
                dve.wait_ge(prep_step, base + 2)
            for k in range(KT):
                dve.wait_ge(weights_ready, KT + k if k else KT)
                nc.vector.tensor_tensor(cb_lo[:, k], cb_raw[:, k], cb_hi[:, k].bitcast(F32),
                                        ALU.subtract).then_inc(weights_ready, 1)

            def x_lo(a, q, par):
                dve.wait_ge(xt_hi_done[a], q + 1)
                nc.vector.tensor_tensor(xt_lo[a][:, par], psum_xt[a][:], xt_hi[a][:, par].bitcast(F32),
                                        ALU.subtract).then_inc(xt_lo_done[a], 1)

            def ln_apply(a, q, par):
                dve.wait_ge(rstd_done[a], q + 1)
                free(dve, xt_filled[a], q, 2)
                nc.vector.tensor_scalar(xn[a][:, par], x_all[:, q], mean_var[a][:, par, 0:1],
                                        rstd[a][:, par:par + 1], ALU.subtract, ALU.mult).then_inc(xn_ready[a], 1)

            def step(g, r, has):
                even, odd = r % 2, (r + 1) % 2
                if has(g + 1):
                    free(dve, xn_ready[0], g + 1, 2)
                    if r == 3:
                        wait_apart(dve, x_loaded, (g + 1) * 8 + 32, spare)
                    else:
                        free(dve, stats_done[0], g + 1, 1)
                        dve.sem_inc(spare, 1)
                    nc.vector.bn_stats(stats[0][:, odd], x_all[:, g + 1]).then_inc(stats_done[0], 1)
                    wait_apart(dve, stats_done[0], g + 2, spare)
                    nc.vector.bn_aggr(mean_var[0][:, odd], stats[0][:, odd]).then_inc(mean_var_done[0], 1)
                if has(g):
                    x_lo(0, g, even)
                if has(g - 1):
                    free(dve, exp_done, g - 1, 2)
                    dve.wait_ge(s_filled, g)
                    nc.vector.tensor_reduce(minus_max[:, odd:odd + 1], psum_s[:], AX_X, ALU.max,
                                            negate=True).then_inc(max_done, 1)
                if has(g - 2):
                    dve.wait_ge(pt_hi_done, g - 1)
                    nc.vector.tensor_tensor(pt_lo[:, even], psum_pt[:], pt_hi[:, even].bitcast(F32),
                                            ALU.subtract).then_inc(pt_lo_done, 1)
                    dve.wait_ge(exp_done, g - 1)
                    free(dve, x_mid, g - 2, 2)
                    nc.vector.reciprocal(inv_sum[:, even:even + 1], weight_sum[:, even:even + 1]).then_inc(inv_done, 1)
                if has(g + 1):
                    ln_apply(0, g + 1, odd)
                if has(g - 3):
                    dve.wait_ge(inv_done, g - 2)
                    dve.wait_ge(o_filled, g - 2)
                    nc.vector.scalar_tensor_tensor(out=x_all[:, g - 3], in0=psum_o[:], scalar=inv_sum[:, odd:odd + 1],
                                                   in1=x_all[:, g - 3], op0=ALU.mult, op1=ALU.add).then_inc(x_mid, 1)
                if has(g - 4):
                    ln_apply(1, g - 4, even)
                if has(g - 3):
                    free(dve, xn_ready[1], g - 3, 2)
                    wait_apart(dve, x_mid, g - 2, spare)
                    nc.vector.bn_stats(stats[1][:, odd], x_all[:, g - 3]).then_inc(stats_done[1], 1)
                    wait_apart(dve, stats_done[1], g - 2, spare)
                    nc.vector.bn_aggr(mean_var[1][:, odd], stats[1][:, odd]).then_inc(mean_var_done[1], 1)
                if has(g - 5):
                    x_lo(1, g - 5, odd)
                if has(g - 6):
                    free(dve, out_ready, g - 6, 2)
                    dve.wait_ge(f_filled, g - 5)
                    nc.vector.tensor_tensor(scaled[:, even], psum_f[:], scb_rows[:], ALU.mult).then_inc(scaled_done, 1)

            steps(dve, step)

        @block.tensor
        def _(pe):
            pe.wait_ge(consts_loaded, 16 * 10)
            use = 0

            def prep_group(out, pairs):
                nonlocal use
                if use >= 2:
                    pe.wait_ge(prep_read, use - 1)
                for k, (stat, mov) in enumerate(pairs):
                    mm = nc.tensor.matmul(out, stat, mov, start=(k == 0), stop=(k == len(pairs) - 1))
                mm.then_inc(prep_filled, 1)
                use += 1

            for e in range(KT):
                prep_group(psum_prep[:, use % 2, 0:BATCH * CTX],
                           [(wk_sb[:, k, e * P:(e + 1) * P], ctx_sb[:, k]) for k in range(KC)])
            pe.wait_ge(prep_read, KT)
            for d in range(KT):
                prep_group(psum_prep[:, use % 2, 0:BATCH * CTX],
                           [(wq_sb[:, e, d * P:(d + 1) * P], k_t[:, e]) for e in range(KT)])
            for j in range(2 * BATCH):
                prep_group(psum_prep[0:HK, use % 2],
                           [(ctx_sb[:, k, j * HK:(j + 1) * HK], wv_sb[:, k]) for k in range(KC)])

            def transposes(a, q, par):
                pe.wait_ge(xn_ready[a], q + 1)
                free(pe, xt_lo_done[a], q, 1)
                for k in range(KT):
                    mm = nc.tensor.transpose(psum_xt[a][:, k], xn[a][:, par, k * P:(k + 1) * P], ident[:])
                mm.then_inc(xt_filled[a], 1)

            pe.wait_ge(ones_ready, 1)
            pe.wait_ge(weights_ready, 2 * KT)

            def step(g, r, has):
                even, odd = r % 2, (r + 1) % 2
                if has(g):
                    transposes(0, g, even)
                if has(g - 1):
                    keys = slice(odd * CTX, (odd + 1) * CTX)
                    pe.wait_ge(xt_lo_done[0], g)
                    free(pe, exp_done, g - 1, 1)
                    for k in range(KT):
                        split_matmul(nc, psum_s[:], (xt_hi[0][:, odd, k], xt_lo[0][:, odd, k]),
                                     (m_hi[:, k, keys], m_lo[:, k, keys]), k == 0, False)
                    nc.tensor.matmul(psum_s[:], ones_r[:], bqk_hi[:, keys], start=False, stop=False)
                    nc.tensor.matmul(psum_s[:], ones_r[:], bqk_lo[:, keys], start=False, stop=True).then_inc(s_filled, 1)
                if has(g - 2):
                    pe.wait_ge(exp_done, g - 1)
                    free(pe, pt_lo_done, g - 2, 1)
                    for half in range(2):
                        mm = nc.tensor.transpose(psum_pt[:, half], probs[:, even, half * HK:(half + 1) * HK], ident[:])
                    mm.then_inc(pt_filled, 1)
                if has(g - 3):
                    pe.wait_ge(pt_lo_done, g - 2)
                    free(pe, x_mid, g - 3, 1)
                    for half in range(2):
                        mm = split_matmul(nc, psum_o[:], (pt_hi[:, odd, half], pt_lo[:, odd, half]),
                                          (v_hi[:, odd, half], v_lo[:, odd, half]), half == 0, half == 1)
                    mm.then_inc(o_filled, 1)
                if has(g - 5):
                    transposes(1, g - 5, odd)
                if has(g - 6):
                    pe.wait_ge(xt_lo_done[1], g - 5)
                    free(pe, scaled_done, g - 6, 1)
                    for k in range(KT):
                        mm = split_matmul(nc, psum_f[:], (xt_hi[1][:, even, k], xt_lo[1][:, even, k]),
                                          (cb_hi[:, k], cb_lo[:, k]), k == 0, k == KT - 1)
                    mm.then_inc(f_filled, 1)

            steps(pe, step)


def cross_attention_ffn_twice(nc, a, out):
    x1 = nc.dram_tensor("x_after_attention", (ROWS, D), F32, kind="Internal").ap()
    x2 = nc.dram_tensor("x_after_spikes", (ROWS, D), F32, kind="Internal").ap()
    multi_head_attention(nc, a["x"], x1, a["ctx_t"], a["wq0_t"], a["wk0_t"], a["wv0_t"], a["wo0_t"])
    spiking_ffn(nc, x1, x2, a["w_fc"], a["w_proj"])
    single_head_attention_and_linear(nc, x2, out, a["ctx_t"], a["wq1_t"], a["bq1"], a["wk1"], a["bk1"],
                                     a["wv1"], a["bv1"], a["cb_t"], a["scb"], a["bias"])


def kernel(**inputs):
    import numpy as _np
    import concourse.bacc as _bacc
    from concourse import mybir as _mybir
    from concourse.bass_utils import run_bass_kernel_spmd as _run

    g = {k: _np.asarray(v) for k, v in inputs.items()}

    def tiles(w):
        return w.reshape(-1, 128, w.shape[-1]).transpose(1, 0, 2)

    def column(v):
        return v.reshape(-1, 128).T

    w_kv = g["L0_xattn_Wkv"]
    arrays = {
        "x": g["x"].reshape(ROWS, D),
        "ctx_t": tiles(g["ctx_512"].reshape(BATCH * CTX, CTXD).T),
        "wq0_t": tiles(g["L0_xattn_Wq"].T), "wk0_t": tiles(w_kv[:D].T), "wv0_t": tiles(w_kv[D:].T),
        "wo0_t": tiles(g["L0_xattn_Wo"].T),
        "w_fc": g["L0_ffn_W_fc"].T.reshape(KT, P, NF, P).transpose(1, 2, 0, 3).reshape(P, NF, KT * P),
        "w_proj": tiles(g["L0_ffn_W_proj"].T),
        "wq1_t": tiles(g["L1_xattn_Wq"].T), "bq1": column(g["L1_xattn_bq"]),
        "wk1": tiles(g["L1_xattn_Wk"]), "bk1": column(g["L1_xattn_bk"]),
        "wv1": tiles(g["L1_xattn_Wv"]), "bv1": g["L1_xattn_bv"].reshape(1, D),
        "cb_t": tiles(g["L1_ffn_CB"].T),
        "scb": g["L1_ffn_SCB"].reshape(1, D), "bias": g["L1_ffn_bias"].reshape(1, D),
    }
    nc = _bacc.Bacc("TRN2", target_bir_lowering=False, num_devices=1)
    args, sent = {}, {}
    for name, a in arrays.items():
        a = _np.ascontiguousarray(a)
        sent[f"in_{name}_dram"] = a
        args[name] = nc.dram_tensor(f"in_{name}_dram", a.shape, _mybir.dt.from_np(a.dtype), kind="ExternalInput").ap()
    out = nc.dram_tensor("out_0_dram", (ROWS, D), _mybir.dt.float32, kind="ExternalOutput").ap()
    cross_attention_ffn_twice(nc, args, out)
    r = _run(nc, [sent], core_ids=[0])
    return r.results[0]["out_0_dram"].reshape(BATCH, SEQ, D)
```

```python
from contextlib import ExitStack

import concourse.bass as bass
import numpy as np
from concourse import mybir
from concourse.alu_op_type import AluOpType as ALU

ACT = mybir.ActivationFunctionType
AX_X = mybir.AxisListType.X
F32 = mybir.dt.float32
F32R = mybir.dt.float32r

P = 128
D = 512
BATCH, SEQ = 2, 2048
ROWS = BATCH * SEQ
CTX, CTXD = 154, 256
HEADS, HD = 16, 32
FF = 2048
KT = D // P
T = 4
CH = T * P
NCH = ROWS // CH
NF = FF // P
EPS = 1e-5
LIF_BETA, LIF_THRESHOLD, LIF_STEPS = 0.9, 1.0, 5


def split_matmul(nc, out, stat, mov, start, stop):
    nc.tensor.matmul(out, stat[0], mov[0], start=start, stop=False)
    nc.tensor.matmul(out, stat[0], mov[1], start=False, stop=False)
    return nc.tensor.matmul(out, stat[1], mov[0], start=False, stop=stop)


def spike_thresholds():
    one, beta = np.float32(LIF_THRESHOLD), np.float32(LIF_BETA)

    def count(y):
        mem, n = np.float32(0), 0
        for _ in range(LIF_STEPS):
            reset = one if mem > one else np.float32(0)
            mem = np.float32(np.float32(beta * mem + y) - reset)
            n += bool(mem > one)
        return n

    found = []
    for n in range(LIF_STEPS):
        low, high = np.float32(0), np.float32(2)
        while np.nextafter(low, high) < high:
            mid = np.float32((np.float64(low) + np.float64(high)) / 2)
            if mid in (low, high):
                break
            low, high = (low, mid) if count(mid) > n else (mid, high)
        found.append(float(low))
    return found


def wait_apart(engine, sem, value, spare):
    engine.wait_ge(sem, value)
    engine.sem_inc(spare, 1)



def multi_head_attention(nc, x_in, x_out, ctx_t, wq_t, wk_t, wv_t, wo_t):
    KC = CTXD // P
    NG = HEADS * HD // P
    GH = P // HD
    GC = GH * CTX
    NB = -(-GC // P)
    size = [min(P, GC - b * P) for b in range(NB)]
    SCALE = HD ** -0.5
    with ExitStack() as ctx:
        def sb(name, shape, dt=F32):
            return ctx.enter_context(nc.sbuf_tensor(name, shape, dt))

        def bank(name, shape):
            return ctx.enter_context(nc.psum_tensor(name, shape, F32))

        def sem(name):
            return ctx.enter_context(nc.semaphore("a_" + name))

        wq_hi, wq_lo = sb("wq_hi", [P, KT, D], F32R), sb("wq_lo", [P, KT, D], F32R)
        wo_hi, wo_lo = sb("wo_hi", [P, NG, D], F32R), sb("wo_lo", [P, NG, D], F32R)
        k_hi, k_lo = sb("k_hi", [P, BATCH, NG, GC], F32R), sb("k_lo", [P, BATCH, NG, GC], F32R)
        v_hi, v_lo = sb("va_hi", [P, BATCH, NG, NB, P], F32R), sb("va_lo", [P, BATCH, NG, NB, P], F32R)
        x_ln = sb("x_ln", [P, T, D])
        x_res = sb("x_res", [P, 2, D])
        xt_hi, xt_lo = sb("xta_hi", [P, KT, CH], F32R), sb("xta_lo", [P, KT, CH], F32R)
        q_hi, q_lo = sb("q_hi", [P, 2, CH], F32R), sb("q_lo", [P, 2, CH], F32R)
        probs = sb("probs_a", [P, 2, T, GC])
        pt_hi, pt_lo = sb("pta_hi", [P, NB, CH], F32R), sb("pta_lo", [P, NB, CH], F32R)
        o_hi, o_lo = sb("o_hi", [P, NG, CH], F32R), sb("o_lo", [P, NG, CH], F32R)
        ctx_sb = sb("ctx_a", [P, KC, BATCH * CTX])
        mask = sb("mask", [P, NB, GH])
        ident = sb("ident_a", [P, P])
        minus_half = sb("minus_half_a", [P, 1])
        stats, mean_var = sb("stats_a", [P, T, 6]), sb("mean_var_a", [P, T, 2])
        var_eps, rstd = sb("var_eps_a", [P, T]), sb("rstd_a", [P, T])
        minus_max, bias_max = sb("minus_max_a", [P, T, GH]), sb("bias_max_a", [P, T, GH])
        weight_sum, inv_sum = sb("weight_sum_a", [P, T, GH]), sb("inv_sum_a", [P, T, GH])
        flat = probs[:].rearrange("p a t c -> p a (t c)")
        ctx_rep = [flat[:, b, 0:KC * GC].rearrange("p (k c) -> p k c", k=KC) for b in range(BATCH)]
        wk_sb, wv_sb = (flat[:, b, KC * GC:KC * (GC + D)].rearrange("p (k n) -> p k n", k=KC) for b in range(2))
        heads_of = [range(b * P // CTX, (b * P + size[b] - 1) // CTX + 1) for b in range(NB)]
        PIECES = sum(len(heads) for heads in heads_of)

        psum_s = bank("psum_s_a", [P, 2, 2, 512])
        psum_tr = bank("psum_tr", [P, 2, 512])
        psum_q, psum_o = bank("psum_q", [P, CH]), bank("psum_o_a", [P, CH])

        ctx_loaded, rep_loaded = sem("ctx_loaded"), [sem("rep_loaded0"), sem("rep_loaded1")]
        raw_loaded = [sem("raw_loaded0"), sem("raw_loaded1")]
        consts_set, k_hi_zeroed, k_lo_zeroed = sem("consts_set"), sem("k_hi_zeroed"), sem("k_lo_zeroed")
        v_zeroed = sem("v_zeroed")
        k_filled, k_hi_done, k_lo_done = sem("k_filled"), sem("k_hi_done"), sem("k_lo_done")
        v_filled, v_hi_done, v_lo_done = sem("v_filled"), sem("v_hi_done"), sem("v_lo_done")
        w_hi_done, w_lo_done = sem("w_hi_done"), sem("w_lo_done")
        ln_loaded = [sem("ln_loaded0"), sem("ln_loaded1")]
        stats_done, mean_var_done, var_eps_done = sem("stats_done"), sem("mean_var_done"), sem("var_eps_done")
        rstd_done, xn_ready, xt_hi_done = sem("rstd_done"), sem("xn_ready"), sem("xt_hi_done")
        tr_filled, tr_free = sem("tr_filled"), sem("tr_free")
        q_filled, q_hi_done, q_lo_done = sem("q_filled"), sem("q_hi_done"), sem("q_lo_done")
        o_hi_done, o_lo_done = sem("o_hi_done"), sem("o_lo_done")
        pt_hi_done, pv_done = sem("pt_hi_done"), sem("pv_done")
        s_filled, max_done, bias_done = sem("s_filled"), sem("max_done"), sem("bias_done")
        exp_done, inv_done, probs_ready = sem("exp_done"), sem("inv_done"), sem("probs_ready")
        res_loaded, x_stored = [sem("res_loaded0"), sem("res_loaded1")], [sem("x_stored0"), sem("x_stored1")]
        spare = sem("spare")

        x_view = x_in.rearrange("(b m t p) d -> b m t p d", b=BATCH, t=T, p=P)
        o_view = x_out.rearrange("(b m t p) d -> b m t p d", b=BATCH, t=T, p=P)

        def after(n, m, par):
            return (n + 1, m + par, 1 - par)

        def before(n, m, par):
            return (n - 1, m - 1 + par, 1 - par)

        def chunks(engine, body):
            body((0, 0, 0), True, False)
            with engine.Fori(1, NCH // 2) as i:
                body((i * 2 - 1, i - 1, 1), False, False)
                body((i * 2, i, 0), False, False)
            body((NCH - 1, NCH // 2 - 1, 1), False, True)

        TR_USES = NG * NB + 2 * T
        step_start = [0, NB, 2 * NB + T, 3 * NB + T]

        def is_chunk(n, number):
            return isinstance(n, int) and n == number

        def use_pt(n, g, b):
            if is_chunk(n, 0) and g == 1:
                return T + b
            alone = g in (0, 2) or (g == NG - 1 and is_chunk(n, NCH - 1))
            place = b if alone else min(2 * b, NB + T - 1)
            return n * TR_USES + (step_start[g] + place - NB - (T if is_chunk(n, NCH) else 0))

        def use_wo(n, t):
            if is_chunk(n, NCH - 1):
                return NCH * TR_USES - T + t
            return (n + 1) * TR_USES + (2 * t + 1)

        def use_xt(n, t):
            if is_chunk(n, 0):
                return t
            return (n - 1) * TR_USES + (step_start[NG - 1] + 2 * t + 1 - NB)

        def tr_bank(use, n, *place):
            return use(n if isinstance(n, int) else 2, *place) % 2

        assert TR_USES % 2 == 0

        def has_before(c, g):
            return not (isinstance(c[0], int) and c[0] == 0 and g <= 0)

        def v_bank(j):
            return (psum_o[:], psum_q[:])[j % 2] if j < NB else (psum_tr[:, 0], psum_tr[:, 1], psum_o[:])[(j - NB) % 3]

        def v_source(j):
            return v_bank(j).rearrange("p (g c) -> p g c", g=NG)

        def v_pieces(j):
            return sum(len(heads_of[i % NB]) for i in range(j))

        block = ctx.enter_context(nc.Block())

        @block.sync
        def _(sp):
            def load_ln(c, t):
                n, m, par = c
                sp.dma_start(x_ln[:, t], x_view[par, m, t]).then_inc(ln_loaded[t % 2], 16)

            def load_res(c, t):
                n, m, par = c
                if not (isinstance(n, int) and 2 * n + t // 2 == 0):
                    sp.wait_ge(x_stored[t % 2], (n * 2 + t // 2) * 16)
                sp.dma_start(x_res[:, t % 2], x_view[par, m, t]).then_inc(res_loaded[t % 2], 16)

            def load_weights(js):
                for j in js:
                    if j >= 2:
                        sp.wait_ge(w_lo_done, j - 1)
                    src = wq_t[:, j] if j < KT else wo_t[:, j - KT]
                    sp.dma_start(x_res[:, j % 2], src).then_inc(raw_loaded[j % 2], 16)

            for t in range(2):
                load_ln((0, 0, 0), t)
            sp.dma_start(ctx_sb[:], ctx_t).then_inc(ctx_loaded, 16)
            sp.dma_start(wk_sb, wk_t).then_inc(ctx_loaded, 16)
            for t in range(2, T):
                sp.wait_ge(ln_loaded[t % 2], 16)
                load_ln((0, 0, 0), t)
            load_weights(range(2))
            sp.dma_start(wv_sb, wv_t).then_inc(rep_loaded[0], 16)
            for b in range(BATCH):
                for h in range(GH):
                    sp.dma_start(ctx_rep[b][:, :, h * CTX:(h + 1) * CTX],
                                 ctx_t[:, :, b * CTX:(b + 1) * CTX]).then_inc(rep_loaded[b], 16)
            load_weights(range(2, KT + 2))

            def residual(c):
                n, m, par = c
                load_res(c, 0)
                load_res(c, 1)
                for t in range(T):
                    sp.wait_ge(tr_free, use_wo(n, t) + 1)
                    sp.dma_start(o_view[par, m, t], x_res[:, t % 2]).then_inc(x_stored[t % 2], 16)
                    if t + 2 < T:
                        load_res(c, t + 2)

            def body(c, first, last):
                if not last:
                    for t in range(T):
                        sp.wait_ge(tr_filled, use_xt(c[0], t) + 1)
                        if t >= 2:
                            sp.wait_ge(ln_loaded[t % 2], (after(*c)[0] * 2 + 1) * 16)
                        load_ln(after(*c), t)
                if first:
                    load_weights(range(KT + 2, 2 * KT))
                    sp.wait_ge(w_lo_done, 2 * KT)
                else:
                    residual(before(*c))

            chunks(sp, body)
            residual((NCH - 1, NCH // 2 - 1, 1))
            for parity in range(2):
                sp.wait_ge(x_stored[parity], 16 * NCH * T // 2)

        @block.gpsimd
        def _(pool):
            nc.gpsimd.memset(ident[:], 0.0).then_inc(consts_set, 1)
            pool.wait_ge(consts_set, 1)
            nc.gpsimd.affine_select(out=ident[:], in_=ident[:], compare_op=ALU.not_equal, fill=1.0,
                                    base=0, pattern=[[-1, P]], channel_multiplier=1).then_inc(consts_set, 1)
            nc.gpsimd.memset(minus_half[:], -0.5).then_inc(consts_set, 1)
            nc.gpsimd.memset(mask[:], 1.0).then_inc(consts_set, 1)
            nc.gpsimd.memset(k_hi[:].bitcast(F32), 0.0).then_inc(k_hi_zeroed, 1)
            pool.wait_ge(consts_set, 4)

            def inverse_std(n, t):
                q = n * T + t
                wait_apart(pool, mean_var_done, q + 1, spare)
                nc.gpsimd.tensor_scalar(var_eps[:, t:t + 1], mean_var[:, t, 1:2], EPS, None,
                                        ALU.add).then_inc(var_eps_done, 1)
                pool.wait_ge(var_eps_done, q + 1)
                nc.gpsimd.tensor_tensor(rstd[:, t:t + 1], var_eps[:, t:t + 1], minus_half[:],
                                        ALU.pow).then_inc(rstd_done, 1)

            def zero_v(b):
                for half in (v_hi, v_lo):
                    nc.gpsimd.memset(half[:, b].bitcast(F32), 0.0).then_inc(v_zeroed, 1)

            def weights_lo(lo, hi, js):
                for j in js:
                    pool.wait_ge(w_hi_done, j + 1)
                    nc.gpsimd.tensor_tensor(lo[:, j % KT], x_res[:, j % 2], hi[:, j % KT].bitcast(F32),
                                            ALU.subtract).then_inc(w_lo_done, 1)

            for t in range(T):
                inverse_std(0, t)
            weights_lo(wq_lo, wq_hi, range(2))
            nc.gpsimd.affine_select(out=mask[:], in_=mask[:], compare_op=ALU.is_ge, fill=0.0, base=0,
                                    pattern=[[P, NB], [-CTX, GH]], channel_multiplier=1).then_inc(consts_set, 1)
            pool.wait_ge(consts_set, 5)
            nc.gpsimd.affine_select(out=mask[:], in_=mask[:], compare_op=ALU.is_ge, fill=0.0, base=CTX - 1,
                                    pattern=[[-P, NB], [CTX, GH]], channel_multiplier=-1).then_inc(consts_set, 1)

            zero_v(0)
            weights_lo(wq_lo, wq_hi, range(2, KT))
            zero_v(1)

            def body(c, first, last):
                for g in range(NG):
                    for t in range(T):
                        s = c[0] * (NG * T) + (g * T + t)
                        tile = probs[:, g % 2, t].rearrange("p (h c) -> p h c", h=GH)
                        pool.wait_ge(inv_done, s + 1)
                        nc.gpsimd.tensor_tensor(tile, tile, inv_sum[:, t].unsqueeze(2).to_broadcast([P, GH, CTX]),
                                                ALU.mult).then_inc(probs_ready, 1)
                        if not last and g == 1:
                            inverse_std(after(*c)[0], t)
                    if first and g < 2:
                        weights_lo(wo_lo, wo_hi, range(KT + 2 * g, KT + 2 * g + 2))

            chunks(pool, body)

        @block.scalar
        def _(act):
            def x_hi(n, t):
                act.wait_ge(tr_filled, use_xt(n, t) + 1)
                nc.scalar.copy(xt_hi[:, :, t * P:(t + 1) * P],
                               psum_tr[:, tr_bank(use_xt, n, t)].rearrange(
                                   "p (k c) -> p k c", k=KT)).then_inc(xt_hi_done, 1)

            def group_hi(filled, count, out, in_, done):
                act.wait_ge(filled, count)
                nc.scalar.copy(out, in_).then_inc(done, 1)

            def weights_hi(hi, js):
                for j in js:
                    act.wait_ge(raw_loaded[j % 2], 16 * (j // 2 + 1))
                    nc.scalar.copy(hi[:, j % KT], x_res[:, j % 2]).then_inc(w_hi_done, 1)

            def values_hi(j):
                b, blk = j // NB, j % NB
                rows = slice(0, size[blk])
                act.wait_ge(v_filled, j + 1)
                for h in heads_of[blk]:
                    cols = slice(h * HD, (h + 1) * HD)
                    nc.scalar.activation(v_hi[rows, b, :, blk, cols], v_source(j)[rows, :, cols], ACT.Copy,
                                         scale=mask[rows, blk, h:h + 1]).then_inc(v_hi_done, 1)

            weights_hi(wq_hi, range(2))
            act.wait_ge(k_filled, NG)
            act.wait_ge(k_hi_zeroed, 1)
            for h in range(GH):
                rows = slice(h * HD, (h + 1) * HD)
                for b in range(BATCH):
                    nc.scalar.copy(k_hi[rows, b, :, h * CTX:(h + 1) * CTX],
                                   psum_s[rows, :, :, b * CTX:(b + 1) * CTX].rearrange("p a c n -> p (a c) n")
                                   ).then_inc(k_hi_done, 1)
                if h < 2:
                    x_hi(0, 2 * h)
                    x_hi(0, 2 * h + 1)
            act.wait_ge(consts_set, 6)
            act.wait_ge(v_zeroed, 1)
            for j in range(NB):
                values_hi(j)
                if j == 0:
                    weights_hi(wq_hi, range(2, KT))
            group_hi(q_filled, 1, q_hi[:, 0], psum_q[:], q_hi_done)
            act.wait_ge(v_zeroed, 3)

            def p_hi(c, g, b):
                G = c[0] * NG + (g - 1)
                if not (isinstance(G, int) and G == 0):
                    act.wait_ge(pv_done, G * NB + (b + 1 - NB))
                act.wait_ge(tr_filled, use_pt(c[0], g, b) + 1)
                nc.scalar.copy(pt_hi[0:size[b], b], psum_tr[0:size[b], tr_bank(use_pt, c[0], g, b)]).then_inc(pt_hi_done, 1)

            def exps(c, g, t):
                s = c[0] * (NG * T) + (g * T + t)
                act.wait_ge(bias_done, s + 1)
                for h in range(GH):
                    ins = nc.scalar.activation(probs[:, g % 2, t, h * CTX:(h + 1) * CTX],
                                               psum_s[:, t % 2, h // 2, (h % 2) * CTX:(h % 2 + 1) * CTX], ACT.Exp,
                                               bias=bias_max[:, t, h:h + 1], scale=SCALE,
                                               accum_out=weight_sum[:, t, h:h + 1])
                ins.then_inc(exp_done, 1)

            def q_first(c, g):
                group_hi(q_filled, c[0] * NG + (g + 2), q_hi[:, (g + 1) % 2], psum_q[:], q_hi_done)

            def o_first(c, g):
                group_hi(pv_done, (c[0] * NG + (g - 1)) * NB, o_hi[:, (g - 2) % NG], psum_o[:], o_hi_done)

            def body(c, first, last):
                for g in range(NG):
                    there = has_before(c, g)
                    if has_before(c, g - 1):
                        o_first(c, g)
                    exps(c, g, 0)
                    for t in range(T):
                        if there:
                            p_hi(c, g, t)
                        if g == NG - 1 and not last:
                            x_hi(after(*c)[0], t)
                        if t + 1 < T:
                            exps(c, g, t + 1)
                        if first and g == 0:
                            values_hi(NB + t)
                    if first and g == 0:
                        values_hi(2 * NB - 1)
                    if g < NG - 1:
                        q_first(c, g)
                    if first and g < 2:
                        weights_hi(wo_hi, range(KT + 2 * g, KT + 2 * g + 2))
                    if there:
                        p_hi(c, g, NB - 1)
                    if g == NG - 1 and not last:
                        q_first(c, g)

            chunks(act, body)
            end = (NCH, 0, 0)
            o_first(end, 0)
            for b in range(NB):
                p_hi(end, 0, b)
            o_first(end, 1)

        @block.vector
        def _(dve):
            def ln_stats(n, t):
                q = n * T + t
                if not (isinstance(n, int) and n == 0):
                    wait_apart(dve, rstd_done, n * T, spare)
                wait_apart(dve, ln_loaded[t % 2], (n * 2 + (t // 2 + 1)) * 16, spare)
                nc.vector.bn_stats(stats[:, t], x_ln[:, t]).then_inc(stats_done, 1)
                wait_apart(dve, stats_done, q + 1, spare)
                nc.vector.bn_aggr(mean_var[:, t], stats[:, t]).then_inc(mean_var_done, 1)

            def ln_apply(n, t):
                dve.wait_ge(rstd_done, n * T + (t + 1))
                nc.vector.tensor_scalar(x_ln[:, t], x_ln[:, t], mean_var[:, t, 0:1], rstd[:, t:t + 1],
                                        ALU.subtract, ALU.mult).then_inc(xn_ready, 1)

            def x_lo(n, t):
                cols = slice(t * P, (t + 1) * P)
                bank = tr_bank(use_xt, n, t)
                dve.wait_ge(xt_hi_done, n * T + (t + 1))
                nc.vector.tensor_tensor(xt_lo[:, :, cols], psum_tr[:, bank].rearrange("p (k c) -> p k c", k=KT),
                                        xt_hi[:, :, cols].bitcast(F32), ALU.subtract).then_inc(tr_free, 1)

            def group_lo(hi_done, G, out, in_, hi, done):
                dve.wait_ge(hi_done, G + 1)
                nc.vector.tensor_tensor(out, in_, hi.bitcast(F32), ALU.subtract).then_inc(done, 1)

            nc.vector.memset(k_lo[:].bitcast(F32), 0.0).then_inc(k_lo_zeroed, 1)
            for t in range(T):
                ln_stats(0, t)
            for t in range(T):
                ln_apply(0, t)
            dve.wait_ge(k_lo_zeroed, 1)
            for h in range(GH):
                rows = slice(h * HD, (h + 1) * HD)
                dve.wait_ge(k_hi_done, BATCH * (h + 1))
                for b in range(BATCH):
                    nc.vector.tensor_tensor(k_lo[rows, b, :, h * CTX:(h + 1) * CTX],
                                            psum_s[rows, :, :, b * CTX:(b + 1) * CTX].rearrange("p a c n -> p (a c) n"),
                                            k_hi[rows, b, :, h * CTX:(h + 1) * CTX].bitcast(F32),
                                            ALU.subtract).then_inc(k_lo_done, 1)
                if h < 2:
                    x_lo(0, 2 * h)
                    x_lo(0, 2 * h + 1)

            def values_lo(j):
                b, blk = j // NB, j % NB
                rows = slice(0, size[blk])
                dve.wait_ge(v_hi_done, v_pieces(j + 1))
                for h in heads_of[blk]:
                    cols = slice(h * HD, (h + 1) * HD)
                    nc.vector.scalar_tensor_tensor(out=v_lo[rows, b, :, blk, cols], in0=v_source(j)[rows, :, cols],
                                                   scalar=mask[rows, blk, h:h + 1],
                                                   in1=v_hi[rows, b, :, blk, cols].bitcast(F32),
                                                   op0=ALU.mult, op1=ALU.subtract).then_inc(v_lo_done, 1)

            dve.wait_ge(v_zeroed, 2)
            for j in range(NB):
                values_lo(j)
            group_lo(q_hi_done, 0, q_lo[:, 0], psum_q[:], q_hi[:, 0], q_lo_done)
            dve.wait_ge(v_zeroed, 4)

            def p_lo(c, g, b):
                G = c[0] * NG + (g - 1)
                dve.wait_ge(pt_hi_done, G * NB + (b + 1))
                nc.vector.tensor_tensor(pt_lo[0:size[b], b], psum_tr[0:size[b], tr_bank(use_pt, c[0], g, b)],
                                        pt_hi[0:size[b], b].bitcast(F32), ALU.subtract).then_inc(tr_free, 1)

            def maxima(c, g, t):
                s = c[0] * (NG * T) + (g * T + t)
                dve.wait_ge(s_filled, s + 1)
                nc.vector.tensor_reduce(minus_max[:, t],
                                        psum_s[:, t % 2, :, 0:2 * CTX].rearrange("p a (h c) -> p a h c", h=2),
                                        AX_X, ALU.max, negate=True).then_inc(max_done, 1)
                dve.wait_ge(max_done, s + 1)
                nc.vector.tensor_scalar(bias_max[:, t], minus_max[:, t], SCALE, None, ALU.mult).then_inc(bias_done, 1)

            def inverse(c, g, t):
                s = c[0] * (NG * T) + (g * T + t)
                if not (isinstance(s, int) and s < T):
                    dve.wait_ge(probs_ready, s + (1 - T))
                dve.wait_ge(exp_done, s + 1)
                nc.vector.reciprocal(inv_sum[:, t], weight_sum[:, t]).then_inc(inv_done, 1)

            def wo_rows(c, t):
                n = c[0]
                dve.wait_ge(res_loaded[t % 2], (n * 2 + (t // 2 + 1)) * 16)
                dve.wait_ge(tr_filled, use_wo(n, t) + 1)
                nc.vector.tensor_tensor(x_res[:, t % 2], psum_tr[:, tr_bank(use_wo, c[0], t)], x_res[:, t % 2],
                                        ALU.add).then_inc(tr_free, 1)

            def q_second(c, g):
                group_lo(q_hi_done, c[0] * NG + (g + 1), q_lo[:, (g + 1) % 2], psum_q[:], q_hi[:, (g + 1) % 2], q_lo_done)

            def o_second(c, g):
                gb = (g - 2) % NG
                group_lo(o_hi_done, c[0] * NG + (g - 2), o_lo[:, gb], psum_o[:], o_hi[:, gb], o_lo_done)

            def body(c, first, last):
                for g in range(NG):
                    there = has_before(c, g)
                    maxima(c, g, 0)
                    if has_before(c, g - 1):
                        o_second(c, g)
                    for t in range(T):
                        if t + 1 < T:
                            maxima(c, g, t + 1)
                        inverse(c, g, t)
                        if first and g == 0:
                            values_lo(NB + t)
                        if there:
                            p_lo(c, g, t)
                        if g == 1 and not first:
                            wo_rows(before(*c), t)
                        if not last:
                            if g == 1:
                                ln_stats(after(*c)[0], t)
                            if 4 * g + t in range(5, 9):
                                ln_apply(after(*c)[0], 4 * g + t - 5)
                            if g == NG - 1:
                                x_lo(after(*c)[0], t)
                    if first and g == 0:
                        values_lo(2 * NB - 1)
                    if g < NG - 1:
                        q_second(c, g)
                    if there:
                        p_lo(c, g, NB - 1)
                    if g == NG - 1 and not last:
                        q_second(c, g)

            chunks(dve, body)
            end = (NCH, NCH // 2, 0)
            o_second(end, 0)
            for b in range(NB):
                p_lo(end, 0, b)
            o_second(end, 1)
            for t in range(T):
                wo_rows(before(*end), t)

        @block.tensor
        def _(pe):
            def claim_tr(use):
                if not (isinstance(use, int) and use < 2):
                    pe.wait_ge(tr_free, use - 1)

            def x_transposes(n, t):
                bank = tr_bank(use_xt, n, t)
                pe.wait_ge(xn_ready, n * T + (t + 1))
                claim_tr(use_xt(n, t))
                for k in range(KT):
                    mm = nc.tensor.transpose(psum_tr[:, bank, k * P:(k + 1) * P], x_ln[:, t, k * P:(k + 1) * P], ident[:])
                mm.then_inc(tr_filled, 1)

            def q_part(G, g, k):
                mm = split_matmul(nc, psum_q[:], (wq_hi[:, k, g * P:(g + 1) * P], wq_lo[:, k, g * P:(g + 1) * P]),
                                  (xt_hi[:, k], xt_lo[:, k]), k == 0, k == KT - 1)
                if k == KT - 1:
                    mm.then_inc(q_filled, 1)

            pe.wait_ge(ctx_loaded, 32)
            for g in range(NG):
                for k in range(KC):
                    mm = nc.tensor.matmul(psum_s[:, g // 2, g % 2, 0:BATCH * CTX], wk_sb[:, k, g * P:(g + 1) * P],
                                          ctx_sb[:, k], start=(k == 0), stop=(k == KC - 1))
                mm.then_inc(k_filled, 1)
            pe.wait_ge(consts_set, 2)
            for t in range(T):
                x_transposes(0, t)

            def v_block(j):
                b, blk = j // NB, j % NB
                if j % NB == 0:
                    pe.wait_ge(rep_loaded[b], 16 * (GH + 1 - b))
                if 2 <= j < NB:
                    pe.wait_ge(v_lo_done, v_pieces(j - 1))
                elif j >= NB + 2:
                    pe.wait_ge(v_lo_done, v_pieces(j - 2))
                for k in range(KC):
                    mm = nc.tensor.matmul(v_bank(j)[0:size[blk]],
                                          ctx_rep[b][:, k, blk * P:blk * P + size[blk]], wv_sb[:, k],
                                          start=(k == 0), stop=(k == KC - 1))
                mm.then_inc(v_filled, 1)

            for j in range(NB):
                v_block(j)
            pe.wait_ge(tr_free, T)
            pe.wait_ge(v_lo_done, v_pieces(NB - 1))
            for k in range(KT):
                pe.wait_ge(w_lo_done, k + 1)
                q_part(0, 0, k)
            pe.wait_ge(k_lo_done, BATCH * GH)

            def scores(c, g, t):
                n, m, par = c
                s = n * (NG * T) + (g * T + t)
                if t == 0:
                    pe.wait_ge(q_lo_done, n * NG + (g + 1))
                if not (isinstance(s, int) and s < 2):
                    pe.wait_ge(exp_done, s - 1)
                rows = slice(t * P, (t + 1) * P)
                for pair in range(2):
                    keys = slice(pair * 2 * CTX, (pair + 1) * 2 * CTX)
                    mm = split_matmul(nc, psum_s[:, t % 2, pair, 0:2 * CTX],
                                      (q_hi[:, g % 2, rows], q_lo[:, g % 2, rows]),
                                      (k_hi[:, par, g, keys], k_lo[:, par, g, keys]), True, True)
                mm.then_inc(s_filled, 1)

            def p_transposes(c, g, b):
                if b == 0:
                    pe.wait_ge(probs_ready, c[0] * (NG * T) + g * T)
                claim_tr(use_pt(c[0], g, b))
                cols = slice(b * P, b * P + size[b])
                for t in range(T):
                    mm = nc.tensor.transpose(psum_tr[0:size[b], tr_bank(use_pt, c[0], g, b), t * P:(t + 1) * P],
                                             probs[:, (g - 1) % 2, t, cols], ident[:])
                mm.then_inc(tr_filled, 1)

            def values(c, g, b):
                G = c[0] * NG + (g - 1)
                gb = (g - 1) % NG
                par = c[2] if g else 1 - c[2]
                if b == 0 and not (isinstance(G, int) and G == 0):
                    pe.wait_ge(o_lo_done, G)
                pe.wait_ge(tr_free, use_pt(c[0], g, b) + 1)
                rows = slice(0, size[b])
                mm = split_matmul(nc, psum_o[:], (v_hi[rows, par, gb, b], v_lo[rows, par, gb, b]),
                                  (pt_hi[rows, b], pt_lo[rows, b]), b == 0, b == NB - 1)
                mm.then_inc(pv_done, 1)

            def wo_product(c, t):
                if t == 0:
                    pe.wait_ge(w_lo_done, 2 * KT)
                    pe.wait_ge(o_lo_done, c[0] * NG + NG)
                claim_tr(use_wo(c[0], t))
                rows = slice(t * P, (t + 1) * P)
                for g in range(NG):
                    mm = split_matmul(nc, psum_tr[:, tr_bank(use_wo, c[0], t)], (o_hi[:, g, rows], o_lo[:, g, rows]),
                                      (wo_hi[:, g], wo_lo[:, g]), g == 0, g == NG - 1)
                mm.then_inc(tr_filled, 1)

            def body(c, first, last):
                n = c[0]
                for g in range(NG):
                    there = has_before(c, g)
                    scores(c, g, 0)
                    if g and has_before(c, g - 1):
                        values(c, g - 1, NB - 1)
                    for t in range(T):
                        if t + 1 < T:
                            scores(c, g, t + 1)
                        if there:
                            p_transposes(c, g, t)
                        if g == 1 and not first:
                            wo_product(before(*c), t)
                        if g == NG - 1 and not last:
                            x_transposes(after(*c)[0], t)
                        if g < NG - 1:
                            for k in ((0, 1), (2,), (), (3,))[t]:
                                q_part(n * NG + (g + 1), g + 1, k)
                        if first and g == 0:
                            v_block(NB + t)
                        if there and t:
                            values(c, g, t - 1)
                        if t == T - 1 and there:
                            p_transposes(c, g, NB - 1)
                    if first and g == 0:
                        v_block(2 * NB - 1)
                        pe.wait_ge(v_lo_done, 2 * PIECES)
                    if g == NG - 1 and not last:
                        pe.wait_ge(tr_free, use_xt(after(*c)[0], T - 1) + 1)
                        for k in range(KT):
                            q_part(n * NG + NG, 0, k)
                    if there:
                        values(c, g, NB - 2)
                        if g == NG - 1:
                            values(c, g, NB - 1)

            chunks(pe, body)
            end = (NCH, NCH // 2, 0)
            for b in range(NB - 1):
                p_transposes(end, 0, b)
                if b:
                    values(end, 0, b - 1)
            p_transposes(end, 0, NB - 1)
            values(end, 0, NB - 2)
            values(end, 0, NB - 1)
            for t in range(T):
                wo_product(before(*end), t)


def spiking_ffn(nc, x_in, x_out, w_fc, w_proj):
    XT_STEP = 11
    thresholds = spike_thresholds()
    with ExitStack() as ctx:
        def sb(name, shape, dt=F32):
            return ctx.enter_context(nc.sbuf_tensor(name, shape, dt))

        def sem(name):
            return ctx.enter_context(nc.semaphore("b_" + name))

        wfc_hi = sb("wfc_hi", [P, NF, KT, P], F32R)
        wfc_lo = sb("wfc_lo", [P, NF, KT, P], F32R)
        wpr_hi = sb("wpr_hi", [P, NF, D], F32R)
        wpr_lo = sb("wpr_lo", [P, NF, D], F32R)
        xt_hi = sb("xt_hi", [P, 2, KT, CH], F32R)
        xt_lo = sb("xt_lo", [P, 2, KT, CH], F32R)
        x_rows = sb("x_rows", [P, 2, T, D])
        xn = sb("xn", [P, 2, D])
        relu = sb("relu", [P, 2, CH])
        h_hi = sb("h_hi", [P, 2, CH], F32R)
        h_lo = sb("h_lo", [P, 2, CH], F32R)
        y = sb("y", [P, T, D])
        count = sb("count", [P, 2, D])
        stats = sb("stats", [P, T, 6])
        moments = sb("moments", [P, 5, T])
        mean = sb("mean", [P, T])
        var_eps = sb("var_eps", [P, T])
        rstd = sb("rstd", [P, T])
        minus_half = sb("minus_half", [P, T])
        ident = sb("ident_b", [P, P])
        raw = y

        psum_fc = ctx.enter_context(nc.psum_tensor("psum_fc", [P, 2, CH], F32))
        psum_y = ctx.enter_context(nc.psum_tensor("psum_y", [P, T, D], F32))
        psum_xt = ctx.enter_context(nc.psum_tensor("psum_xt", [P, 2, KT * P], F32))

        ident_ready = sem("ident_ready")
        raw_loaded = [sem(f"raw_loaded{i}") for i in range(4)]
        w_hi_done, w_lo_done = sem("w_hi_done"), sem("w_lo_done")
        x_loaded, x_stored = sem("x_loaded"), sem("x_stored")
        stat_step = sem("stat_step")
        rstd_done = sem("rstd_done")
        var_ready = sem("var_ready")
        xn_ready = sem("xn_ready")
        xt_filled = sem("xt_filled")
        xt_hi_done, xt_lo_done = sem("xt_hi_done"), sem("xt_lo_done")
        fc_done = sem("fc_done")
        relu_done, sq_done = sem("relu_done"), sem("sq_done")
        h_hi_done, h_lo_done = sem("h_hi_done"), sem("h_lo_done")
        proj_done = sem("proj_done")
        y_copied = sem("y_copied")
        lif_step = sem("lif_step")
        out_ready = sem("out_ready")

        x_view = x_in.rearrange("(n t p) d -> n p t d", p=P, t=T)
        o_view = x_out.rearrange("(n t p) d -> n p t d", p=P, t=T)
        W_TILES = 2 * NF

        def w_tile(j):
            f = j // 2
            if j % 2 == 0:
                flat = lambda w: w[:, f, :, :].rearrange("p k n -> p (k n)")
                return w_fc[:, f, :], flat(wfc_hi), flat(wfc_lo)
            return w_proj[:, f, :], wpr_hi[:, f, :], wpr_lo[:, f, :]

        def chunks(engine, body):
            body(0, 0, True, False)
            with engine.Fori(1, NCH // 2) as i:
                for u in range(2):
                    body(i * 2 + (u - 1), (u + 1) % 2, False, False)
            body(NCH - 1, 1, False, True)

        block = ctx.enter_context(nc.Block())

        @block.sync
        def _(sp):
            sp.dma_start(x_rows[:, 0], x_view[0]).then_inc(x_loaded, 16)
            for j in range(W_TILES):
                if j == T:
                    sp.wait_ge(x_loaded, 16)
                    sp.dma_start(x_rows[:, 1], x_view[1]).then_inc(x_loaded, 16)
                if j >= T:
                    sp.wait_ge(w_lo_done, j - T + 1)
                sp.dma_start(raw[:, j % T, :], w_tile(j)[0]).then_inc(raw_loaded[j % T], 16)

            def body(n, par, first, last):
                if not first and not last:
                    sp.wait_ge(x_stored, 16 * T * n)
                    sp.dma_start(x_rows[:, 1 - par], x_view[n + 1]).then_inc(x_loaded, 16)
                for t in range(T):
                    sp.wait_ge(out_ready, T * n + t + 1)
                    sp.dma_start(o_view[n, :, t], x_rows[:, par, t]).then_inc(x_stored, 16)

            chunks(sp, body)
            sp.wait_ge(x_stored, 16 * T * NCH)

        @block.gpsimd
        def _(pool):
            nc.gpsimd.memset(ident[:], 0.0).then_inc(ident_ready, 1)
            pool.wait_ge(ident_ready, 1)
            nc.gpsimd.affine_select(out=ident[:], in_=ident[:], compare_op=ALU.not_equal, fill=1.0,
                                    base=0, pattern=[[-1, P]], channel_multiplier=1).then_inc(ident_ready, 1)
            nc.gpsimd.memset(minus_half[:], -0.5).then_inc(ident_ready, 1)
            pool.wait_ge(ident_ready, 3)

            def inverse_std(n):
                pool.wait_ge(var_ready, n + 1)
                nc.gpsimd.tensor_tensor(rstd[:], var_eps[:], minus_half[:], ALU.pow).then_inc(rstd_done, 1)

            def weights_lo(f):
                for j in (2 * f, 2 * f + 1):
                    pool.wait_ge(w_hi_done, j + 1)
                    _, hi, lo = w_tile(j)
                    nc.gpsimd.tensor_tensor(lo, raw[:, j % T, :], hi.bitcast(F32), ALU.subtract).then_inc(w_lo_done, 1)

            inverse_std(0)
            for f in range(2):
                weights_lo(f)

            def body(n, par, first, last):
                for f in range(NF):
                    if first and f + 2 < NF:
                        weights_lo(f + 2)
                    if f == 9 and not last:
                        inverse_std(n + 1)
                    pool.wait_ge(h_hi_done, NF * n + f + 1)
                    nc.gpsimd.tensor_tensor(h_lo[:, f % 2], relu[:, f % 2], h_hi[:, f % 2].bitcast(F32),
                                            ALU.subtract).then_inc(h_lo_done, 1)

            chunks(pool, body)

        @block.scalar
        def _(act):
            def x_hi(n, par, t):
                act.wait_ge(xt_filled, T * n + t + 1)
                nc.scalar.copy(xt_hi[:, par, :, t * P:(t + 1) * P],
                               psum_xt[:, t % 2].rearrange("p (k c) -> p k c", k=KT)).then_inc(xt_hi_done, 1)

            def weights_hi(f):
                for j in (2 * f, 2 * f + 1):
                    act.wait_ge(raw_loaded[j % T], 16 * (j // T + 1))
                    nc.scalar.copy(w_tile(j)[1], raw[:, j % T, :]).then_inc(w_hi_done, 1)

            for f in range(2):
                weights_hi(f)
            for t in range(T):
                x_hi(0, 0, t)

            def h_first(n, f):
                act.wait_ge(fc_done, NF * n + f + 1)
                if not (isinstance(n, int) and NF * n + f < 2):
                    act.wait_ge(h_lo_done, NF * n + f - 1)
                nc.scalar.activation(relu[:, f % 2], psum_fc[:, f % 2], ACT.Relu).then_inc(relu_done, 1)

            def h_second(n, f):
                act.wait_ge(sq_done, NF * n + f + 1)
                if not (isinstance(n, int) and NF * n + f < 2):
                    act.wait_ge(proj_done, NF * n + f - 1)
                nc.scalar.copy(h_hi[:, f % 2], relu[:, f % 2]).then_inc(h_hi_done, 1)

            def copy_y(n):
                act.wait_ge(proj_done, NF * (n + 1))
                for t in range(T):
                    nc.scalar.copy(y[:, t], psum_y[:, t]).then_inc(y_copied, 1)

            def body(n, par, first, last):
                for f in range(NF):
                    if first and f + 2 < NF:
                        weights_hi(f + 2)
                    h_first(n, f)
                    h_second(n, f)
                    if not last and XT_STEP <= f < XT_STEP + T:
                        x_hi(n + 1, 1 - par, f - XT_STEP)
                    if f == 0 and not first:
                        copy_y(n - 1)
                if first:
                    act.wait_ge(w_lo_done, W_TILES)
                else:
                    act.wait_ge(out_ready, T * n)
                if last:
                    copy_y(n)

            chunks(act, body)

        @block.vector
        def _(dve):
            def ln_stats(n, par, t):
                if t == 0:
                    dve.wait_ge(x_loaded, 16 * (n + 1))
                nc.vector.bn_stats(stats[:, t], x_rows[:, par, t]).then_inc(stat_step, 1)

            def ln_variance(n):
                mean_e, m2_e, mean_o, m2_o = (stats[:, :, c] for c in (1, 2, 4, 5))
                done = T * n + T + 6 * n
                dve.wait_ge(stat_step, done)
                nc.vector.tensor_tensor(moments[:, 0], mean_e, mean_o, ALU.add).then_inc(stat_step, 1)
                nc.vector.tensor_tensor(moments[:, 1], mean_e, mean_o, ALU.subtract).then_inc(stat_step, 1)
                nc.vector.tensor_tensor(moments[:, 2], m2_e, m2_o, ALU.add).then_inc(stat_step, 1)
                dve.wait_ge(stat_step, done + 2)
                nc.vector.scalar_tensor_tensor(out=moments[:, 3], in0=moments[:, 1], scalar=D / 4.0,
                                               in1=moments[:, 1], op0=ALU.mult, op1=ALU.mult).then_inc(stat_step, 1)
                nc.vector.tensor_scalar(mean[:], moments[:, 0], 0.5, None, ALU.mult).then_inc(stat_step, 1)
                dve.wait_ge(stat_step, done + 4)
                nc.vector.tensor_tensor(moments[:, 4], moments[:, 3], moments[:, 2], ALU.add).then_inc(stat_step, 1)
                dve.wait_ge(stat_step, done + 6)
                nc.vector.tensor_scalar(var_eps[:], moments[:, 4], 1.0 / D, EPS, ALU.mult, ALU.add).then_inc(var_ready, 1)

            def ln_apply(n, par, t):
                if t == 0:
                    dve.wait_ge(rstd_done, n + 1)
                if not (isinstance(n, int) and T * n + t < 2):
                    dve.wait_ge(xt_filled, T * n + t - 1)
                nc.vector.tensor_scalar(xn[:, t % 2], x_rows[:, par, t], mean[:, t:t + 1],
                                        rstd[:, t:t + 1], ALU.subtract, ALU.mult).then_inc(xn_ready, 1)

            def x_lo(n, par, t):
                dve.wait_ge(xt_hi_done, T * n + t + 1)
                cols = slice(t * P, (t + 1) * P)
                nc.vector.tensor_tensor(xt_lo[:, par, :, cols],
                                        psum_xt[:, t % 2].rearrange("p (k c) -> p k c", k=KT),
                                        xt_hi[:, par, :, cols].bitcast(F32), ALU.subtract).then_inc(xt_lo_done, 1)

            def square(n, f):
                dve.wait_ge(relu_done, NF * n + f + 1)
                nc.vector.scalar_tensor_tensor(out=relu[:, f % 2], in0=psum_fc[:, f % 2], scalar=0.0,
                                               in1=relu[:, f % 2], op0=ALU.max, op1=ALU.mult).then_inc(sq_done, 1)

            def neuron(n, par, t, s):
                c = count[:, t % 2]
                pair, j = LIF_STEPS * (T * n + t - t % 2), t % 2
                if s == 0:
                    if t >= 2:
                        dve.wait_ge(out_ready, T * n + t - 1)
                    dve.wait_ge(y_copied, T * n + t + 1)
                    nc.vector.tensor_scalar(c, y[:, t], thresholds[0], None, ALU.is_gt).then_inc(lif_step, 1)
                elif s < LIF_STEPS:
                    dve.wait_ge(lif_step, pair + 2 * s - 1 + j)
                    nc.vector.scalar_tensor_tensor(out=c, in0=y[:, t], scalar=thresholds[s], in1=c,
                                                   op0=ALU.is_gt, op1=ALU.add).then_inc(lif_step, 1)
                else:
                    dve.wait_ge(lif_step, pair + 2 * LIF_STEPS - 1 + j)
                    nc.vector.scalar_tensor_tensor(out=x_rows[:, par, t], in0=c, scalar=1.0 / LIF_STEPS,
                                                   in1=x_rows[:, par, t], op0=ALU.mult, op1=ALU.add).then_inc(out_ready, 1)

            def neurons(n, par, part):
                for s in range(2 * (part % 3), 2 * (part % 3) + 2):
                    for t in (2 * (part // 3), 2 * (part // 3) + 1):
                        neuron(n, par, t, s)

            def whole_ln(n, par):
                for t in range(T):
                    ln_stats(n, par, t)
                ln_variance(n)
                for t in range(T):
                    ln_apply(n, par, t)
                    if t >= 1:
                        x_lo(n, par, t - 1)
                x_lo(n, par, T - 1)

            dve.wait_ge(ident_ready, 3)
            whole_ln(0, 0)

            def body(n, par, first, last):
                for f in range(NF):
                    square(n, f)
                    if not first and 1 <= f <= 6:
                        neurons(n - 1, 1 - par, f - 1)
                    if last:
                        continue
                    if f == 8:
                        for t in range(T):
                            ln_stats(n + 1, 1 - par, t)
                        ln_variance(n + 1)
                    if XT_STEP - 2 <= f < XT_STEP + T - 2:
                        ln_apply(n + 1, 1 - par, f - XT_STEP + 2)
                    if XT_STEP <= f < XT_STEP + T:
                        x_lo(n + 1, 1 - par, f - XT_STEP)
                if last:
                    for part in range(6):
                        neurons(n, par, part)

            chunks(dve, body)

        @block.tensor
        def _(pe):
            def transposes(n, t):
                pe.wait_ge(xn_ready, T * n + t + 1)
                if not (isinstance(n, int) and T * n + t < 2):
                    pe.wait_ge(xt_lo_done, T * n + t - 1)
                for k in range(KT):
                    mm = nc.tensor.transpose(psum_xt[:, t % 2, k * P:(k + 1) * P], xn[:, t % 2, k * P:(k + 1) * P], ident[:])
                mm.then_inc(xt_filled, 1)

            def hidden(n, par, f):
                if not (isinstance(n, int) and NF * n + f < 2):
                    pe.wait_ge(sq_done, NF * n + f - 1)
                for k in range(KT):
                    mm = split_matmul(nc, psum_fc[:, f % 2], (wfc_hi[:, f, k], wfc_lo[:, f, k]),
                                      (xt_hi[:, par, k], xt_lo[:, par, k]), k == 0, k == KT - 1)
                mm.then_inc(fc_done, 1)

            def project(n, f):
                pe.wait_ge(h_lo_done, NF * n + f + 1)
                for t in range(T):
                    cols = slice(t * P, (t + 1) * P)
                    mm = split_matmul(nc, psum_y[:, t], (h_hi[:, f % 2, cols], h_lo[:, f % 2, cols]),
                                      (wpr_hi[:, f], wpr_lo[:, f]), f == 0, f == NF - 1)
                mm.then_inc(proj_done, 1)

            pe.wait_ge(ident_ready, 3)
            for t in range(T):
                transposes(0, t)

            pe.wait_ge(xt_lo_done, T)
            pe.wait_ge(w_lo_done, 2)
            hidden(0, 0, 0)

            def body(n, par, first, last):
                for f in range(NF):
                    if not last and XT_STEP <= f < XT_STEP + T:
                        transposes(n + 1, f - XT_STEP)
                    if f + 1 < NF:
                        if first:
                            pe.wait_ge(w_lo_done, 2 * (f + 2))
                        hidden(n, par, f + 1)
                    elif not last:
                        pe.wait_ge(xt_lo_done, T * (n + 2))
                        hidden(n + 1, 1 - par, 0)
                    if f == 0 and not first:
                        pe.wait_ge(y_copied, T * n)
                    project(n, f)

            chunks(pe, body)



def single_head_attention_and_linear(nc, x_in, x_out, ctx_t, wq_t, bq, wk, bk, wv, bv, cb_t, scb, bias):
    KC = CTXD // P
    HK = CTX // 2
    NT = ROWS // P
    LAST_LAG = 6
    with ExitStack() as ctx:
        def sb(name, shape, dt=F32):
            return ctx.enter_context(nc.sbuf_tensor(name, shape, dt))

        def bank(name, shape):
            return ctx.enter_context(nc.psum_tensor(name, shape, F32))

        def sem(name):
            return ctx.enter_context(nc.semaphore("c_" + name))

        x_all = sb("x_all", [P, NT, D])
        ctx_sb = sb("ctx_sb", [P, KC, BATCH * CTX])
        wk_sb, wv_sb = sb("wk_sb", [P, KC, D]), sb("wv_sb", [P, KC, D])
        wq_sb = sb("wq_sb", [P, KT, D])
        bq_sb, bk_sb = sb("bq_sb", [P, KT]), sb("bk_sb", [P, KT])
        bv_rows, bias_rows, scb_rows = sb("bv_rows", [P, D]), sb("bias_rows", [P, D]), sb("scb_rows", [P, D])
        k_t = sb("k_t", [P, KT, BATCH * CTX])
        m_hi, m_lo = sb("m_hi", [P, KT, BATCH * CTX], F32R), sb("m_lo", [P, KT, BATCH * CTX], F32R)
        bqk = sb("bqk", [P, BATCH * CTX])
        bqk_hi, bqk_lo = sb("bqk_hi", [P, BATCH * CTX], F32R), sb("bqk_lo", [P, BATCH * CTX], F32R)
        v_rows = sb("v_rows", [HK, 2, D])
        v_hi, v_lo = sb("v_hi", [HK, BATCH, 2, D], F32R), sb("v_lo", [HK, BATCH, 2, D], F32R)
        cb_raw = sb("cb_raw", [P, KT, D])
        cb_hi, cb_lo = sb("cb_hi", [P, KT, D], F32R), sb("cb_lo", [P, KT, D], F32R)
        ident, ones, ones_r = sb("ident_c", [P, P]), sb("ones_c", [P, P]), sb("ones_r", [P, P], F32R)
        minus_half = sb("minus_half_c", [P, 1])

        stats = [sb(f"stats{a}", [P, 2, 6]) for a in (1, 2)]
        mean_var = [sb(f"mean_var{a}", [P, 2, 2]) for a in (1, 2)]
        var_eps = [sb(f"var_eps{a}", [P, 2]) for a in (1, 2)]
        rstd = [sb(f"rstd{a}", [P, 2]) for a in (1, 2)]
        xn = [sb(f"xn{a}", [P, 2, D]) for a in (1, 2)]
        xt_hi = [sb(f"xt_hi{a}", [P, 2, KT, P], F32R) for a in (1, 2)]
        xt_lo = [sb(f"xt_lo{a}", [P, 2, KT, P], F32R) for a in (1, 2)]
        minus_max, weight_sum, inv_sum = sb("minus_max", [P, 2]), sb("weight_sum", [P, 2]), sb("inv_sum", [P, 2])
        probs = sb("probs", [P, 2, CTX])
        pt_hi, pt_lo = sb("pt_hi", [HK, 2, 2, P], F32R), sb("pt_lo", [HK, 2, 2, P], F32R)
        scaled = sb("scaled", [P, 2, D])

        psum_xt = [bank(f"psum_xt{a}", [P, KT, P]) for a in (1, 2)]
        psum_s, psum_pt = bank("psum_s", [P, CTX]), bank("psum_pt", [HK, 2, P])
        psum_o, psum_f = bank("psum_o", [P, D]), bank("psum_f", [P, D])
        psum_prep = bank("psum_prep", [P, 2, D])

        k_loaded, wq_loaded, v_loaded = sem("k_loaded"), sem("wq_loaded"), sem("v_loaded")
        cb_loaded, rows_loaded = sem("cb_loaded"), sem("rows_loaded")
        consts_set, ones_ready = sem("consts_set"), sem("ones_ready")
        prep_filled, prep_read = sem("prep_filled"), sem("prep_read")
        bqk_step, scb_ready = sem("bqk_step"), sem("scb_ready")
        m_hi_done, v_biased = sem("m_hi_done"), sem("v_biased")
        v_hi_done, v_lo_done = sem("v_hi_done"), sem("v_lo_done")
        cb_hi_done, cb_lo_done = sem("cb_hi_done"), sem("cb_lo_done")
        x_loaded, x_stored = sem("x_loaded"), sem("x_stored")
        stats_done = [sem(f"stats_done{a}") for a in (1, 2)]
        mean_var_done = [sem(f"mean_var_done{a}") for a in (1, 2)]
        var_eps_done = [sem(f"var_eps_done{a}") for a in (1, 2)]
        rstd_done = [sem(f"rstd_done{a}") for a in (1, 2)]
        xn_ready = [sem(f"xn_ready{a}") for a in (1, 2)]
        xt_filled = [sem(f"xt_filled{a}") for a in (1, 2)]
        xt_hi_done = [sem(f"xt_hi_done{a}") for a in (1, 2)]
        xt_lo_done = [sem(f"xt_lo_done{a}") for a in (1, 2)]
        s_filled, max_done, exp_done = sem("s_filled"), sem("max_done"), sem("exp_done")
        pt_filled, pt_hi_done, pt_lo_done = sem("pt_filled"), sem("pt_hi_done"), sem("pt_lo_done")
        inv_done, o_filled, x_mid = sem("inv_done"), sem("o_filled"), sem("x_mid")
        f_filled, scaled_done, biased, out_ready = sem("f_filled"), sem("scaled_done"), sem("biased"), sem("out_ready")
        spare = sem("spare")

        x_view = x_in.rearrange("(b i s p) d -> b i p s d", b=BATCH, s=2, p=P)
        o_view = x_out.rearrange("(b i s p) d -> b i p s d", b=BATCH, s=2, p=P)
        slots = x_all[:].rearrange("p (m b) d -> p m b d", b=BATCH)

        def steps(engine, step):
            begin, end = 7, NT - 1
            known = lambda q: isinstance(q, int)
            for g in range(-1, begin):
                step(g, g % 4, lambda q: 0 <= q < NT)
            with engine.Fori(0, (end - begin) // 4) as i:
                for u in range(4):
                    step(i * 4 + (begin + u), (begin + u) % 4, lambda q: True)
            for g in range(end, NT + LAST_LAG):
                step(g, g % 4, lambda q: 0 <= q < NT)

        def v_groups(g):
            return {0: (0, 1), 1: (2,), 2: (3,)}.get(g, ()) if isinstance(g, int) else ()

        def free(engine, sem, q, ring):
            if isinstance(q, int):
                if q - ring >= 0:
                    engine.wait_ge(sem, q - ring + 1)
            else:
                engine.wait_ge(sem, q + (1 - ring))

        block = ctx.enter_context(nc.Block())

        @block.sync
        def _(sp):
            def load(m):
                for b in range(BATCH):
                    sp.dma_start(slots[:, 2 * m:2 * m + 2, b], x_view[b, m]).then_inc(x_loaded, 16)

            for dst, src in ((ctx_sb, ctx_t), (wk_sb, wk), (bk_sb, bk), (bq_sb, bq)):
                sp.dma_start(dst[:], src).then_inc(k_loaded, 16)
            sp.dma_start(wq_sb[:], wq_t).then_inc(wq_loaded, 16)
            load(0)
            sp.dma_start(wv_sb[:], wv).then_inc(v_loaded, 16)
            sp.dma_start(bv_rows[:], bv.broadcast_to([P, D])).then_inc(v_loaded, 16)
            sp.dma_start(cb_raw[:], cb_t).then_inc(cb_loaded, 16)
            for dst, src in ((bias_rows, bias), (scb_rows, scb)):
                sp.dma_start(dst[:], src.broadcast_to([P, D])).then_inc(rows_loaded, 16)
            for m in range(1, NT // 4):
                sp.wait_ge(x_loaded, 32 * m)
                load(m)
            with sp.Fori(0, NT // 4) as m:
                sp.wait_ge(out_ready, m * 4 + 4)
                for b in range(BATCH):
                    sp.dma_start(o_view[b, m], slots[:, bass.ds(m * 2, 2), b]).then_inc(x_stored, 16)
            sp.wait_ge(x_stored, 32 * (NT // 4))

        @block.gpsimd
        def _(pool):
            nc.gpsimd.memset(ident[:], 0.0).then_inc(consts_set, 1)
            pool.wait_ge(consts_set, 1)
            nc.gpsimd.affine_select(out=ident[:], in_=ident[:], compare_op=ALU.not_equal, fill=1.0,
                                    base=0, pattern=[[-1, P]], channel_multiplier=1).then_inc(consts_set, 1)
            nc.gpsimd.memset(minus_half[:], -0.5).then_inc(consts_set, 1)
            nc.gpsimd.memset(ones[:], 1.0).then_inc(consts_set, 1)
            pool.wait_ge(consts_set, 4)

            def inverse_std(a, q, par):
                wait_apart(pool, mean_var_done[a], q + 1, spare)
                nc.gpsimd.tensor_scalar(var_eps[a][:, par:par + 1], mean_var[a][:, par, 1:2], EPS, None,
                                        ALU.add).then_inc(var_eps_done[a], 1)
                pool.wait_ge(var_eps_done[a], q + 1)
                nc.gpsimd.tensor_tensor(rstd[a][:, par:par + 1], var_eps[a][:, par:par + 1], minus_half[:],
                                        ALU.pow).then_inc(rstd_done[a], 1)

            def step(g, r, has):
                if has(g + 1):
                    inverse_std(0, g + 1, (r + 1) % 2)
                if isinstance(g, int) and 1 <= g <= KT:
                    pool.wait_ge(cb_hi_done, g)
                    nc.gpsimd.tensor_tensor(cb_lo[:, g - 1], cb_raw[:, g - 1], cb_hi[:, g - 1].bitcast(F32),
                                            ALU.subtract).then_inc(cb_lo_done, 1)
                if isinstance(g, int) and g == KT + 1:
                    pool.wait_ge(rows_loaded, 32)
                if has(g - 5):
                    wait_apart(pool, xn_ready[1], g - 4, spare)
                    nc.gpsimd.tensor_tensor(x_all[:, g - 5], x_all[:, g - 5], bias_rows[:], ALU.add).then_inc(biased, 1)
                if has(g - 3):
                    inverse_std(1, g - 3, (r + 1) % 2)
                if has(g - 6):
                    pool.wait_ge(biased, g - 5)
                    wait_apart(pool, scaled_done, g - 5, spare)
                    nc.gpsimd.tensor_tensor(x_all[:, g - 6], scaled[:, r % 2], x_all[:, g - 6], ALU.add).then_inc(out_ready, 1)

            steps(pool, step)

        @block.scalar
        def _(act):
            for k in range(KT):
                act.wait_ge(prep_filled, KT + k + 1)
                nc.scalar.copy(m_hi[:, k], psum_prep[:, k % 2, 0:BATCH * CTX]).then_inc(m_hi_done, 1)

            def copy_hi(filled, q, out, in_, done):
                act.wait_ge(filled, q + 1)
                nc.scalar.copy(out, in_).then_inc(done, 1)

            def step(g, r, has):
                if has(g):
                    free(act, s_filled, g, 2)
                    copy_hi(xt_filled[0], g, xt_hi[0][:, r % 2], psum_xt[0][:], xt_hi_done[0])
                for j in v_groups(g):
                    act.wait_ge(v_biased, j + 1)
                    nc.scalar.copy(v_hi[:, j // 2, j % 2], v_rows[:, j % 2]).then_inc(v_hi_done, 1)
                if isinstance(g, int) and 1 <= g <= KT:
                    act.wait_ge(cb_loaded, 16)
                    nc.scalar.copy(cb_hi[:, g - 1], cb_raw[:, g - 1]).then_inc(cb_hi_done, 1)
                if has(g - 2):
                    free(act, o_filled, g - 2, 2)
                    copy_hi(pt_filled, g - 2, pt_hi[:, r % 2], psum_pt[:], pt_hi_done)
                if has(g - 1):
                    par = (r + 1) % 2
                    free(act, pt_filled, g - 1, 2)
                    free(act, inv_done, g - 1, 2)
                    act.wait_ge(max_done, g)
                    nc.scalar.activation(probs[:, par], psum_s[:], ACT.Exp, bias=minus_max[:, par:par + 1],
                                         accum_out=weight_sum[:, par:par + 1]).then_inc(exp_done, 1)
                if has(g - 5):
                    free(act, f_filled, g - 5, 2)
                    copy_hi(xt_filled[1], g - 5, xt_hi[1][:, (r + 1) % 2], psum_xt[1][:], xt_hi_done[1])

            steps(act, step)

        @block.vector
        def _(dve):
            dve.wait_ge(consts_set, 4)
            nc.vector.tensor_copy(ones_r[:], ones[:]).then_inc(ones_ready, 1)
            dve.wait_ge(k_loaded, 64)
            for e in range(KT):
                dve.wait_ge(prep_filled, e + 1)
                nc.vector.tensor_scalar(k_t[:, e], psum_prep[:, e % 2, 0:BATCH * CTX], bk_sb[:, e:e + 1], None,
                                        ALU.add).then_inc(prep_read, 1)
            dve.wait_ge(prep_read, KT)
            nc.vector.tensor_scalar(bqk[:], k_t[:, 0], bq_sb[:, 0:1], None, ALU.mult).then_inc(bqk_step, 1)
            for e in range(1, KT):
                dve.wait_ge(bqk_step, e)
                nc.vector.scalar_tensor_tensor(out=bqk[:], in0=k_t[:, e], scalar=bq_sb[:, e:e + 1], in1=bqk[:],
                                               op0=ALU.mult, op1=ALU.add).then_inc(bqk_step, 1)
            dve.wait_ge(bqk_step, KT)
            nc.vector.tensor_copy(bqk_hi[:], bqk[:]).then_inc(bqk_step, 1)
            dve.wait_ge(bqk_step, KT + 1)
            nc.vector.tensor_tensor(bqk_lo[:], bqk[:], bqk_hi[:].bitcast(F32), ALU.subtract).then_inc(bqk_step, 1)

            def products_lo():
                for k in range(KT):
                    dve.wait_ge(m_hi_done, k + 1)
                    nc.vector.tensor_tensor(m_lo[:, k], psum_prep[:, k % 2, 0:BATCH * CTX], m_hi[:, k].bitcast(F32),
                                            ALU.subtract).then_inc(prep_read, 1)

            def v_group(j):
                half = j % 2
                if j == 0:
                    dve.wait_ge(v_loaded, 32)
                if j >= 2:
                    dve.wait_ge(v_lo_done, j - 1)
                dve.wait_ge(prep_filled, 2 * KT + j + 1)
                nc.vector.tensor_tensor(v_rows[:, half], psum_prep[0:HK, half], bv_rows[0:HK], ALU.add
                                        ).then_inc(v_biased, 1)
                dve.wait_ge(v_hi_done, j + 1)
                nc.vector.tensor_tensor(v_lo[:, j // 2, half], v_rows[:, half], v_hi[:, j // 2, half].bitcast(F32),
                                        ALU.subtract).then_inc(v_lo_done, 1)

            def x_lo(a, q, par):
                dve.wait_ge(xt_hi_done[a], q + 1)
                nc.vector.tensor_tensor(xt_lo[a][:, par], psum_xt[a][:], xt_hi[a][:, par].bitcast(F32),
                                        ALU.subtract).then_inc(xt_lo_done[a], 1)

            def ln_apply(a, q, par):
                dve.wait_ge(rstd_done[a], q + 1)
                free(dve, xt_filled[a], q, 2)
                nc.vector.tensor_scalar(xn[a][:, par], x_all[:, q], mean_var[a][:, par, 0:1],
                                        rstd[a][:, par:par + 1], ALU.subtract, ALU.mult).then_inc(xn_ready[a], 1)

            def step(g, r, has):
                even, odd = r % 2, (r + 1) % 2
                if has(g + 1):
                    free(dve, xn_ready[0], g + 1, 2)
                    if r == 3:
                        wait_apart(dve, x_loaded, (g + 1) * 8 + 32, spare)
                    else:
                        free(dve, stats_done[0], g + 1, 1)
                        dve.sem_inc(spare, 1)
                    nc.vector.bn_stats(stats[0][:, odd], x_all[:, g + 1]).then_inc(stats_done[0], 1)
                    wait_apart(dve, stats_done[0], g + 2, spare)
                    nc.vector.bn_aggr(mean_var[0][:, odd], stats[0][:, odd]).then_inc(mean_var_done[0], 1)
                if isinstance(g, int) and g == 0:
                    products_lo()
                if has(g):
                    x_lo(0, g, even)
                for j in v_groups(g):
                    v_group(j)
                if has(g - 1):
                    free(dve, exp_done, g - 1, 2)
                    dve.wait_ge(s_filled, g)
                    nc.vector.tensor_reduce(minus_max[:, odd:odd + 1], psum_s[:], AX_X, ALU.max,
                                            negate=True).then_inc(max_done, 1)
                if has(g - 2):
                    dve.wait_ge(pt_hi_done, g - 1)
                    nc.vector.tensor_tensor(pt_lo[:, even], psum_pt[:], pt_hi[:, even].bitcast(F32),
                                            ALU.subtract).then_inc(pt_lo_done, 1)
                    dve.wait_ge(exp_done, g - 1)
                    free(dve, x_mid, g - 2, 2)
                    nc.vector.reciprocal(inv_sum[:, even:even + 1], weight_sum[:, even:even + 1]).then_inc(inv_done, 1)
                if has(g + 1):
                    ln_apply(0, g + 1, odd)
                if has(g - 3):
                    dve.wait_ge(inv_done, g - 2)
                    dve.wait_ge(o_filled, g - 2)
                    nc.vector.scalar_tensor_tensor(out=x_all[:, g - 3], in0=psum_o[:], scalar=inv_sum[:, odd:odd + 1],
                                                   in1=x_all[:, g - 3], op0=ALU.mult, op1=ALU.add).then_inc(x_mid, 1)
                if has(g - 4):
                    ln_apply(1, g - 4, even)
                if has(g - 3):
                    free(dve, xn_ready[1], g - 3, 2)
                    wait_apart(dve, x_mid, g - 2, spare)
                    nc.vector.bn_stats(stats[1][:, odd], x_all[:, g - 3]).then_inc(stats_done[1], 1)
                    wait_apart(dve, stats_done[1], g - 2, spare)
                    nc.vector.bn_aggr(mean_var[1][:, odd], stats[1][:, odd]).then_inc(mean_var_done[1], 1)
                if has(g - 5):
                    x_lo(1, g - 5, odd)
                if isinstance(g, int) and g == 3:
                    dve.wait_ge(rows_loaded, 32)
                    nc.vector.tensor_scalar(scb_rows[:], scb_rows[:], 1.0 / 127.0, None, ALU.mult).then_inc(scb_ready, 1)
                if isinstance(g, int) and g == 6:
                    dve.wait_ge(scb_ready, 1)
                if has(g - 6):
                    free(dve, out_ready, g - 6, 2)
                    dve.wait_ge(f_filled, g - 5)
                    nc.vector.tensor_tensor(scaled[:, even], psum_f[:], scb_rows[:], ALU.mult).then_inc(scaled_done, 1)

            steps(dve, step)

        @block.tensor
        def _(pe):
            def prep_group(out, pairs):
                for k, (stat, mov) in enumerate(pairs):
                    mm = nc.tensor.matmul(out, stat, mov, start=(k == 0), stop=(k == len(pairs) - 1))
                mm.then_inc(prep_filled, 1)

            pe.wait_ge(k_loaded, 64)
            for e in range(KT):
                if e >= 2:
                    pe.wait_ge(prep_read, e - 1)
                prep_group(psum_prep[:, e % 2, 0:BATCH * CTX],
                           [(wk_sb[:, k, e * P:(e + 1) * P], ctx_sb[:, k]) for k in range(KC)])
            pe.wait_ge(wq_loaded, 16)
            pe.wait_ge(prep_read, KT)
            for d in range(KT):
                if d >= 2:
                    pe.wait_ge(prep_read, KT + d - 1)
                prep_group(psum_prep[:, d % 2, 0:BATCH * CTX],
                           [(wq_sb[:, e, d * P:(d + 1) * P], k_t[:, e]) for e in range(KT)])

            def v_group(j):
                if j == 0:
                    pe.wait_ge(v_loaded, 32)
                    pe.wait_ge(prep_read, 2 * KT)
                if j >= 2:
                    pe.wait_ge(v_biased, j - 1)
                prep_group(psum_prep[0:HK, j % 2],
                           [(ctx_sb[:, k, j * HK:(j + 1) * HK], wv_sb[:, k]) for k in range(KC)])

            def transposes(a, q, par):
                pe.wait_ge(xn_ready[a], q + 1)
                free(pe, xt_lo_done[a], q, 1)
                for k in range(KT):
                    mm = nc.tensor.transpose(psum_xt[a][:, k], xn[a][:, par, k * P:(k + 1) * P], ident[:])
                mm.then_inc(xt_filled[a], 1)

            pe.wait_ge(ones_ready, 1)
            pe.wait_ge(consts_set, 4)

            def step(g, r, has):
                even, odd = r % 2, (r + 1) % 2
                if has(g):
                    transposes(0, g, even)
                for j in v_groups(g):
                    v_group(j)
                if isinstance(g, int) and g == 1:
                    pe.wait_ge(prep_read, 2 * KT)
                    pe.wait_ge(bqk_step, KT + 2)
                if isinstance(g, int) and g in (3, 4):
                    pe.wait_ge(v_lo_done, 2 * (g - 2))
                if isinstance(g, int) and g == 6:
                    pe.wait_ge(cb_lo_done, KT)
                if has(g - 1):
                    keys = slice(odd * CTX, (odd + 1) * CTX)
                    pe.wait_ge(xt_lo_done[0], g)
                    free(pe, exp_done, g - 1, 1)
                    for k in range(KT):
                        split_matmul(nc, psum_s[:], (xt_hi[0][:, odd, k], xt_lo[0][:, odd, k]),
                                     (m_hi[:, k, keys], m_lo[:, k, keys]), k == 0, False)
                    nc.tensor.matmul(psum_s[:], ones_r[:], bqk_hi[:, keys], start=False, stop=False)
                    nc.tensor.matmul(psum_s[:], ones_r[:], bqk_lo[:, keys], start=False, stop=True).then_inc(s_filled, 1)
                if has(g - 2):
                    pe.wait_ge(exp_done, g - 1)
                    free(pe, pt_lo_done, g - 2, 1)
                    for half in range(2):
                        mm = nc.tensor.transpose(psum_pt[:, half], probs[:, even, half * HK:(half + 1) * HK], ident[:])
                    mm.then_inc(pt_filled, 1)
                if has(g - 3):
                    pe.wait_ge(pt_lo_done, g - 2)
                    free(pe, x_mid, g - 3, 1)
                    for half in range(2):
                        mm = split_matmul(nc, psum_o[:], (pt_hi[:, odd, half], pt_lo[:, odd, half]),
                                          (v_hi[:, odd, half], v_lo[:, odd, half]), half == 0, half == 1)
                    mm.then_inc(o_filled, 1)
                if has(g - 5):
                    transposes(1, g - 5, odd)
                if has(g - 6):
                    pe.wait_ge(xt_lo_done[1], g - 5)
                    free(pe, scaled_done, g - 6, 1)
                    for k in range(KT):
                        mm = split_matmul(nc, psum_f[:], (xt_hi[1][:, even, k], xt_lo[1][:, even, k]),
                                          (cb_hi[:, k], cb_lo[:, k]), k == 0, k == KT - 1)
                    mm.then_inc(f_filled, 1)

            steps(pe, step)


def cross_attention_ffn_twice(nc, a, out):
    x1 = nc.dram_tensor("x_after_attention", (ROWS, D), F32, kind="Internal").ap()
    x2 = nc.dram_tensor("x_after_spikes", (ROWS, D), F32, kind="Internal").ap()
    multi_head_attention(nc, a["x"], x1, a["ctx_t"], a["wq0_t"], a["wk0_t"], a["wv0_t"], a["wo0_t"])
    spiking_ffn(nc, x1, x2, a["w_fc"], a["w_proj"])
    single_head_attention_and_linear(nc, x2, out, a["ctx_t"], a["wq1_t"], a["bq1"], a["wk1"], a["bk1"],
                                     a["wv1"], a["bv1"], a["cb_t"], a["scb"], a["bias"])


def kernel(**inputs):
    import numpy as _np
    import concourse.bacc as _bacc
    from concourse import mybir as _mybir
    from concourse.bass_utils import run_bass_kernel_spmd as _run

    g = {k: _np.asarray(v) for k, v in inputs.items()}

    def tiles(w):
        return w.reshape(-1, 128, w.shape[-1]).transpose(1, 0, 2)

    def column(v):
        return v.reshape(-1, 128).T

    w_kv = g["L0_xattn_Wkv"]
    arrays = {
        "x": g["x"].reshape(ROWS, D),
        "ctx_t": tiles(g["ctx_512"].reshape(BATCH * CTX, CTXD).T),
        "wq0_t": tiles(g["L0_xattn_Wq"].T), "wk0_t": tiles(w_kv[:D].T), "wv0_t": tiles(w_kv[D:].T),
        "wo0_t": tiles(g["L0_xattn_Wo"].T),
        "w_fc": g["L0_ffn_W_fc"].T.reshape(KT, P, NF, P).transpose(1, 2, 0, 3).reshape(P, NF, KT * P),
        "w_proj": tiles(g["L0_ffn_W_proj"].T),
        "wq1_t": tiles(g["L1_xattn_Wq"].T), "bq1": column(g["L1_xattn_bq"]),
        "wk1": tiles(g["L1_xattn_Wk"]), "bk1": column(g["L1_xattn_bk"]),
        "wv1": tiles(g["L1_xattn_Wv"]), "bv1": g["L1_xattn_bv"].reshape(1, D),
        "cb_t": tiles(g["L1_ffn_CB"].T),
        "scb": g["L1_ffn_SCB"].reshape(1, D), "bias": g["L1_ffn_bias"].reshape(1, D),
    }
    nc = _bacc.Bacc("TRN2", target_bir_lowering=False, num_devices=1)
    args, sent = {}, {}
    for name, a in arrays.items():
        a = _np.ascontiguousarray(a)
        sent[f"in_{name}_dram"] = a
        args[name] = nc.dram_tensor(f"in_{name}_dram", a.shape, _mybir.dt.from_np(a.dtype), kind="ExternalInput").ap()
    out = nc.dram_tensor("out_0_dram", (ROWS, D), _mybir.dt.float32, kind="ExternalOutput").ap()
    cross_attention_ffn_twice(nc, args, out)
    r = _run(nc, [sent], core_ids=[0])
    return r.results[0]["out_0_dram"].reshape(BATCH, SEQ, D)
```

```python
from contextlib import ExitStack

import concourse.bass as bass
import numpy as np
from concourse import mybir
from concourse.alu_op_type import AluOpType as ALU

ACT = mybir.ActivationFunctionType
AX_X = mybir.AxisListType.X
F32 = mybir.dt.float32
F32R = mybir.dt.float32r

P = 128
D = 512
BATCH, SEQ = 2, 2048
ROWS = BATCH * SEQ
CTX, CTXD = 154, 256
HEADS, HD = 16, 32
FF = 2048
KT = D // P
T = 4
CH = T * P
NCH = ROWS // CH
NF = FF // P
EPS = 1e-5
LIF_BETA, LIF_THRESHOLD, LIF_STEPS = 0.9, 1.0, 5


def split_matmul(nc, out, stat, mov, start, stop):
    nc.tensor.matmul(out, stat[0], mov[0], start=start, stop=False)
    nc.tensor.matmul(out, stat[0], mov[1], start=False, stop=False)
    return nc.tensor.matmul(out, stat[1], mov[0], start=False, stop=stop)


def spike_thresholds():
    one, beta = np.float32(LIF_THRESHOLD), np.float32(LIF_BETA)

    def count(y):
        mem, n = np.float32(0), 0
        for _ in range(LIF_STEPS):
            reset = one if mem > one else np.float32(0)
            mem = np.float32(np.float32(beta * mem + y) - reset)
            n += bool(mem > one)
        return n

    found = []
    for n in range(LIF_STEPS):
        low, high = np.float32(0), np.float32(2)
        while np.nextafter(low, high) < high:
            mid = np.float32((np.float64(low) + np.float64(high)) / 2)
            if mid in (low, high):
                break
            low, high = (low, mid) if count(mid) > n else (mid, high)
        found.append(float(low))
    return found


def neurons(nc, dve, part, y, count, x_rows, lif_step, out_ready, earlier, y_copied=None):
    thresholds = spike_thresholds()
    first = 2 * (part // 3)
    for s in range(2 * (part % 3), 2 * (part % 3) + 2):
        for t in (first, first + 1):
            c, j = count[:, t % 2], t % 2
            pair = LIF_STEPS * (earlier + first)
            if s == 0:
                if t >= 2:
                    dve.wait_ge(out_ready, earlier + (t - 1))
                if y_copied is not None:
                    dve.wait_ge(y_copied, earlier + (t + 1))
                nc.vector.tensor_scalar(c, y[:, t], thresholds[0], None, ALU.is_gt).then_inc(lif_step, 1)
            elif s < LIF_STEPS:
                dve.wait_ge(lif_step, pair + (2 * s - 1 + j))
                nc.vector.scalar_tensor_tensor(out=c, in0=y[:, t], scalar=thresholds[s], in1=c,
                                               op0=ALU.is_gt, op1=ALU.add).then_inc(lif_step, 1)
            else:
                dve.wait_ge(lif_step, pair + (2 * LIF_STEPS - 1 + j))
                nc.vector.scalar_tensor_tensor(out=x_rows[:, t], in0=c, scalar=1.0 / LIF_STEPS,
                                               in1=x_rows[:, t], op0=ALU.mult, op1=ALU.add).then_inc(out_ready, 1)


def wait_apart(engine, sem, value, spare):
    engine.wait_ge(sem, value)
    engine.sem_inc(spare, 1)



def multi_head_attention(nc, x_in, x_out, ctx_t, wq_t, wk_t, wv_t, wo_t, first_rows, mean_var, rstd,
                         x_stored):
    KC = CTXD // P
    NG = HEADS * HD // P
    GH = P // HD
    GC = GH * CTX
    NB = -(-GC // P)
    size = [min(P, GC - b * P) for b in range(NB)]
    PT_RING = NG
    SCALE = HD ** -0.5
    with ExitStack() as ctx:
        def sb(name, shape, dt=F32):
            return ctx.enter_context(nc.sbuf_tensor(name, shape, dt))

        def bank(name, shape):
            return ctx.enter_context(nc.psum_tensor(name, shape, F32))

        def sem(name):
            return ctx.enter_context(nc.semaphore("a_" + name))

        wq_hi, wq_lo = sb("wq_hi", [P, KT, D], F32R), sb("wq_lo", [P, KT, D], F32R)
        wo_hi, wo_lo = sb("wo_hi", [P, NG, D], F32R), sb("wo_lo", [P, NG, D], F32R)
        k_hi, k_lo = sb("k_hi", [P, BATCH, NG, GC], F32R), sb("k_lo", [P, BATCH, NG, GC], F32R)
        v_hi, v_lo = sb("va_hi", [P, BATCH, NG, NB, P], F32R), sb("va_lo", [P, BATCH, NG, NB, P], F32R)
        x_ln = first_rows
        x_res = sb("x_res", [P, 2, D])
        xt_hi, xt_lo = sb("xta_hi", [P, KT, CH], F32R), sb("xta_lo", [P, KT, CH], F32R)
        q_hi, q_lo = sb("q_hi", [P, 2, CH], F32R), sb("q_lo", [P, 2, CH], F32R)
        probs = sb("probs_a", [P, 2, T, GC])
        pt_hi, pt_lo = sb("pta_hi", [P, PT_RING, CH], F32R), sb("pta_lo", [P, PT_RING, CH], F32R)
        o_hi, o_lo = sb("o_hi", [P, NG + 2, CH], F32R), sb("o_lo", [P, NG + 2, CH], F32R)
        mask = sb("mask", [P, NB, GH])
        ident = sb("ident_a", [P, P])
        minus_half = sb("minus_half_a", [P, 1])
        stats, var_eps = sb("stats_a", [P, T, 6]), sb("var_eps_a", [P, T])
        minus_max, bias_max = sb("minus_max_a", [P, T, GH]), sb("bias_max_a", [P, T, GH])
        weight_sum, inv_sum = sb("weight_sum_a", [P, T, GH]), sb("inv_sum_a", [P, T, GH])
        flat = probs[:].rearrange("p a t c -> p a (t c)")
        ctx_rep = [flat[:, b, 0:KC * GC].rearrange("p (k c) -> p k c", k=KC) for b in range(BATCH)]
        wk_sb, wv_sb = (flat[:, b, KC * GC:KC * (GC + D)].rearrange("p (k n) -> p k n", k=KC) for b in range(2))
        heads_of = [range(b * P // CTX, (b * P + size[b] - 1) // CTX + 1) for b in range(NB)]
        PIECES = sum(len(heads) for heads in heads_of)

        psum_s = bank("psum_s_a", [P, 2, 2, 512])
        psum_tr = bank("psum_tr", [P, 2, 512])
        psum_q, psum_o = bank("psum_q", [P, CH]), bank("psum_o_a", [P, CH])

        ctx_loaded, rep_loaded = sem("ctx_loaded"), [sem("rep_loaded0"), sem("rep_loaded1")]
        raw_loaded = [sem("raw_loaded0"), sem("raw_loaded1")]
        consts_set, k_hi_zeroed, k_lo_zeroed = sem("consts_set"), sem("k_hi_zeroed"), sem("k_lo_zeroed")
        v_zeroed = sem("v_zeroed")
        k_filled, k_hi_done, k_lo_done = sem("k_filled"), sem("k_hi_done"), sem("k_lo_done")
        v_filled, v_hi_done, v_lo_done = sem("v_filled"), sem("v_hi_done"), sem("v_lo_done")
        w_hi_done, w_lo_done = sem("w_hi_done"), sem("w_lo_done")
        ln_loaded = [sem("ln_loaded0"), sem("ln_loaded1")]
        stats_done, mean_var_done, var_eps_done = sem("stats_done"), sem("mean_var_done"), sem("var_eps_done")
        rstd_done, xn_ready, xt_hi_done = sem("rstd_done"), sem("xn_ready"), sem("xt_hi_done")
        tr_filled, tr_free = sem("tr_filled"), sem("tr_free")
        wo_filled, wo_free = sem("wo_filled"), sem("wo_free")
        q_filled, q_hi_done, q_lo_done = sem("q_filled"), sem("q_hi_done"), sem("q_lo_done")
        o_hi_done, o_lo_done = sem("o_hi_done"), sem("o_lo_done")
        pt_hi_done, pv_done = sem("pt_hi_done"), sem("pv_done")
        s_filled, max_done, bias_done = sem("s_filled"), sem("max_done"), sem("bias_done")
        exp_done, inv_done, probs_ready = sem("exp_done"), sem("inv_done"), sem("probs_ready")
        res_loaded, tail_loaded = ([sem(f"{name}_loaded{parity}") for parity in range(2)] for name in ("res", "tail"))
        spare = sem("spare")

        x_view = x_in.rearrange("(b m t p) d -> b m t p d", b=BATCH, t=T, p=P)
        o_view = x_out.rearrange("(b m t p) d -> b m t p d", b=BATCH, t=T, p=P)

        def after(n, m, par):
            return (n + 1, m + par, 1 - par)

        def before(n, m, par):
            return (n - 1, m - 1 + par, 1 - par)

        def chunks(engine, body):
            body((0, 0, 0), True, False)
            with engine.Fori(1, NCH // 2) as i:
                body((i * 2 - 1, i - 1, 1), False, False)
                body((i * 2, i, 0), False, False)
            body((NCH - 1, NCH // 2 - 1, 1), False, True)

        def pt_slot(g, b):
            return (g - 1 + b) % PT_RING

        def o_slot(par, g):
            return g + NG * par if g < 2 else g

        WO_AT = (1, 3)
        TR_USES = NG * NB + 2 + T
        LEAD = T - 2 - NB
        step_start = [LEAD, LEAD + NB, LEAD + 2 * NB + 2, LEAD + 3 * NB + 2]

        def is_chunk(n, number):
            return isinstance(n, int) and n == number

        def use_pt(n, g, b):
            if is_chunk(n, 0) and g == 1:
                return T + b
            others = WO_AT if g == 1 else range(T) if g == NG - 1 and not is_chunk(n, NCH - 1) else ()
            earlier = sum(at < b for at in others)
            return n * TR_USES + (step_start[g] + b + earlier - (T if is_chunk(n, NCH) else 0))

        def use_wo(n, t):
            if is_chunk(n, NCH - 1):
                return use_pt(NCH, 0, NB + t)
            return (n + 1) * TR_USES + (step_start[1] + WO_AT[t] + t + 1)

        def use_xt(n, t):
            if is_chunk(n, 0):
                return t
            return (n - 1) * TR_USES + (step_start[NG - 1] + 2 * t + 1)

        def res_tile(n, t):
            if is_chunk(n, NCH - 1) and t >= 2:
                return flat[:, 0, (t - 2) * D:(t - 1) * D]
            return x_res[:, t % 2]

        def wo_bank(n, t):
            if is_chunk(n, NCH - 1) and t == T - 1:
                return psum_s[:, 0, 0]
            return psum_tr[:, tr_bank(use_wo, n, t)] if t < 2 else psum_q[:]

        def tr_bank(use, n, *place):
            return use(n if isinstance(n, int) else 2, *place) % 2

        assert TR_USES % 2 == 0

        def has_before(c, g):
            return not (isinstance(c[0], int) and c[0] == 0 and g <= 0)

        def v_bank(j):
            return (psum_o[:], psum_q[:])[j % 2] if j < NB else (psum_tr[:, 0], psum_tr[:, 1], psum_o[:])[(j - NB) % 3]

        def v_source(j):
            return v_bank(j).rearrange("p (g c) -> p g c", g=NG)

        def v_pieces(j):
            return sum(len(heads_of[i % NB]) for i in range(j))

        block = ctx.enter_context(nc.Block())

        @block.sync
        def _(sp):
            def load_ln(c, t):
                n, m, par = c
                sp.dma_start(x_ln[:, t], x_view[par, m, t]).then_inc(ln_loaded[t % 2], 16)

            def load_res(c, t):
                n, m, par = c
                if not (isinstance(n, int) and 2 * n + t // 2 == 0):
                    sp.wait_ge(x_stored[t % 2], (n * 2 + t // 2) * 16)
                sp.dma_start(x_res[:, t % 2], x_view[par, m, t]).then_inc(res_loaded[t % 2], 16)

            def load_weights(js):
                for j in js:
                    if j >= 2:
                        sp.wait_ge(w_lo_done, j - 1)
                    src = wq_t[:, j] if j < KT else wo_t[:, j - KT]
                    sp.dma_start(x_res[:, j % 2], src).then_inc(raw_loaded[j % 2], 16)

            for t in range(2):
                load_ln((0, 0, 0), t)
            def load_keys(b, h, loaded):
                sp.dma_start(ctx_rep[b][:, :, h * CTX:(h + 1) * CTX],
                             ctx_t[:, :, b * CTX:(b + 1) * CTX]).then_inc(loaded, 16)

            for b in range(BATCH):
                load_keys(b, 0, ctx_loaded)
            sp.dma_start(wk_sb, wk_t).then_inc(ctx_loaded, 16)
            for t in range(2, T):
                sp.wait_ge(ln_loaded[t % 2], 16)
                load_ln((0, 0, 0), t)
            load_weights(range(2))
            sp.dma_start(wv_sb, wv_t).then_inc(rep_loaded[0], 16)
            for b in range(BATCH):
                for h in range(1, GH):
                    load_keys(b, h, rep_loaded[b])
            load_weights(range(2, KT + 2))

            def residual(c):
                n, m, par = c
                load_res(c, 0)
                load_res(c, 1)
                if is_chunk(n, NCH - 1):
                    sp.wait_ge(tr_filled, use_pt(n, NG - 1, NB - 1) + 1)
                    for t in range(2, T):
                        sp.dma_start(res_tile(n, t), x_view[par, m, t]).then_inc(tail_loaded[t % 2], 16)
                for t in range(T):
                    if t < 2:
                        sp.wait_ge(tr_free, use_wo(n, t) + 1)
                    else:
                        sp.wait_ge(wo_free, n * 2 + (t - 1))
                    sp.dma_start(o_view[par, m, t], res_tile(n, t)).then_inc(x_stored[t % 2], 16)
                    if t + 2 < T and not is_chunk(n, NCH - 1):
                        load_res(c, t + 2)

            def body(c, first, last):
                if last:
                    for parity in range(2):
                        sp.wait_ge(x_stored[parity], 16 * T // 2)
                for t in range(T):
                    sp.wait_ge(tr_filled, use_xt(c[0], t) + 1)
                    if t >= 2:
                        sp.wait_ge(ln_loaded[t % 2], (after(*c)[0] * 2 + 1) * 16)
                    if last:
                        sp.dma_start(x_ln[:, t], o_view[0, 0, t]).then_inc(ln_loaded[t % 2], 16)
                    else:
                        load_ln(after(*c), t)
                if first:
                    load_weights(range(KT + 2, 2 * KT))
                    sp.wait_ge(w_lo_done, 2 * KT)
                else:
                    residual(before(*c))

            chunks(sp, body)
            residual((NCH - 1, NCH // 2 - 1, 1))

        @block.gpsimd
        def _(pool):
            nc.gpsimd.memset(ident[:], 0.0).then_inc(consts_set, 1)
            pool.wait_ge(consts_set, 1)
            nc.gpsimd.affine_select(out=ident[:], in_=ident[:], compare_op=ALU.not_equal, fill=1.0,
                                    base=0, pattern=[[-1, P]], channel_multiplier=1).then_inc(consts_set, 1)
            nc.gpsimd.memset(minus_half[:], -0.5).then_inc(consts_set, 1)
            nc.gpsimd.memset(mask[:], 1.0).then_inc(consts_set, 1)
            nc.gpsimd.memset(k_hi[:].bitcast(F32), 0.0).then_inc(k_hi_zeroed, 1)
            pool.wait_ge(consts_set, 4)

            def inverse_std(n, t):
                q = n * T + t
                wait_apart(pool, mean_var_done, q + 1, spare)
                nc.gpsimd.tensor_scalar(var_eps[:, t:t + 1], mean_var[:, t, 1:2], EPS, None,
                                        ALU.add).then_inc(var_eps_done, 1)
                pool.wait_ge(var_eps_done, q + 1)
                nc.gpsimd.tensor_tensor(rstd[:, t:t + 1], var_eps[:, t:t + 1], minus_half[:],
                                        ALU.pow).then_inc(rstd_done, 1)

            def zero_v(b):
                for half in (v_hi, v_lo):
                    nc.gpsimd.memset(half[:, b].bitcast(F32), 0.0).then_inc(v_zeroed, 1)

            def weights_lo(lo, hi, js):
                for j in js:
                    pool.wait_ge(w_hi_done, j + 1)
                    nc.gpsimd.tensor_tensor(lo[:, j % KT], x_res[:, j % 2], hi[:, j % KT].bitcast(F32),
                                            ALU.subtract).then_inc(w_lo_done, 1)

            for t in range(T):
                inverse_std(0, t)
            weights_lo(wq_lo, wq_hi, range(2))
            nc.gpsimd.affine_select(out=mask[:], in_=mask[:], compare_op=ALU.is_ge, fill=0.0, base=0,
                                    pattern=[[P, NB], [-CTX, GH]], channel_multiplier=1).then_inc(consts_set, 1)
            pool.wait_ge(consts_set, 5)
            nc.gpsimd.affine_select(out=mask[:], in_=mask[:], compare_op=ALU.is_ge, fill=0.0, base=CTX - 1,
                                    pattern=[[-P, NB], [CTX, GH]], channel_multiplier=-1).then_inc(consts_set, 1)

            zero_v(0)
            weights_lo(wq_lo, wq_hi, range(2, KT))
            zero_v(1)

            def body(c, first, last):
                for g in range(NG):
                    for t in range(T):
                        s = c[0] * (NG * T) + (g * T + t)
                        tile = probs[:, g % 2, t].rearrange("p (h c) -> p h c", h=GH)
                        pool.wait_ge(inv_done, s + 1)
                        nc.gpsimd.tensor_tensor(tile, tile, inv_sum[:, t].unsqueeze(2).to_broadcast([P, GH, CTX]),
                                                ALU.mult).then_inc(probs_ready, 1)
                        if g == 1:
                            inverse_std(after(*c)[0], t)
                    if first and g < 2:
                        weights_lo(wo_lo, wo_hi, range(KT + 2 * g, KT + 2 * g + 2))

            chunks(pool, body)

        @block.scalar
        def _(act):
            def x_hi(n, t):
                act.wait_ge(tr_filled, use_xt(n, t) + 1)
                nc.scalar.copy(xt_hi[:, :, t * P:(t + 1) * P],
                               psum_tr[:, tr_bank(use_xt, n, t)].rearrange(
                                   "p (k c) -> p k c", k=KT)).then_inc(xt_hi_done, 1)

            def group_hi(filled, count, out, in_, done):
                act.wait_ge(filled, count)
                nc.scalar.copy(out, in_).then_inc(done, 1)

            def weights_hi(hi, js):
                for j in js:
                    act.wait_ge(raw_loaded[j % 2], 16 * (j // 2 + 1))
                    nc.scalar.copy(hi[:, j % KT], x_res[:, j % 2]).then_inc(w_hi_done, 1)

            def values_hi(j):
                b, blk = j // NB, j % NB
                rows = slice(0, size[blk])
                act.wait_ge(v_filled, j + 1)
                for h in heads_of[blk]:
                    cols = slice(h * HD, (h + 1) * HD)
                    nc.scalar.activation(v_hi[rows, b, :, blk, cols], v_source(j)[rows, :, cols], ACT.Copy,
                                         scale=mask[rows, blk, h:h + 1]).then_inc(v_hi_done, 1)

            weights_hi(wq_hi, range(2))
            act.wait_ge(k_filled, NG)
            act.wait_ge(k_hi_zeroed, 1)
            for h in range(GH):
                rows = slice(h * HD, (h + 1) * HD)
                for b in range(BATCH):
                    nc.scalar.copy(k_hi[rows, b, :, h * CTX:(h + 1) * CTX],
                                   psum_s[rows, :, :, b * CTX:(b + 1) * CTX].rearrange("p a c n -> p (a c) n")
                                   ).then_inc(k_hi_done, 1)
                if h < 2:
                    x_hi(0, 2 * h)
                    x_hi(0, 2 * h + 1)
            act.wait_ge(consts_set, 6)
            act.wait_ge(v_zeroed, 1)
            for j in range(NB):
                values_hi(j)
                if j == 0:
                    weights_hi(wq_hi, range(2, KT))
            group_hi(q_filled, 1, q_hi[:, 0], psum_q[:], q_hi_done)
            act.wait_ge(v_zeroed, 3)

            def p_hi(c, g, b):
                G = c[0] * NG + (g - 1)
                if not isinstance(G, int) or G * NB + b >= PT_RING:
                    act.wait_ge(pv_done, G * NB + (b + 1 - PT_RING))
                act.wait_ge(tr_filled, use_pt(c[0], g, b) + 1)
                nc.scalar.copy(pt_hi[0:size[b], pt_slot(g, b)], psum_tr[0:size[b], tr_bank(use_pt, c[0], g, b)]).then_inc(pt_hi_done, 1)

            def exps(c, g, t):
                s = c[0] * (NG * T) + (g * T + t)
                act.wait_ge(bias_done, s + 1)
                for h in range(GH):
                    ins = nc.scalar.activation(probs[:, g % 2, t, h * CTX:(h + 1) * CTX],
                                               psum_s[:, t % 2, h // 2, (h % 2) * CTX:(h % 2 + 1) * CTX], ACT.Exp,
                                               bias=bias_max[:, t, h:h + 1], scale=SCALE,
                                               accum_out=weight_sum[:, t, h:h + 1])
                ins.then_inc(exp_done, 1)

            def q_first(c, g):
                group_hi(q_filled, c[0] * NG + (g + 2), q_hi[:, (g + 1) % 2], psum_q[:], q_hi_done)

            def o_first(c, g):
                group_hi(pv_done, (c[0] * NG + (g - 1)) * NB, o_hi[:, o_slot(c[2], (g - 2) % NG)], psum_o[:], o_hi_done)

            def body(c, first, last):
                for g in range(NG):
                    there = has_before(c, g)
                    if has_before(c, g - 1):
                        o_first(c, g)
                    exps(c, g, 0)
                    for t in range(T):
                        if there:
                            p_hi(c, g, t)
                        if g == NG - 1 and not last:
                            x_hi(after(*c)[0], t)
                        if t + 1 < T:
                            exps(c, g, t + 1)
                        if first and g == 0:
                            values_hi(NB + t)
                    if first and g == 0:
                        values_hi(2 * NB - 1)
                    if g < NG - 1:
                        q_first(c, g)
                    if first and g < 2:
                        weights_hi(wo_hi, range(KT + 2 * g, KT + 2 * g + 2))
                    if there:
                        p_hi(c, g, NB - 1)
                    if g == NG - 1 and not last:
                        q_first(c, g)

            chunks(act, body)
            end = (NCH, 0, 0)
            o_first(end, 0)
            for b in range(NB):
                p_hi(end, 0, b)
            o_first(end, 1)

        @block.vector
        def _(dve):
            def ln_stats(n, t):
                q = n * T + t
                if not (isinstance(n, int) and n == 0):
                    wait_apart(dve, rstd_done, n * T, spare)
                wait_apart(dve, ln_loaded[t % 2], (n * 2 + (t // 2 + 1)) * 16, spare)
                nc.vector.bn_stats(stats[:, t], x_ln[:, t]).then_inc(stats_done, 1)
                wait_apart(dve, stats_done, q + 1, spare)
                nc.vector.bn_aggr(mean_var[:, t], stats[:, t]).then_inc(mean_var_done, 1)

            def ln_apply(n, t):
                dve.wait_ge(rstd_done, n * T + (t + 1))
                nc.vector.tensor_scalar(x_ln[:, t], x_ln[:, t], mean_var[:, t, 0:1], rstd[:, t:t + 1],
                                        ALU.subtract, ALU.mult).then_inc(xn_ready, 1)

            def x_lo(n, t):
                cols = slice(t * P, (t + 1) * P)
                bank = tr_bank(use_xt, n, t)
                dve.wait_ge(xt_hi_done, n * T + (t + 1))
                nc.vector.tensor_tensor(xt_lo[:, :, cols], psum_tr[:, bank].rearrange("p (k c) -> p k c", k=KT),
                                        xt_hi[:, :, cols].bitcast(F32), ALU.subtract).then_inc(tr_free, 1)

            def group_lo(hi_done, G, out, in_, hi, done):
                dve.wait_ge(hi_done, G + 1)
                nc.vector.tensor_tensor(out, in_, hi.bitcast(F32), ALU.subtract).then_inc(done, 1)

            nc.vector.memset(k_lo[:].bitcast(F32), 0.0).then_inc(k_lo_zeroed, 1)
            for t in range(T):
                ln_stats(0, t)
            for t in range(T):
                ln_apply(0, t)
            dve.wait_ge(k_lo_zeroed, 1)
            for h in range(GH):
                rows = slice(h * HD, (h + 1) * HD)
                dve.wait_ge(k_hi_done, BATCH * (h + 1))
                for b in range(BATCH):
                    nc.vector.tensor_tensor(k_lo[rows, b, :, h * CTX:(h + 1) * CTX],
                                            psum_s[rows, :, :, b * CTX:(b + 1) * CTX].rearrange("p a c n -> p (a c) n"),
                                            k_hi[rows, b, :, h * CTX:(h + 1) * CTX].bitcast(F32),
                                            ALU.subtract).then_inc(k_lo_done, 1)
                if h < 2:
                    x_lo(0, 2 * h)
                    x_lo(0, 2 * h + 1)

            def values_lo(j):
                b, blk = j // NB, j % NB
                rows = slice(0, size[blk])
                dve.wait_ge(v_hi_done, v_pieces(j + 1))
                for h in heads_of[blk]:
                    cols = slice(h * HD, (h + 1) * HD)
                    nc.vector.scalar_tensor_tensor(out=v_lo[rows, b, :, blk, cols], in0=v_source(j)[rows, :, cols],
                                                   scalar=mask[rows, blk, h:h + 1],
                                                   in1=v_hi[rows, b, :, blk, cols].bitcast(F32),
                                                   op0=ALU.mult, op1=ALU.subtract).then_inc(v_lo_done, 1)

            dve.wait_ge(v_zeroed, 2)
            for j in range(NB):
                values_lo(j)
            group_lo(q_hi_done, 0, q_lo[:, 0], psum_q[:], q_hi[:, 0], q_lo_done)
            dve.wait_ge(v_zeroed, 4)

            def p_lo(c, g, b):
                G = c[0] * NG + (g - 1)
                dve.wait_ge(pt_hi_done, G * NB + (b + 1))
                slot = pt_slot(g, b)
                nc.vector.tensor_tensor(pt_lo[0:size[b], slot], psum_tr[0:size[b], tr_bank(use_pt, c[0], g, b)],
                                        pt_hi[0:size[b], slot].bitcast(F32), ALU.subtract).then_inc(tr_free, 1)

            def maxima(c, g, t):
                s = c[0] * (NG * T) + (g * T + t)
                dve.wait_ge(s_filled, s + 1)
                nc.vector.tensor_reduce(minus_max[:, t],
                                        psum_s[:, t % 2, :, 0:2 * CTX].rearrange("p a (h c) -> p a h c", h=2),
                                        AX_X, ALU.max, negate=True).then_inc(max_done, 1)
                dve.wait_ge(max_done, s + 1)
                nc.vector.tensor_scalar(bias_max[:, t], minus_max[:, t], SCALE, None, ALU.mult).then_inc(bias_done, 1)

            def inverse(c, g, t):
                s = c[0] * (NG * T) + (g * T + t)
                if not (isinstance(s, int) and s < T):
                    dve.wait_ge(probs_ready, s + (1 - T))
                dve.wait_ge(exp_done, s + 1)
                nc.vector.reciprocal(inv_sum[:, t], weight_sum[:, t]).then_inc(inv_done, 1)

            def wo_rows(c, t):
                n = c[0]
                if is_chunk(n, NCH - 1) and t >= 2:
                    dve.wait_ge(tail_loaded[t % 2], 16)
                else:
                    dve.wait_ge(res_loaded[t % 2], (n * 2 + (t // 2 + 1)) * 16)
                if t < 2:
                    dve.wait_ge(tr_filled, use_wo(n, t) + 1)
                else:
                    dve.wait_ge(wo_filled, n * 2 + (t - 1))
                rows = res_tile(n, t)
                nc.vector.tensor_tensor(rows, wo_bank(n, t), rows, ALU.add).then_inc(tr_free if t < 2 else wo_free, 1)

            def q_second(c, g):
                group_lo(q_hi_done, c[0] * NG + (g + 1), q_lo[:, (g + 1) % 2], psum_q[:], q_hi[:, (g + 1) % 2], q_lo_done)

            def o_second(c, g):
                slot = o_slot(c[2], (g - 2) % NG)
                group_lo(o_hi_done, c[0] * NG + (g - 2), o_lo[:, slot], psum_o[:], o_hi[:, slot], o_lo_done)

            def body(c, first, last):
                for g in range(NG):
                    there = has_before(c, g)
                    maxima(c, g, 0)
                    if has_before(c, g - 1):
                        o_second(c, g)
                    for t in range(T):
                        if t + 1 < T:
                            maxima(c, g, t + 1)
                        inverse(c, g, t)
                        if first and g == 0:
                            values_lo(NB + t)
                        if there:
                            p_lo(c, g, t)
                        if g == 1 and t in WO_AT and not first:
                            wo_rows(before(*c), WO_AT.index(t))
                        if g == NG - 1 and t % 2 and not first:
                            wo_rows(before(*c), 2 + t // 2)
                        if g == 1:
                            ln_stats(after(*c)[0], t)
                        if not last:
                            if 4 * g + t in range(5, 9):
                                ln_apply(after(*c)[0], 4 * g + t - 5)
                            if g == NG - 1:
                                x_lo(after(*c)[0], t)
                    if first and g == 0:
                        values_lo(2 * NB - 1)
                    if g < NG - 1:
                        q_second(c, g)
                    if there:
                        p_lo(c, g, NB - 1)
                    if g == NG - 1 and not last:
                        q_second(c, g)

            chunks(dve, body)
            end = (NCH, NCH // 2, 0)
            o_second(end, 0)
            for b in range(NB):
                p_lo(end, 0, b)
            o_second(end, 1)
            for t in range(T):
                wo_rows(before(*end), t)

        @block.tensor
        def _(pe):
            def claim_tr(use):
                if not (isinstance(use, int) and use < 2):
                    pe.wait_ge(tr_free, use - 1)

            def x_transposes(n, t):
                bank = tr_bank(use_xt, n, t)
                pe.wait_ge(xn_ready, n * T + (t + 1))
                claim_tr(use_xt(n, t))
                for k in range(KT):
                    mm = nc.tensor.transpose(psum_tr[:, bank, k * P:(k + 1) * P], x_ln[:, t, k * P:(k + 1) * P], ident[:])
                mm.then_inc(tr_filled, 1)

            def q_part(G, g, k):
                mm = split_matmul(nc, psum_q[:], (wq_hi[:, k, g * P:(g + 1) * P], wq_lo[:, k, g * P:(g + 1) * P]),
                                  (xt_hi[:, k], xt_lo[:, k]), k == 0, k == KT - 1)
                if k == KT - 1:
                    mm.then_inc(q_filled, 1)

            pe.wait_ge(ctx_loaded, 48)
            for g in range(NG):
                for b in range(BATCH):
                    for k in range(KC):
                        mm = nc.tensor.matmul(psum_s[:, g // 2, g % 2, b * CTX:(b + 1) * CTX],
                                              wk_sb[:, k, g * P:(g + 1) * P], ctx_rep[b][:, k, 0:CTX],
                                              start=(k == 0), stop=(k == KC - 1))
                mm.then_inc(k_filled, 1)
            pe.wait_ge(consts_set, 2)
            for t in range(T):
                x_transposes(0, t)

            def v_block(j):
                b, blk = j // NB, j % NB
                if j % NB == 0:
                    pe.wait_ge(rep_loaded[b], 16 * (GH - b))
                if 2 <= j < NB:
                    pe.wait_ge(v_lo_done, v_pieces(j - 1))
                elif j >= NB + 2:
                    pe.wait_ge(v_lo_done, v_pieces(j - 2))
                for k in range(KC):
                    mm = nc.tensor.matmul(v_bank(j)[0:size[blk]],
                                          ctx_rep[b][:, k, blk * P:blk * P + size[blk]], wv_sb[:, k],
                                          start=(k == 0), stop=(k == KC - 1))
                mm.then_inc(v_filled, 1)

            for j in range(NB):
                v_block(j)
            pe.wait_ge(tr_free, T)
            pe.wait_ge(v_lo_done, v_pieces(NB - 1))
            for k in range(KT):
                pe.wait_ge(w_lo_done, k + 1)
                q_part(0, 0, k)
            pe.wait_ge(k_lo_done, BATCH * GH)

            Q_PARTS = ((0, 1), (), (), (2, 3))

            def scores(c, g, t):
                n, m, par = c
                s = n * (NG * T) + (g * T + t)
                if t == 0:
                    pe.wait_ge(q_lo_done, n * NG + (g + 1))
                if not (isinstance(s, int) and s < 2):
                    pe.wait_ge(exp_done, s - 1)
                rows = slice(t * P, (t + 1) * P)
                for pair in range(2):
                    keys = slice(pair * 2 * CTX, (pair + 1) * 2 * CTX)
                    mm = split_matmul(nc, psum_s[:, t % 2, pair, 0:2 * CTX],
                                      (q_hi[:, g % 2, rows], q_lo[:, g % 2, rows]),
                                      (k_hi[:, par, g, keys], k_lo[:, par, g, keys]), True, True)
                mm.then_inc(s_filled, 1)

            def p_transposes(c, g, b):
                if b == 0:
                    pe.wait_ge(probs_ready, c[0] * (NG * T) + g * T)
                claim_tr(use_pt(c[0], g, b))
                cols = slice(b * P, b * P + size[b])
                for t in range(T):
                    mm = nc.tensor.transpose(psum_tr[0:size[b], tr_bank(use_pt, c[0], g, b), t * P:(t + 1) * P],
                                             probs[:, (g - 1) % 2, t, cols], ident[:])
                mm.then_inc(tr_filled, 1)

            def values(c, g, b):
                G = c[0] * NG + (g - 1)
                gb = (g - 1) % NG
                par = c[2] if g else 1 - c[2]
                if b == 0 and not (isinstance(G, int) and G == 0):
                    pe.wait_ge(o_lo_done, G)
                pe.wait_ge(tr_free, use_pt(c[0], g, b) + 1)
                rows = slice(0, size[b])
                mm = split_matmul(nc, psum_o[:], (v_hi[rows, par, gb, b], v_lo[rows, par, gb, b]),
                                  (pt_hi[rows, pt_slot(g, b)], pt_lo[rows, pt_slot(g, b)]), b == 0, b == NB - 1)
                mm.then_inc(pv_done, 1)

            def q_count(n):
                return NCH * NG if is_chunk(n, NCH - 1) else n * NG + 2 * NG

            def wo_product(c, t, groups=range(NG)):
                n = c[0]
                if t == 0:
                    pe.wait_ge(w_lo_done, 2 * KT)
                    pe.wait_ge(o_lo_done, n * NG + NG)
                if groups[0] == 0:
                    if t < 2:
                        claim_tr(use_wo(n, t))
                    elif t == 2:
                        pe.wait_ge(q_lo_done, q_count(n))
                    elif not is_chunk(n, NCH - 1):
                        pe.wait_ge(wo_free, n * 2 + 1)
                product = wo_bank(n, t)
                rows = slice(t * P, (t + 1) * P)
                for g in groups:
                    slot = o_slot(c[2], g)
                    mm = split_matmul(nc, product, (o_hi[:, slot, rows], o_lo[:, slot, rows]),
                                      (wo_hi[:, g], wo_lo[:, g]), g == 0, g == NG - 1)
                if groups[-1] == NG - 1:
                    mm.then_inc(tr_filled if t < 2 else wo_filled, 1)

            def body(c, first, last):
                n = c[0]
                for g in range(NG):
                    there = has_before(c, g)
                    scores(c, g, 0)
                    if g and has_before(c, g - 1):
                        values(c, g - 1, NB - 1)
                    for t in range(T):
                        if t + 1 < T:
                            scores(c, g, t + 1)
                        if there:
                            p_transposes(c, g, t)
                        if g == NG - 1 and not first:
                            half = range(NG // 2) if t % 2 == 0 else range(NG // 2, NG)
                            wo_product(before(*c), 2 + t // 2, half)
                        if g == 1 and t in WO_AT and not first:
                            wo_product(before(*c), WO_AT.index(t))
                        if g == NG - 1 and not last:
                            x_transposes(after(*c)[0], t)
                        if g < NG - 1:
                            for k in Q_PARTS[t]:
                                q_part(n * NG + (g + 1), g + 1, k)
                        if first and g == 0:
                            v_block(NB + t)
                        if there and t:
                            values(c, g, t - 1)
                        if t == T - 1 and there:
                            p_transposes(c, g, NB - 1)
                    if first and g == 0:
                        v_block(2 * NB - 1)
                        pe.wait_ge(v_lo_done, 2 * PIECES)
                    if g == NG - 1 and not last:
                        if not first:
                            pe.wait_ge(wo_free, n * 2)
                        pe.wait_ge(tr_free, use_xt(after(*c)[0], T - 1) + 1)
                        for k in range(KT):
                            q_part(n * NG + NG, 0, k)
                    if there:
                        values(c, g, NB - 2)
                        if g == NG - 1:
                            values(c, g, NB - 1)

            chunks(pe, body)
            end = (NCH, NCH // 2, 0)
            for b in range(NB - 1):
                p_transposes(end, 0, b)
                if b:
                    values(end, 0, b - 1)
            p_transposes(end, 0, NB - 1)
            values(end, 0, NB - 2)
            values(end, 0, NB - 1)
            for t in range(T):
                wo_product(before(*end), t)


def spiking_ffn(nc, x_in, x_out, w_fc, w_proj, y, count, first_rows, first_mean_var, first_rstd, last_rows, x_in_stored,
                next_loads):
    XT_STEP = 11
    with ExitStack() as ctx:
        def sb(name, shape, dt=F32):
            return ctx.enter_context(nc.sbuf_tensor(name, shape, dt))

        def sem(name):
            return ctx.enter_context(nc.semaphore("b_" + name))

        wfc_hi = sb("wfc_hi", [P, NF, KT, P], F32R)
        wfc_lo = sb("wfc_lo", [P, NF, KT, P], F32R)
        wpr_hi = sb("wpr_hi", [P, NF, D], F32R)
        wpr_lo = sb("wpr_lo", [P, NF, D], F32R)
        xt_hi = sb("xt_hi", [P, 2, KT, CH], F32R)
        xt_lo = sb("xt_lo", [P, 2, KT, CH], F32R)
        x_rows = [first_rows, last_rows]
        xn = sb("xn", [P, 2, D])
        relu = sb("relu", [P, 2, CH])
        h_hi = sb("h_hi", [P, 2, CH], F32R)
        h_lo = sb("h_lo", [P, 2, CH], F32R)
        stats = sb("stats", [P, T, 6])
        moments = sb("moments", [P, 5, T])
        mean = sb("mean", [P, T])
        var_eps = sb("var_eps", [P, T])
        rstd = sb("rstd", [P, T])
        minus_half = sb("minus_half", [P, T])
        ident = sb("ident_b", [P, P])
        raw = y

        psum_fc = ctx.enter_context(nc.psum_tensor("psum_fc", [P, 2, CH], F32))
        psum_y = ctx.enter_context(nc.psum_tensor("psum_y", [P, T, D], F32))
        psum_xt = ctx.enter_context(nc.psum_tensor("psum_xt", [P, 2, KT * P], F32))

        ident_ready = sem("ident_ready")
        raw_loaded = [sem(f"raw_loaded{i}") for i in range(4)]
        w_hi_done, w_lo_done = sem("w_hi_done"), sem("w_lo_done")
        x_loaded, x_stored, next_loaded = sem("x_loaded"), sem("x_stored"), sem("next_loaded")
        stat_step = sem("stat_step")
        rstd_done = sem("rstd_done")
        var_ready = sem("var_ready")
        xn_ready = sem("xn_ready")
        xt_filled = sem("xt_filled")
        xt_hi_done, xt_lo_done = sem("xt_hi_done"), sem("xt_lo_done")
        fc_done = sem("fc_done")
        relu_done, sq_done = sem("relu_done"), sem("sq_done")
        h_hi_done, h_lo_done = sem("h_hi_done"), sem("h_lo_done")
        proj_done = sem("proj_done")
        y_copied = sem("y_copied")
        lif_step = sem("lif_step")
        out_ready = sem("out_ready")

        x_view = x_in.rearrange("(n t p) d -> n p t d", p=P, t=T)
        o_view = x_out.rearrange("(n t p) d -> n p t d", p=P, t=T)
        W_TILES = 2 * NF

        def w_tile(j):
            f = j // 2
            if j % 2 == 0:
                flat = lambda w: w[:, f, :, :].rearrange("p k n -> p (k n)")
                return w_fc[:, f, :], flat(wfc_hi), flat(wfc_lo)
            return w_proj[:, f, :], wpr_hi[:, f, :], wpr_lo[:, f, :]

        def chunks(engine, body):
            body(0, 0, True, False)
            with engine.Fori(1, NCH // 2) as i:
                for u in range(2):
                    body(i * 2 + (u - 1), (u + 1) % 2, False, False)
            body(NCH - 1, 1, False, True)

        block = ctx.enter_context(nc.Block())

        @block.sync
        def _(sp):
            for j in range(W_TILES):
                if j == T:
                    for stored in x_in_stored:
                        sp.wait_ge(stored, 16 * ROWS // P // 2)
                    sp.dma_start(x_rows[1][:], x_view[1]).then_inc(x_loaded, 16)
                if j >= T:
                    sp.wait_ge(w_lo_done, j - T + 1)
                sp.dma_start(raw[:, j % T, :], w_tile(j)[0]).then_inc(raw_loaded[j % T], 16)

            def body(n, par, first, last):
                if not first and not last:
                    sp.wait_ge(x_stored, 16 * T * n)
                    sp.dma_start(x_rows[1 - par][:], x_view[n + 1]).then_inc(x_loaded, 16)
                for t in range(0 if last else T):
                    sp.wait_ge(out_ready, T * n + t + 1)
                    sp.dma_start(o_view[n, :, t], x_rows[par][:, t]).then_inc(x_stored, 16)

            chunks(sp, body)
            sp.wait_ge(x_stored, 16 * T * (NCH - 1))
            for part, source in next_loads:
                sp.dma_start(part, source).then_inc(next_loaded, 16)
            sp.wait_ge(next_loaded, 16 * len(next_loads))

        @block.gpsimd
        def _(pool):
            nc.gpsimd.memset(ident[:], 0.0).then_inc(ident_ready, 1)
            pool.wait_ge(ident_ready, 1)
            nc.gpsimd.affine_select(out=ident[:], in_=ident[:], compare_op=ALU.not_equal, fill=1.0,
                                    base=0, pattern=[[-1, P]], channel_multiplier=1).then_inc(ident_ready, 1)
            nc.gpsimd.memset(minus_half[:], -0.5).then_inc(ident_ready, 1)
            pool.wait_ge(ident_ready, 3)

            def inverse_std(n):
                pool.wait_ge(var_ready, n)
                nc.gpsimd.tensor_tensor(rstd[:], var_eps[:], minus_half[:], ALU.pow).then_inc(rstd_done, 1)

            def weights_lo(f):
                for j in (2 * f, 2 * f + 1):
                    pool.wait_ge(w_hi_done, j + 1)
                    _, hi, lo = w_tile(j)
                    nc.gpsimd.tensor_tensor(lo, raw[:, j % T, :], hi.bitcast(F32), ALU.subtract).then_inc(w_lo_done, 1)

            for f in range(2):
                weights_lo(f)

            def body(n, par, first, last):
                for f in range(NF):
                    if first and f + 2 < NF:
                        weights_lo(f + 2)
                    if f == 9 and not last:
                        inverse_std(n + 1)
                    pool.wait_ge(h_hi_done, NF * n + f + 1)
                    nc.gpsimd.tensor_tensor(h_lo[:, f % 2], relu[:, f % 2], h_hi[:, f % 2].bitcast(F32),
                                            ALU.subtract).then_inc(h_lo_done, 1)

            chunks(pool, body)

        @block.scalar
        def _(act):
            def x_hi(n, par, t):
                act.wait_ge(xt_filled, T * n + t + 1)
                nc.scalar.copy(xt_hi[:, par, :, t * P:(t + 1) * P],
                               psum_xt[:, t % 2].rearrange("p (k c) -> p k c", k=KT)).then_inc(xt_hi_done, 1)

            def weights_hi(f):
                for j in (2 * f, 2 * f + 1):
                    act.wait_ge(raw_loaded[j % T], 16 * (j // T + 1))
                    nc.scalar.copy(w_tile(j)[1], raw[:, j % T, :]).then_inc(w_hi_done, 1)

            for t in range(T):
                x_hi(0, 0, t)
            for f in range(2):
                weights_hi(f)

            def h_first(n, f):
                act.wait_ge(fc_done, NF * n + f + 1)
                if not (isinstance(n, int) and NF * n + f < 2):
                    act.wait_ge(h_lo_done, NF * n + f - 1)
                nc.scalar.activation(relu[:, f % 2], psum_fc[:, f % 2], ACT.Relu).then_inc(relu_done, 1)

            def h_second(n, f):
                act.wait_ge(sq_done, NF * n + f + 1)
                if not (isinstance(n, int) and NF * n + f < 2):
                    act.wait_ge(proj_done, NF * n + f - 1)
                nc.scalar.copy(h_hi[:, f % 2], relu[:, f % 2]).then_inc(h_hi_done, 1)

            def copy_y(n):
                act.wait_ge(proj_done, NF * (n + 1))
                for t in range(T):
                    nc.scalar.copy(y[:, t], psum_y[:, t]).then_inc(y_copied, 1)

            def body(n, par, first, last):
                for f in range(NF):
                    if first and f + 2 < NF:
                        weights_hi(f + 2)
                    h_first(n, f)
                    h_second(n, f)
                    if not last and XT_STEP <= f < XT_STEP + T:
                        x_hi(n + 1, 1 - par, f - XT_STEP)
                    if f == 0 and not first:
                        copy_y(n - 1)
                if first:
                    act.wait_ge(w_lo_done, W_TILES)
                else:
                    act.wait_ge(out_ready, T * n)
                if last:
                    copy_y(n)

            chunks(act, body)

        @block.vector
        def _(dve):
            def ln_stats(n, par, t):
                if t == 0:
                    dve.wait_ge(x_loaded, 16 * n)
                nc.vector.bn_stats(stats[:, t], x_rows[par][:, t]).then_inc(stat_step, 1)

            def ln_variance(n):
                mean_e, m2_e, mean_o, m2_o = (stats[:, :, c] for c in (1, 2, 4, 5))
                done = (T + 6) * n - 6
                dve.wait_ge(stat_step, done)
                nc.vector.tensor_tensor(moments[:, 0], mean_e, mean_o, ALU.add).then_inc(stat_step, 1)
                nc.vector.tensor_tensor(moments[:, 1], mean_e, mean_o, ALU.subtract).then_inc(stat_step, 1)
                nc.vector.tensor_tensor(moments[:, 2], m2_e, m2_o, ALU.add).then_inc(stat_step, 1)
                dve.wait_ge(stat_step, done + 2)
                nc.vector.scalar_tensor_tensor(out=moments[:, 3], in0=moments[:, 1], scalar=D / 4.0,
                                               in1=moments[:, 1], op0=ALU.mult, op1=ALU.mult).then_inc(stat_step, 1)
                nc.vector.tensor_scalar(mean[:], moments[:, 0], 0.5, None, ALU.mult).then_inc(stat_step, 1)
                dve.wait_ge(stat_step, done + 4)
                nc.vector.tensor_tensor(moments[:, 4], moments[:, 3], moments[:, 2], ALU.add).then_inc(stat_step, 1)
                dve.wait_ge(stat_step, done + 6)
                nc.vector.tensor_scalar(var_eps[:], moments[:, 4], 1.0 / D, EPS, ALU.mult, ALU.add).then_inc(var_ready, 1)

            def ln_apply(n, par, t):
                first = isinstance(n, int) and n == 0
                if t == 0 and not first:
                    dve.wait_ge(rstd_done, n)
                if not (isinstance(n, int) and T * n + t < 2):
                    dve.wait_ge(xt_filled, T * n + t - 1)
                center = first_mean_var[:, t, 0:1] if first else mean[:, t:t + 1]
                scale = (first_rstd if first else rstd)[:, t:t + 1]
                nc.vector.tensor_scalar(xn[:, t % 2], x_rows[par][:, t], center, scale,
                                        ALU.subtract, ALU.mult).then_inc(xn_ready, 1)

            def x_lo(n, par, t):
                dve.wait_ge(xt_hi_done, T * n + t + 1)
                cols = slice(t * P, (t + 1) * P)
                nc.vector.tensor_tensor(xt_lo[:, par, :, cols],
                                        psum_xt[:, t % 2].rearrange("p (k c) -> p k c", k=KT),
                                        xt_hi[:, par, :, cols].bitcast(F32), ALU.subtract).then_inc(xt_lo_done, 1)

            def square(n, f):
                dve.wait_ge(relu_done, NF * n + f + 1)
                nc.vector.scalar_tensor_tensor(out=relu[:, f % 2], in0=psum_fc[:, f % 2], scalar=0.0,
                                               in1=relu[:, f % 2], op0=ALU.max, op1=ALU.mult).then_inc(sq_done, 1)

            for t in range(T):
                ln_apply(0, 0, t)
                if t >= 1:
                    x_lo(0, 0, t - 1)
            x_lo(0, 0, T - 1)

            def body(n, par, first, last):
                for f in range(NF):
                    square(n, f)
                    if not first and 1 <= f <= 6:
                        neurons(nc, dve, f - 1, y, count, x_rows[1 - par], lif_step, out_ready, T * (n - 1), y_copied)
                    if last:
                        continue
                    if f == 8:
                        for t in range(T):
                            ln_stats(n + 1, 1 - par, t)
                        ln_variance(n + 1)
                    if XT_STEP - 2 <= f < XT_STEP + T - 2:
                        ln_apply(n + 1, 1 - par, f - XT_STEP + 2)
                    if XT_STEP <= f < XT_STEP + T:
                        x_lo(n + 1, 1 - par, f - XT_STEP)

            chunks(dve, body)

        @block.tensor
        def _(pe):
            def transposes(n, t):
                pe.wait_ge(xn_ready, T * n + t + 1)
                if not (isinstance(n, int) and T * n + t < 2):
                    pe.wait_ge(xt_lo_done, T * n + t - 1)
                for k in range(KT):
                    mm = nc.tensor.transpose(psum_xt[:, t % 2, k * P:(k + 1) * P], xn[:, t % 2, k * P:(k + 1) * P], ident[:])
                mm.then_inc(xt_filled, 1)

            def hidden(n, par, f):
                if not (isinstance(n, int) and NF * n + f < 2):
                    pe.wait_ge(sq_done, NF * n + f - 1)
                for k in range(KT):
                    mm = split_matmul(nc, psum_fc[:, f % 2], (wfc_hi[:, f, k], wfc_lo[:, f, k]),
                                      (xt_hi[:, par, k], xt_lo[:, par, k]), k == 0, k == KT - 1)
                mm.then_inc(fc_done, 1)

            def project(n, f):
                pe.wait_ge(h_lo_done, NF * n + f + 1)
                for t in range(T):
                    cols = slice(t * P, (t + 1) * P)
                    mm = split_matmul(nc, psum_y[:, t], (h_hi[:, f % 2, cols], h_lo[:, f % 2, cols]),
                                      (wpr_hi[:, f], wpr_lo[:, f]), f == 0, f == NF - 1)
                mm.then_inc(proj_done, 1)

            pe.wait_ge(ident_ready, 3)
            for t in range(T):
                transposes(0, t)

            pe.wait_ge(xt_lo_done, T)
            pe.wait_ge(w_lo_done, 1)
            hidden(0, 0, 0)

            def body(n, par, first, last):
                for f in range(NF):
                    if not last and XT_STEP <= f < XT_STEP + T:
                        transposes(n + 1, f - XT_STEP)
                    if f + 1 < NF:
                        if first:
                            pe.wait_ge(w_lo_done, 2 * f + 3)
                        hidden(n, par, f + 1)
                    elif not last:
                        pe.wait_ge(xt_lo_done, T * (n + 2))
                        hidden(n + 1, 1 - par, 0)
                    if f == 0 and not first:
                        pe.wait_ge(y_copied, T * n)
                    if f == NF - 1 and first:
                        pe.wait_ge(w_lo_done, W_TILES)
                    project(n, f)

            chunks(pe, body)



def single_head_attention_and_linear(nc, x_in, x_out, ctx_sb, wq_t, bq_sb, wk_sb, bk_sb, wv, bv, cb_t, scb, bias,
                                     y, count, last_rows):
    KC = CTXD // P
    HK = CTX // 2
    NT = ROWS // P
    LAST_LAG = 6
    with ExitStack() as ctx:
        def sb(name, shape, dt=F32):
            return ctx.enter_context(nc.sbuf_tensor(name, shape, dt))

        def bank(name, shape):
            return ctx.enter_context(nc.psum_tensor(name, shape, F32))

        def sem(name):
            return ctx.enter_context(nc.semaphore("c_" + name))

        x_all = sb("x_all", [P, NT, D])
        wv_sb = sb("wv_sb", [P, KC, D])
        wq_sb = sb("wq_sb", [P, KT, D])
        bv_rows, bias_rows, scb_rows = sb("bv_rows", [P, D]), sb("bias_rows", [P, D]), sb("scb_rows", [P, D])
        k_t = sb("k_t", [P, KT, BATCH * CTX])
        m_hi, m_lo = sb("m_hi", [P, KT, BATCH * CTX], F32R), sb("m_lo", [P, KT, BATCH * CTX], F32R)
        bqk = sb("bqk", [P, BATCH * CTX])
        bqk_hi, bqk_lo = sb("bqk_hi", [P, BATCH * CTX], F32R), sb("bqk_lo", [P, BATCH * CTX], F32R)
        v_rows = sb("v_rows", [HK, 2, D])
        v_hi, v_lo = sb("v_hi", [HK, BATCH, 2, D], F32R), sb("v_lo", [HK, BATCH, 2, D], F32R)
        cb_raw = sb("cb_raw", [P, KT, D])
        cb_hi, cb_lo = sb("cb_hi", [P, KT, D], F32R), sb("cb_lo", [P, KT, D], F32R)
        ident, ones, ones_r = sb("ident_c", [P, P]), sb("ones_c", [P, P]), sb("ones_r", [P, P], F32R)
        minus_half = sb("minus_half_c", [P, 1])

        stats = [sb(f"stats{a}", [P, 2, 6]) for a in (1, 2)]
        mean_var = [sb(f"mean_var{a}", [P, 2, 2]) for a in (1, 2)]
        var_eps = [sb(f"var_eps{a}", [P, 2]) for a in (1, 2)]
        rstd = [sb(f"rstd{a}", [P, 2]) for a in (1, 2)]
        xn = [sb(f"xn{a}", [P, 2, D]) for a in (1, 2)]
        xt_hi = [sb(f"xt_hi{a}", [P, 2, KT, P], F32R) for a in (1, 2)]
        xt_lo = [sb(f"xt_lo{a}", [P, 2, KT, P], F32R) for a in (1, 2)]
        minus_max, weight_sum, inv_sum = sb("minus_max", [P, 2]), sb("weight_sum", [P, 2]), sb("inv_sum", [P, 2])
        probs = sb("probs", [P, 2, CTX])
        pt_hi, pt_lo = sb("pt_hi", [HK, 2, 2, P], F32R), sb("pt_lo", [HK, 2, 2, P], F32R)
        scaled = sb("scaled", [P, 2, D])

        psum_xt = [bank(f"psum_xt{a}", [P, KT, P]) for a in (1, 2)]
        psum_s, psum_pt = bank("psum_s", [P, CTX]), bank("psum_pt", [HK, 2, P])
        psum_o, psum_f = bank("psum_o", [P, D]), bank("psum_f", [P, D])
        psum_prep = bank("psum_prep", [P, 2, D])
        prep_bank = [psum_prep[:, 0], psum_prep[:, 1], psum_f[:], psum_o[:]]
        v_bank = [prep_bank[j % 3] for j in range(2 * BATCH)]

        lif_step, last_ready, last_stored = sem("lif_step"), sem("last_ready"), sem("last_stored")
        wq_loaded, v_loaded = sem("wq_loaded"), sem("v_loaded")
        cb_loaded, rows_loaded = sem("cb_loaded"), sem("rows_loaded")
        consts_set, ones_ready = sem("consts_set"), sem("ones_ready")
        prep_filled, prep_read = sem("prep_filled"), sem("prep_read")
        bqk_step, scb_ready = sem("bqk_step"), sem("scb_ready")
        m_hi_done, v_biased = sem("m_hi_done"), sem("v_biased")
        v_hi_done, v_lo_done = sem("v_hi_done"), sem("v_lo_done")
        cb_hi_done, cb_lo_done = sem("cb_hi_done"), sem("cb_lo_done")
        x_loaded, x_stored = sem("x_loaded"), sem("x_stored")
        stats_done = [sem(f"stats_done{a}") for a in (1, 2)]
        mean_var_done = [sem(f"mean_var_done{a}") for a in (1, 2)]
        var_eps_done = [sem(f"var_eps_done{a}") for a in (1, 2)]
        rstd_done = [sem(f"rstd_done{a}") for a in (1, 2)]
        xn_ready = [sem(f"xn_ready{a}") for a in (1, 2)]
        xt_filled = [sem(f"xt_filled{a}") for a in (1, 2)]
        xt_hi_done = [sem(f"xt_hi_done{a}") for a in (1, 2)]
        xt_lo_done = [sem(f"xt_lo_done{a}") for a in (1, 2)]
        s_filled, max_done, exp_done = sem("s_filled"), sem("max_done"), sem("exp_done")
        pt_filled, pt_hi_done, pt_lo_done = sem("pt_filled"), sem("pt_hi_done"), sem("pt_lo_done")
        inv_done, o_filled, x_mid = sem("inv_done"), sem("o_filled"), sem("x_mid")
        f_filled, scaled_done, biased, out_ready = sem("f_filled"), sem("scaled_done"), sem("biased"), sem("out_ready")
        spare = sem("spare")

        x_view = x_in.rearrange("(b i s p) d -> b i p s d", b=BATCH, s=2, p=P)
        o_view = x_out.rearrange("(b i s p) d -> b i p s d", b=BATCH, s=2, p=P)
        slots = x_all[:].rearrange("p (m b) d -> p m b d", b=BATCH)

        def steps(engine, step):
            begin, end = 7, NT - 1
            known = lambda q: isinstance(q, int)
            for g in range(-1, begin):
                step(g, g % 4, lambda q: 0 <= q < NT)
            with engine.Fori(0, (end - begin) // 4) as i:
                for u in range(4):
                    step(i * 4 + (begin + u), (begin + u) % 4, lambda q: True)
            for g in range(end, NT + LAST_LAG):
                step(g, g % 4, lambda q: 0 <= q < NT)

        def v_groups(g):
            return {0: (0, 1), 1: (2,), 2: (3,)}.get(g, ()) if isinstance(g, int) else ()

        def free(engine, sem, q, ring):
            if isinstance(q, int):
                if q - ring >= 0:
                    engine.wait_ge(sem, q - ring + 1)
            else:
                engine.wait_ge(sem, q + (1 - ring))

        block = ctx.enter_context(nc.Block())

        @block.sync
        def _(sp):
            def load(m):
                for b in range(BATCH):
                    sp.dma_start(slots[:, 2 * m:2 * m + 2, b], x_view[b, m]).then_inc(x_loaded, 16)

            sp.dma_start(wq_sb[:], wq_t).then_inc(wq_loaded, 16)
            load(0)
            sp.dma_start(wv_sb[:], wv).then_inc(v_loaded, 16)
            sp.dma_start(bv_rows[:], bv.broadcast_to([P, D])).then_inc(v_loaded, 16)
            sp.dma_start(cb_raw[:], cb_t).then_inc(cb_loaded, 16)
            for dst, src in ((bias_rows, bias), (scb_rows, scb)):
                sp.dma_start(dst[:], src.broadcast_to([P, D])).then_inc(rows_loaded, 16)
            for m in range(1, NT // 4):
                sp.wait_ge(x_loaded, 32 * m)
                if m == 4:
                    for t in range(T):
                        sp.wait_ge(last_ready, t + 1)
                        sp.dma_start(x_in[ROWS - CH + t * P:ROWS - CH + (t + 1) * P], last_rows[:, t]
                                     ).then_inc(last_stored, 16)
                if m == (SEQ - CH) // (2 * P):
                    sp.wait_ge(last_stored, 16 * T)
                load(m)
            with sp.Fori(0, NT // 4) as m:
                sp.wait_ge(out_ready, m * 4 + 4)
                for b in range(BATCH):
                    sp.dma_start(o_view[b, m], slots[:, bass.ds(m * 2, 2), b]).then_inc(x_stored, 16)
            sp.wait_ge(x_stored, 32 * (NT // 4))

        @block.gpsimd
        def _(pool):
            nc.gpsimd.memset(ident[:], 0.0).then_inc(consts_set, 1)
            pool.wait_ge(consts_set, 1)
            nc.gpsimd.affine_select(out=ident[:], in_=ident[:], compare_op=ALU.not_equal, fill=1.0,
                                    base=0, pattern=[[-1, P]], channel_multiplier=1).then_inc(consts_set, 1)
            nc.gpsimd.memset(minus_half[:], -0.5).then_inc(consts_set, 1)
            nc.gpsimd.memset(ones[:], 1.0).then_inc(consts_set, 1)
            pool.wait_ge(consts_set, 4)

            def inverse_std(a, q, par):
                wait_apart(pool, mean_var_done[a], q + 1, spare)
                nc.gpsimd.tensor_scalar(var_eps[a][:, par:par + 1], mean_var[a][:, par, 1:2], EPS, None,
                                        ALU.add).then_inc(var_eps_done[a], 1)
                pool.wait_ge(var_eps_done[a], q + 1)
                nc.gpsimd.tensor_tensor(rstd[a][:, par:par + 1], var_eps[a][:, par:par + 1], minus_half[:],
                                        ALU.pow).then_inc(rstd_done[a], 1)

            def step(g, r, has):
                if has(g + 1):
                    inverse_std(0, g + 1, (r + 1) % 2)
                for j in v_groups(g):
                    pool.wait_ge(v_hi_done, j + 1)
                    nc.gpsimd.tensor_tensor(v_lo[:, j // 2, j % 2], v_rows[:, j % 2],
                                            v_hi[:, j // 2, j % 2].bitcast(F32), ALU.subtract).then_inc(v_lo_done, 1)
                if isinstance(g, int) and 1 <= g <= KT:
                    pool.wait_ge(cb_hi_done, g)
                    nc.gpsimd.tensor_tensor(cb_lo[:, g - 1], cb_raw[:, g - 1], cb_hi[:, g - 1].bitcast(F32),
                                            ALU.subtract).then_inc(cb_lo_done, 1)
                if isinstance(g, int) and g == KT + 1:
                    pool.wait_ge(rows_loaded, 32)
                if has(g - 5):
                    wait_apart(pool, xn_ready[1], g - 4, spare)
                    nc.gpsimd.tensor_tensor(x_all[:, g - 5], x_all[:, g - 5], bias_rows[:], ALU.add).then_inc(biased, 1)
                if has(g - 3):
                    inverse_std(1, g - 3, (r + 1) % 2)
                if has(g - 6):
                    pool.wait_ge(biased, g - 5)
                    wait_apart(pool, scaled_done, g - 5, spare)
                    nc.gpsimd.tensor_tensor(x_all[:, g - 6], scaled[:, r % 2], x_all[:, g - 6], ALU.add).then_inc(out_ready, 1)

            steps(pool, step)

        @block.scalar
        def _(act):
            for k in range(KT):
                act.wait_ge(prep_filled, KT + k + 1)
                nc.scalar.copy(m_hi[:, k], prep_bank[k][:, 0:BATCH * CTX]).then_inc(m_hi_done, 1)

            def copy_hi(filled, q, out, in_, done):
                act.wait_ge(filled, q + 1)
                nc.scalar.copy(out, in_).then_inc(done, 1)

            def step(g, r, has):
                if has(g):
                    free(act, s_filled, g, 2)
                    copy_hi(xt_filled[0], g, xt_hi[0][:, r % 2], psum_xt[0][:], xt_hi_done[0])
                for j in v_groups(g):
                    act.wait_ge(v_biased, j + 1)
                    nc.scalar.copy(v_hi[:, j // 2, j % 2], v_rows[:, j % 2]).then_inc(v_hi_done, 1)
                if isinstance(g, int) and 1 <= g <= KT:
                    act.wait_ge(cb_loaded, 16)
                    nc.scalar.copy(cb_hi[:, g - 1], cb_raw[:, g - 1]).then_inc(cb_hi_done, 1)
                if has(g - 2):
                    free(act, o_filled, g - 2, 2)
                    copy_hi(pt_filled, g - 2, pt_hi[:, r % 2], psum_pt[:], pt_hi_done)
                if has(g - 1):
                    par = (r + 1) % 2
                    free(act, pt_filled, g - 1, 2)
                    free(act, inv_done, g - 1, 2)
                    act.wait_ge(max_done, g)
                    nc.scalar.activation(probs[:, par], psum_s[:], ACT.Exp, bias=minus_max[:, par:par + 1],
                                         accum_out=weight_sum[:, par:par + 1]).then_inc(exp_done, 1)
                if has(g - 5):
                    free(act, f_filled, g - 5, 2)
                    copy_hi(xt_filled[1], g - 5, xt_hi[1][:, (r + 1) % 2], psum_xt[1][:], xt_hi_done[1])

            steps(act, step)

        @block.vector
        def _(dve):
            dve.wait_ge(consts_set, 4)
            nc.vector.tensor_copy(ones_r[:], ones[:]).then_inc(ones_ready, 1)
            def last_neurons(part):
                neurons(nc, dve, part, y, count, last_rows, lif_step, last_ready, 0)

            last_neurons(0)
            for e in range(KT):
                dve.wait_ge(prep_filled, e + 1)
                nc.vector.tensor_scalar(k_t[:, e], prep_bank[e][:, 0:BATCH * CTX], bk_sb[:, e:e + 1], None,
                                        ALU.add).then_inc(prep_read, 1)
            dve.wait_ge(prep_read, KT)
            nc.vector.tensor_scalar(bqk[:], k_t[:, 0], bq_sb[:, 0:1], None, ALU.mult).then_inc(bqk_step, 1)
            for e in range(1, KT):
                dve.wait_ge(bqk_step, e)
                nc.vector.scalar_tensor_tensor(out=bqk[:], in0=k_t[:, e], scalar=bq_sb[:, e:e + 1], in1=bqk[:],
                                               op0=ALU.mult, op1=ALU.add).then_inc(bqk_step, 1)
            dve.wait_ge(bqk_step, KT)
            nc.vector.tensor_copy(bqk_hi[:], bqk[:]).then_inc(bqk_step, 1)
            dve.wait_ge(bqk_step, KT + 1)
            nc.vector.tensor_tensor(bqk_lo[:], bqk[:], bqk_hi[:].bitcast(F32), ALU.subtract).then_inc(bqk_step, 1)

            def products_lo():
                for k in range(KT):
                    dve.wait_ge(m_hi_done, k + 1)
                    nc.vector.tensor_tensor(m_lo[:, k], prep_bank[k][:, 0:BATCH * CTX], m_hi[:, k].bitcast(F32),
                                            ALU.subtract).then_inc(prep_read, 1)

            def v_group(j):
                half = j % 2
                if j == 0:
                    dve.wait_ge(v_loaded, 32)
                if j >= 2:
                    dve.wait_ge(v_lo_done, j - 1)
                dve.wait_ge(prep_filled, 2 * KT + j + 1)
                nc.vector.tensor_tensor(v_rows[:, half], v_bank[j][0:HK], bv_rows[0:HK], ALU.add
                                        ).then_inc(v_biased, 1)

            def x_lo(a, q, par):
                dve.wait_ge(xt_hi_done[a], q + 1)
                nc.vector.tensor_tensor(xt_lo[a][:, par], psum_xt[a][:], xt_hi[a][:, par].bitcast(F32),
                                        ALU.subtract).then_inc(xt_lo_done[a], 1)

            def ln_apply(a, q, par):
                dve.wait_ge(rstd_done[a], q + 1)
                free(dve, xt_filled[a], q, 2)
                nc.vector.tensor_scalar(xn[a][:, par], x_all[:, q], mean_var[a][:, par, 0:1],
                                        rstd[a][:, par:par + 1], ALU.subtract, ALU.mult).then_inc(xn_ready[a], 1)

            def step(g, r, has):
                even, odd = r % 2, (r + 1) % 2
                if has(g + 1):
                    free(dve, xn_ready[0], g + 1, 2)
                    if r == 3:
                        wait_apart(dve, x_loaded, (g + 1) * 8 + 32, spare)
                    else:
                        free(dve, stats_done[0], g + 1, 1)
                        dve.sem_inc(spare, 1)
                    nc.vector.bn_stats(stats[0][:, odd], x_all[:, g + 1]).then_inc(stats_done[0], 1)
                    wait_apart(dve, stats_done[0], g + 2, spare)
                    nc.vector.bn_aggr(mean_var[0][:, odd], stats[0][:, odd]).then_inc(mean_var_done[0], 1)
                if isinstance(g, int) and g == 0:
                    last_neurons(1)
                    products_lo()
                if has(g):
                    x_lo(0, g, even)
                for j in v_groups(g):
                    v_group(j)
                if has(g - 1):
                    free(dve, exp_done, g - 1, 2)
                    dve.wait_ge(s_filled, g)
                    nc.vector.tensor_reduce(minus_max[:, odd:odd + 1], psum_s[:], AX_X, ALU.max,
                                            negate=True).then_inc(max_done, 1)
                if has(g + 1):
                    ln_apply(0, g + 1, odd)
                if has(g - 2):
                    dve.wait_ge(pt_hi_done, g - 1)
                    nc.vector.tensor_tensor(pt_lo[:, even], psum_pt[:], pt_hi[:, even].bitcast(F32),
                                            ALU.subtract).then_inc(pt_lo_done, 1)
                    dve.wait_ge(exp_done, g - 1)
                    free(dve, x_mid, g - 2, 2)
                    nc.vector.reciprocal(inv_sum[:, even:even + 1], weight_sum[:, even:even + 1]).then_inc(inv_done, 1)
                if has(g - 3):
                    dve.wait_ge(inv_done, g - 2)
                    dve.wait_ge(o_filled, g - 2)
                    nc.vector.scalar_tensor_tensor(out=x_all[:, g - 3], in0=psum_o[:], scalar=inv_sum[:, odd:odd + 1],
                                                   in1=x_all[:, g - 3], op0=ALU.mult, op1=ALU.add).then_inc(x_mid, 1)
                if has(g - 4):
                    ln_apply(1, g - 4, even)
                if has(g - 3):
                    free(dve, xn_ready[1], g - 3, 2)
                    wait_apart(dve, x_mid, g - 2, spare)
                    nc.vector.bn_stats(stats[1][:, odd], x_all[:, g - 3]).then_inc(stats_done[1], 1)
                    wait_apart(dve, stats_done[1], g - 2, spare)
                    nc.vector.bn_aggr(mean_var[1][:, odd], stats[1][:, odd]).then_inc(mean_var_done[1], 1)
                if has(g - 5):
                    x_lo(1, g - 5, odd)
                if isinstance(g, int) and g == 3:
                    dve.wait_ge(rows_loaded, 32)
                    nc.vector.tensor_scalar(scb_rows[:], scb_rows[:], 1.0 / 127.0, None, ALU.mult).then_inc(scb_ready, 1)
                if isinstance(g, int) and g == 6:
                    dve.wait_ge(scb_ready, 1)
                if has(g - 6):
                    free(dve, out_ready, g - 6, 2)
                    dve.wait_ge(f_filled, g - 5)
                    nc.vector.tensor_tensor(scaled[:, even], psum_f[:], scb_rows[:], ALU.mult).then_inc(scaled_done, 1)
                if isinstance(g, int) and 2 <= g < 6:
                    last_neurons(g)

            steps(dve, step)

        @block.tensor
        def _(pe):
            def prep_group(out, pairs):
                for k, (stat, mov) in enumerate(pairs):
                    mm = nc.tensor.matmul(out, stat, mov, start=(k == 0), stop=(k == len(pairs) - 1))
                mm.then_inc(prep_filled, 1)

            for e in range(KT):
                prep_group(prep_bank[e][:, 0:BATCH * CTX],
                           [(wk_sb[:, k, e * P:(e + 1) * P], ctx_sb[:, k]) for k in range(KC)])
            pe.wait_ge(wq_loaded, 16)
            pe.wait_ge(prep_read, KT)
            for d in range(KT):
                prep_group(prep_bank[d][:, 0:BATCH * CTX],
                           [(wq_sb[:, e, d * P:(d + 1) * P], k_t[:, e]) for e in range(KT)])

            def v_group(j):
                if j == 0:
                    pe.wait_ge(v_loaded, 32)
                    pe.wait_ge(prep_read, 2 * KT)
                if j == 3:
                    pe.wait_ge(v_biased, 1)
                prep_group(v_bank[j][0:HK],
                           [(ctx_sb[:, k, j * HK:(j + 1) * HK], wv_sb[:, k]) for k in range(KC)])

            def transposes(a, q, par):
                pe.wait_ge(xn_ready[a], q + 1)
                free(pe, xt_lo_done[a], q, 1)
                for k in range(KT):
                    mm = nc.tensor.transpose(psum_xt[a][:, k], xn[a][:, par, k * P:(k + 1) * P], ident[:])
                mm.then_inc(xt_filled[a], 1)

            pe.wait_ge(ones_ready, 1)
            pe.wait_ge(consts_set, 4)

            def step(g, r, has):
                even, odd = r % 2, (r + 1) % 2
                if has(g):
                    transposes(0, g, even)
                for j in v_groups(g):
                    v_group(j)
                if isinstance(g, int) and g == 1:
                    pe.wait_ge(prep_read, 2 * KT)
                    pe.wait_ge(bqk_step, KT + 2)
                if isinstance(g, int) and g in (3, 4):
                    pe.wait_ge(v_lo_done, 2 * (g - 2))
                if isinstance(g, int) and g == 6:
                    pe.wait_ge(cb_lo_done, KT)
                if has(g - 1):
                    keys = slice(odd * CTX, (odd + 1) * CTX)
                    pe.wait_ge(xt_lo_done[0], g)
                    free(pe, exp_done, g - 1, 1)
                    for k in range(KT):
                        split_matmul(nc, psum_s[:], (xt_hi[0][:, odd, k], xt_lo[0][:, odd, k]),
                                     (m_hi[:, k, keys], m_lo[:, k, keys]), k == 0, False)
                    nc.tensor.matmul(psum_s[:], ones_r[:], bqk_hi[:, keys], start=False, stop=False)
                    nc.tensor.matmul(psum_s[:], ones_r[:], bqk_lo[:, keys], start=False, stop=True).then_inc(s_filled, 1)
                if has(g - 2):
                    pe.wait_ge(exp_done, g - 1)
                    free(pe, pt_lo_done, g - 2, 1)
                    for half in range(2):
                        mm = nc.tensor.transpose(psum_pt[:, half], probs[:, even, half * HK:(half + 1) * HK], ident[:])
                    mm.then_inc(pt_filled, 1)
                if has(g - 3):
                    pe.wait_ge(pt_lo_done, g - 2)
                    free(pe, x_mid, g - 3, 1)
                    for half in range(2):
                        mm = split_matmul(nc, psum_o[:], (pt_hi[:, odd, half], pt_lo[:, odd, half]),
                                          (v_hi[:, odd, half], v_lo[:, odd, half]), half == 0, half == 1)
                    mm.then_inc(o_filled, 1)
                if has(g - 5):
                    transposes(1, g - 5, odd)
                if has(g - 6):
                    pe.wait_ge(xt_lo_done[1], g - 5)
                    free(pe, scaled_done, g - 6, 1)
                    for k in range(KT):
                        mm = split_matmul(nc, psum_f[:], (xt_hi[1][:, even, k], xt_lo[1][:, even, k]),
                                          (cb_hi[:, k], cb_lo[:, k]), k == 0, k == KT - 1)
                    mm.then_inc(f_filled, 1)

            steps(pe, step)


def cross_attention_ffn_twice(nc, a, out):
    x1 = nc.dram_tensor("x_after_attention", (ROWS, D), F32, kind="Internal").ap()
    x2 = nc.dram_tensor("x_after_spikes", (ROWS, D), F32, kind="Internal").ap()
    with ExitStack() as ctx:
        first_rows = ctx.enter_context(nc.sbuf_tensor("first_rows", [P, T, D], F32))
        mean_var = ctx.enter_context(nc.sbuf_tensor("first_mean_var", [P, T, 2], F32))
        rstd = ctx.enter_context(nc.sbuf_tensor("first_rstd", [P, T], F32))
        x1_stored = [ctx.enter_context(nc.semaphore(f"x1_stored{i}")) for i in range(2)]
        multi_head_attention(nc, a["x"], x1, a["ctx_t"], a["wq0_t"], a["wk0_t"], a["wv0_t"], a["wo0_t"],
                             first_rows, mean_var, rstd, x1_stored)
        y = ctx.enter_context(nc.sbuf_tensor("y", [P, T, D], F32))
        count = ctx.enter_context(nc.sbuf_tensor("count", [P, 2, D], F32))
        last_rows = ctx.enter_context(nc.sbuf_tensor("last_rows", [P, T, D], F32))
        flat, used, parts = first_rows[:].rearrange("p t d -> p (t d)"), 0, []
        for name in ("ctx_t", "wk1", "bk1", "bq1"):
            shape = a[name].shape
            width = int(np.prod(shape[1:]))
            part = flat[:, used:used + width]
            parts.append(part.rearrange("p (k n) -> p k n", k=shape[1]) if len(shape) == 3 else part)
            used += width
        ctx_sb, wk_sb, bk_sb, bq_sb = parts
        spiking_ffn(nc, x1, x2, a["w_fc"], a["w_proj"], y, count, first_rows, mean_var, rstd, last_rows, x1_stored,
                    list(zip(parts, (a["ctx_t"], a["wk1"], a["bk1"], a["bq1"]))))
        single_head_attention_and_linear(nc, x2, out, ctx_sb, a["wq1_t"], bq_sb, wk_sb, bk_sb, a["wv1"], a["bv1"],
                                         a["cb_t"], a["scb"], a["bias"], y, count, last_rows)


def kernel(**inputs):
    import numpy as _np
    import concourse.bacc as _bacc
    from concourse import mybir as _mybir
    from concourse.bass_utils import run_bass_kernel_spmd as _run

    g = {k: _np.asarray(v) for k, v in inputs.items()}

    def tiles(w):
        return w.reshape(-1, 128, w.shape[-1]).transpose(1, 0, 2)

    def column(v):
        return v.reshape(-1, 128).T

    w_kv = g["L0_xattn_Wkv"]
    arrays = {
        "x": g["x"].reshape(ROWS, D),
        "ctx_t": tiles(g["ctx_512"].reshape(BATCH * CTX, CTXD).T),
        "wq0_t": tiles(g["L0_xattn_Wq"].T), "wk0_t": tiles(w_kv[:D].T), "wv0_t": tiles(w_kv[D:].T),
        "wo0_t": tiles(g["L0_xattn_Wo"].T),
        "w_fc": g["L0_ffn_W_fc"].T.reshape(KT, P, NF, P).transpose(1, 2, 0, 3).reshape(P, NF, KT * P),
        "w_proj": tiles(g["L0_ffn_W_proj"].T),
        "wq1_t": tiles(g["L1_xattn_Wq"].T), "bq1": column(g["L1_xattn_bq"]),
        "wk1": tiles(g["L1_xattn_Wk"]), "bk1": column(g["L1_xattn_bk"]),
        "wv1": tiles(g["L1_xattn_Wv"]), "bv1": g["L1_xattn_bv"].reshape(1, D),
        "cb_t": tiles(g["L1_ffn_CB"].T),
        "scb": g["L1_ffn_SCB"].reshape(1, D), "bias": g["L1_ffn_bias"].reshape(1, D),
    }
    nc = _bacc.Bacc("TRN2", target_bir_lowering=False, num_devices=1)
    args, sent = {}, {}
    for name, a in arrays.items():
        a = _np.ascontiguousarray(a)
        sent[f"in_{name}_dram"] = a
        args[name] = nc.dram_tensor(f"in_{name}_dram", a.shape, _mybir.dt.from_np(a.dtype), kind="ExternalInput").ap()
    out = nc.dram_tensor("out_0_dram", (ROWS, D), _mybir.dt.float32, kind="ExternalOutput").ap()
    cross_attention_ffn_twice(nc, args, out)
    r = _run(nc, [sent], core_ids=[0])
    return r.results[0]["out_0_dram"].reshape(BATCH, SEQ, D)
```
